# Optimizing a Trainium2 kernel written in Bass

```python
import numpy as np
import jax
import jax.numpy as jnp

def _softmax(x, axis=-1):
    return jax.nn.softmax(x, axis=axis)

def _gelu(x):
    return jax.nn.gelu(x, approximate=True)

def _silu(x):
    return jax.nn.silu(x)

def _sigmoid(x):
    return jax.nn.sigmoid(x)

def _layernorm(x, axis=-1, eps=1e-05):
    m = jnp.mean(x, axis=axis, keepdims=True)
    v = jnp.var(x, axis=axis, keepdims=True)
    return (x - m) / jnp.sqrt(v + eps)

def _scatter_add(tgt, idx, src, axis=0):
    return tgt.at[idx].add(src)

def _segment_sum(src, seg, n):
    return jax.ops.segment_sum(src, seg, n)
kernel_name = 'mk_gnn_preln_d1_gnn_r8_884bc8'

def setup_inputs(seed: int=0):
    np.random.seed(seed)
    _w = jnp.asarray

    def _rec_inputs():
        import jax
        import jax.numpy as jnp
        _gk = jax.random.key(seed)
        x = -0.000202 + 1 * jax.random.normal(jax.random.fold_in(_gk, 1), (12500, 128), jnp.float32)
        src = jax.random.randint(jax.random.fold_in(_gk, 2), (400000,), 0, 12500, jnp.int32)
        dst = jnp.minimum((12500 * jax.random.uniform(jax.random.fold_in(_gk, 3), (400000,)) ** 2.0).astype(jnp.int32), 99999)
        _o = jnp.argsort(dst, stable=True)
        src = src[_o]
        dst = dst[_o]
        edge_attr_32 = 0.000196303 + 1.00016 * jax.random.normal(jax.random.fold_in(_gk, 13), (400000, 32), jnp.float32)
        edge_weight1 = jax.random.uniform(jax.random.fold_in(_gk, 14), (400000, 1), jnp.float32, 0.0, 1)
        node_vec1 = jax.random.uniform(jax.random.fold_in(_gk, 15), (12500, 1), jnp.float32, 0.0, 1)
        return (x, src, dst, edge_attr_32, edge_weight1, node_vec1)
    x, src, dst, edge_attr_32, edge_weight1, node_vec1 = _rec_inputs()

    def _L0_gnn_setup():
        import jax, jax.numpy as jnp
        import numpy as np
        N, E = (6250, 100000)
        C, A_ALL, RAD_IN, FC1, FC2 = (128, 256, 32, 64, 64)
        H, AH, VH = (8, 16, 16)

        def _radial_mlp(x, w1, b1, w2, b2, w3, b3):
            x = jax.nn.silu(x @ w1 + b1)
            x = jax.nn.silu(x @ w2 + b2)
            return x @ w3 + b3

        def _smooth_leaky_relu(x, a=0.2):
            return 0.5 * (1.0 + a) * x + 0.5 * (1.0 - a) * x * (2.0 * jax.nn.sigmoid(x) - 1.0)

        def _segment_softmax(scores, seg, num_segments):
            m = jax.ops.segment_max(scores, seg, num_segments=num_segments)
            m = jnp.where(jnp.isfinite(m), m, 0.0)
            e = jnp.exp(scores - m[seg])
            s = jax.ops.segment_sum(e, seg, num_segments=num_segments)
            return e / (s[seg] + 1e-16)
        key = jax.random.key(seed)
        ks = jax.random.split(key, 16)

        def g(k, shape):
            scale = 1.0 / np.sqrt(shape[0])
            return jax.random.normal(k, shape, dtype=jnp.float32) * scale
        return {'node_input': jax.random.normal(ks[0], (N, C), dtype=jnp.float32), 'node_attr': jnp.ones((N, 1), jnp.float32), 'edge_attr': jax.random.uniform(ks[1], (E, 1), dtype=jnp.float32), 'edge_scalars': jax.random.normal(ks[2], (E, RAD_IN), dtype=jnp.float32), 'edge_src': jax.random.randint(ks[3], (E,), 0, N, dtype=jnp.int32), 'edge_dst': jax.random.randint(ks[4], (E,), 0, N, dtype=jnp.int32), 'batch': jnp.zeros((N,), jnp.int32), 'w_src': g(ks[5], (C, C)), 'b_src': jnp.zeros((C,), jnp.float32), 'w_dst': g(ks[6], (C, C)), 'fc_w1': g(ks[7], (RAD_IN, FC1)), 'fc_b1': jnp.zeros((FC1,), jnp.float32), 'fc_w2': g(ks[8], (FC1, FC2)), 'fc_b2': jnp.zeros((FC2,), jnp.float32), 'fc_w3': g(ks[9], (FC2, C)), 'fc_b3': jnp.zeros((C,), jnp.float32), 'w_sep': g(ks[10], (C, A_ALL)), 'b_sep': jnp.zeros((A_ALL,), jnp.float32), 'alpha_dot': jax.random.normal(ks[11], (1, H, AH), dtype=jnp.float32) * np.sqrt(2.0 / (H * AH)), 'w_proj': g(ks[12], (H * VH, C)), 'b_proj': jnp.zeros((C,), jnp.float32)}
    _L0_gnn_all = _L0_gnn_setup()
    _L0_gnn_in = {k: v for k, v in _L0_gnn_all.items() if k in ('w_src', 'b_src', 'w_dst', 'fc_w1', 'fc_b1', 'fc_w2', 'fc_b2', 'fc_w3', 'fc_b3', 'w_sep', 'b_sep', 'alpha_dot', 'w_proj', 'b_proj')}
    del _L0_gnn_all
    return {'x': x, 'src': src, 'dst': dst, 'edge_attr_32': edge_attr_32, 'edge_weight1': edge_weight1, 'node_vec1': node_vec1, 'L0_gnn_w_src': _L0_gnn_in['w_src'], 'L0_gnn_b_src': _L0_gnn_in['b_src'], 'L0_gnn_w_dst': _L0_gnn_in['w_dst'], 'L0_gnn_fc_w1': _L0_gnn_in['fc_w1'], 'L0_gnn_fc_b1': _L0_gnn_in['fc_b1'], 'L0_gnn_fc_w2': _L0_gnn_in['fc_w2'], 'L0_gnn_fc_b2': _L0_gnn_in['fc_b2'], 'L0_gnn_fc_w3': _L0_gnn_in['fc_w3'], 'L0_gnn_fc_b3': _L0_gnn_in['fc_b3'], 'L0_gnn_w_sep': _L0_gnn_in['w_sep'], 'L0_gnn_b_sep': _L0_gnn_in['b_sep'], 'L0_gnn_alpha_dot': _L0_gnn_in['alpha_dot'], 'L0_gnn_w_proj': _L0_gnn_in['w_proj'], 'L0_gnn_b_proj': _L0_gnn_in['b_proj']}

def reference(x, src, dst, edge_attr_32, edge_weight1, node_vec1, L0_gnn_w_src, L0_gnn_b_src, L0_gnn_w_dst, L0_gnn_fc_w1, L0_gnn_fc_b1, L0_gnn_fc_w2, L0_gnn_fc_b2, L0_gnn_fc_w3, L0_gnn_fc_b3, L0_gnn_w_sep, L0_gnn_b_sep, L0_gnn_alpha_dot, L0_gnn_w_proj, L0_gnn_b_proj):
    import jax
    import jax.numpy as jnp

    def _L0_gnn_ref(node_input, node_attr, edge_attr, edge_scalars, edge_src, edge_dst, batch, w_src, b_src, w_dst, fc_w1, fc_b1, fc_w2, fc_b2, fc_w3, fc_b3, w_sep, b_sep, alpha_dot, w_proj, b_proj):
        import jax, jax.numpy as jnp
        import numpy as np
        N, E = (6250, 100000)
        C, A_ALL, RAD_IN, FC1, FC2 = (128, 256, 32, 64, 64)
        H, AH, VH = (8, 16, 16)

        def _radial_mlp(x, w1, b1, w2, b2, w3, b3):
            x = jax.nn.silu(x @ w1 + b1)
            x = jax.nn.silu(x @ w2 + b2)
            return x @ w3 + b3

        def _smooth_leaky_relu(x, a=0.2):
            return 0.5 * (1.0 + a) * x + 0.5 * (1.0 - a) * x * (2.0 * jax.nn.sigmoid(x) - 1.0)

        def _segment_softmax(scores, seg, num_segments):
            m = jax.ops.segment_max(scores, seg, num_segments=num_segments)
            m = jnp.where(jnp.isfinite(m), m, 0.0)
            e = jnp.exp(scores - m[seg])
            s = jax.ops.segment_sum(e, seg, num_segments=num_segments)
            return e / (s[seg] + 1e-16)
        n_nodes = node_input.shape[0]
        n_edges = edge_src.shape[0]
        msg_src = node_input @ w_src + b_src
        msg_dst = node_input @ w_dst
        message = msg_src[edge_src] + msg_dst[edge_dst]
        rad_w = _radial_mlp(edge_scalars, fc_w1, fc_b1, fc_w2, fc_b2, fc_w3, fc_b3)
        message = message * edge_attr * rad_w
        message = message @ w_sep + b_sep
        msg_h = message.reshape(n_edges, H, AH + VH)
        alpha = _smooth_leaky_relu(msg_h[:, :, :AH])
        value = msg_h[:, :, AH:]
        score = jnp.einsum('ehk,ahk->eh', alpha, alpha_dot)
        att = _segment_softmax(score, edge_dst, n_nodes)[..., None]
        out = jax.ops.segment_sum(value * att, edge_dst, num_segments=n_nodes)
        out = out.reshape(n_nodes, H * VH)
        return out @ w_proj + b_proj
    batch0 = jnp.zeros((12500,), jnp.int32)
    h = jnp.maximum(_layernorm(x, axis=-1), 0.0)
    x = x + _L0_gnn_ref(h, node_vec1, edge_weight1, edge_attr_32, src, dst, batch0, L0_gnn_w_src, L0_gnn_b_src, L0_gnn_w_dst, L0_gnn_fc_w1, L0_gnn_fc_b1, L0_gnn_fc_w2, L0_gnn_fc_b2, L0_gnn_fc_w3, L0_gnn_fc_b3, L0_gnn_w_sep, L0_gnn_b_sep, L0_gnn_alpha_dot, L0_gnn_w_proj, L0_gnn_b_proj)
    return x

_drawn_inputs = setup_inputs


def setup_inputs(seed=0):
    import zlib

    import numpy as np

    out = dict(_drawn_inputs(seed))
    spreads = {'L0_gnn_b_src': (0.0, 0.8),
     'L0_gnn_fc_b1': (0.0, 0.8),
     'L0_gnn_fc_b2': (0.0, 0.304),
     'L0_gnn_fc_b3': (0.0, 0.1),
     'L0_gnn_b_sep': (0.0, 0.1),
     'L0_gnn_b_proj': (0.0, 0.1)}
    factors = {'L0_gnn_alpha_dot': 8.0}
    for name, (base, spread) in spreads.items():
        noise = np.random.default_rng([zlib.crc32(name.encode()), seed]).standard_normal(out[name].shape)
        drawn = base * np.exp(spread * noise) if base else spread * noise
        out[name] = jnp.asarray(drawn.astype(out[name].dtype))
    for name, factor in factors.items():
        out[name] = (out[name] * factor).astype(out[name].dtype)
    return out
```

```python
import concourse.bass as bass
from concourse import mybir
from contextlib import ExitStack

P = 128
N, E, C = 12500, 400000, 128
RAD, FC = 32, 64
H, AH = 8, 16
SUB = 4
TE = SUB * P
NB = -(-N // P)
NT = -(-E // TE)
CH = P // H
IPC = -(-(NT + NB - 1) // CH)
NI = CH * IPC
TPAD = NI - NB + 1
EPAD = TPAD * TE
RW = 4
RSRC, RDST, REA = 0, 1, 2
VW = C + 1
AW = C + H
EC = E // P
PADC = EPAD // P - EC
BIG = 1e30
FAR = -1e6


def need(eng, sem, count):
    if isinstance(count, int) and count <= 0:
        return
    eng.wait_ge(sem, count)


def drive(eng, body, total, unroll):
    last = total // unroll - 1
    for j in range(unroll):
        body(0, j)
    with eng.Fori(1, last) as g:
        for j in range(unroll):
            body(g, j)
    for i in range(last * unroll, total):
        body(i // unroll, i % unroll)


def gnn_kernel(nc, x, src, dst, edge_attr, edge_weight, w_src, b_src, w_dst, fc_w1, fc_b1, fc_w2, fc_b2,
               fc_w3, fc_b3, w_sep, b_sep, alpha_dot, w_proj, b_proj, out):
    f32, i32, bf16 = mybir.dt.float32, mybir.dt.int32, mybir.dt.bfloat16
    ALU = mybir.AluOpType
    ACT = mybir.ActivationFunctionType
    ctx = ExitStack()

    def sb(name, shape, dt=f32):
        return ctx.enter_context(nc.sbuf_tensor(name, shape, dt))

    def sem(name):
        return ctx.enter_context(nc.semaphore(name))

    def dram(name, shape, dt=f32):
        return nc.dram_tensor(name, shape, dt, kind="Internal").ap()

    def column(v):
        return v.rearrange("(p a) -> p a", a=1)

    def spread(v, n):
        return bass.AP(tensor=v.tensor, offset=v.offset, ap=[[0, n], [1, v.shape[0]]])

    msg_src = dram("msg_src", (NB * P, C))
    msg_dst = dram("msg_dst", (NB, P, C))
    records = dram("records", (EPAD, RW))
    attrs = dram("attrs", (EPAD, RAD))
    dst_rows = dram("dst_rows", (TPAD, TE))
    tile_of = dram("tile_of", (NI,), i32)
    base_of = dram("base_of", (NI,))
    values = dram("values", (NI, P, SUB * VW))
    raw_scores = dram("raw_scores", (P, IPC * TE))
    edge_col = dram("edge_col", (4, P))
    sums = dram("sums", (NI, P, AW))

    with ctx:
        SC = sb("SC", [P, IPC * TE])
        AR = sb("AR", [P, IPC * TE // 2 + 2])
        PS = [ctx.enter_context(nc.psum_tensor(f"PS{i}", [P, TE], f32)) for i in range(8)]
        ident = sb("ident", [P, P])
        iota_row = sb("iota_row", [P, P])
        first_node = sb("first_node", [P, 1])
        base = sb("base", [P, NI])
        keep = sb("keep", [P, NI])
        steer = sb("steer", [1, 2 * NI], i32)
        last_item = sb("last_item", [1, P], i32)
        w1 = sb("w1", [P, 2, P])
        w2 = sb("w2", [P, P])
        w3 = sb("w3", [P, 2, P])
        wsep = sb("wsep", [P, H, 2, AH])
        wa = sb("wa", [P, C])
        wv = sb("wv", [P, C])
        wnode = sb("wnode", [P, 2 * C])
        wproj = sb("wproj", [P, C])
        adot = sb("adot", [P, H])
        b1 = sb("b1", [P, 1])
        b2 = sb("b2", [P, 1])
        b3 = sb("b3", [P, 1])
        ba = sb("ba", [P, 1])
        bsrc = sb("bsrc", [P, C])
        bval = sb("bval", [P, H, 2, AH])
        bproj = sb("bproj", [P, C])
        score_bias = sb("score_bias", [P, H])

        with ExitStack() as part, nc.Block() as block:
            def tb(name, shape, dt=f32):
                return part.enter_context(nc.sbuf_tensor(name, shape, dt))
            def ts(name):
                return part.enter_context(nc.semaphore(name))
            xs = AR[:, 0:NB * C].rearrange("p (b c) -> p b c", b=NB)
            at = [0]

            def region(n):
                at[0] += n
                return SC[:, at[0] - n:at[0]]
            src_in, dst_in = region(EC).bitcast(i32), region(EC).bitcast(i32)
            dst_f, ea_in = region(EC), region(EC)
            rec_out, rec_pad = region(EC * RW), region(PADC * RW)
            attr_pad = region(PADC * RAD)
            stats = tb("stats", [P, NB, 6])
            mean = tb("mean_x2", [P, NB])
            rstd = tb("rstd", [P, NB])
            shift = tb("shift", [P, NB])
            h = tb("h", [P, 2, C])
            hT = tb("hT", [P, 2, C])
            node_out = tb("node_out", [P, 2, 2 * C])
            tail = N - (NB - 1) * P
            s_x, s_w, s_const, s_pad = ts("x_in"), ts("node_weights_in"), ts("ident_made"), ts("pad_made")
            s_tail = ts("x_tail_cleared")
            s_bn, s_std, s_rstd = ts("moments"), ts("std_done"), ts("rstd_done")
            s_h, s_hT, s_hTs, s_mm, s_no = ts("h_done"), ts("hT_done"), ts("hT_copied"), ts("node_mm"), ts("node_rows")
            s_nst = [ts(f"node_stored{i}") for i in range(2)]
            s_ein, s_cp, s_est, s_attr = ts("edges_in"), ts("edge_copies"), ts("records_stored"), ts("attrs_copied")
            rec3 = rec_out.rearrange("p (j f) -> p j f", f=RW)
            pad3 = rec_pad.rearrange("p (j f) -> p j f", f=RW)
            flat = dst_rows.rearrange("t e -> (t e)")

            @block.sync
            def _(sp):
                sp.wait_ge(s_tail, 1)
                sp.dma_start(xs[:, 0:NB - 1, :], x[0:(NB - 1) * P, :].rearrange("(b p) c -> p b c", p=P)).then_inc(s_x, 16)
                sp.dma_start(xs[0:tail, NB - 1, :], x[(NB - 1) * P:N, :]).then_inc(s_x, 16)
                sp.dma_start(wnode[:, 0:C], w_src).then_inc(s_w, 16)
                sp.dma_start(wnode[:, C:2 * C], w_dst).then_inc(s_w, 16)
                sp.dma_start(bsrc[:, :], spread(b_src, P)).then_inc(s_w, 16)

                for to, frm in ((src_in, src), (dst_in, dst), (ea_in, edge_weight)):
                    sp.dma_start(to, frm.rearrange("(p j) -> p j", p=P)).then_inc(s_ein, 16)
                sp.dma_start(attrs[0:E, :].rearrange("(p j) f -> p (j f)", p=P),
                             edge_attr.rearrange("(p j) f -> p (j f)", p=P)).then_inc(s_attr, 16)
                sp.wait_ge(s_attr, 16)

            @block.gpsimd
            def _(pool):
                pool.memset(ident[:, :], 0.0).then_inc(s_const, 1)
                pool.wait_ge(s_const, 1)
                pool.affine_select(out=ident[:, :], in_=ident[:, :], compare_op=ALU.not_equal, fill=1.0,
                                   base=0, pattern=[[-1, P]], channel_multiplier=1).then_inc(s_const, 1)
                pool.iota(iota_row[:, :], [[1, P]], base=0, channel_multiplier=0,
                          allow_small_or_imprecise_dtypes=True)
                pool.iota(first_node[:, :], [[0, 1]], base=0, channel_multiplier=P,
                          allow_small_or_imprecise_dtypes=True)
                pool.memset(rec_pad, 0.0).then_inc(s_pad, 1)
                pool.memset(attr_pad, 0.0).then_inc(s_pad, 1)
                pool.memset(rec3[:, :, RW - 1:RW], 0.0).then_inc(s_pad, 1)
                pool.wait_ge(s_pad, 3)
                pool.memset(pad3[:, :, RDST:RDST + 1], FAR).then_inc(s_pad, 1)
                pool.wait_ge(s_pad, 4)
                pool.dma_start(records[E:EPAD, :].rearrange("(p j) f -> p (j f)", p=P), rec_pad).then_inc(s_est, 16)
                pool.dma_start(attrs[E:EPAD, :].rearrange("(p j) f -> p (j f)", p=P), attr_pad).then_inc(s_est, 16)
                pool.dma_start(flat[E:EPAD].rearrange("(p j) -> p j", p=P), pad3[:, :, RDST],
                               allow_slow_non_contiguous=True).then_inc(s_est, 16)
                pool.wait_ge(s_ein, 48)
                pool.tensor_copy(dst_f, dst_in).then_inc(s_cp, 1)
                pool.tensor_copy(rec3[:, :, RSRC].bitcast(i32), src_in).then_inc(s_cp, 1)
                pool.tensor_copy(rec3[:, :, RDST], dst_in).then_inc(s_cp, 1)
                pool.tensor_copy(rec3[:, :, REA], ea_in).then_inc(s_cp, 1)
                pool.wait_ge(s_cp, 4)
                pool.dma_start(records[0:E, :].rearrange("(p j) f -> p (j f)", p=P), rec_out).then_inc(s_est, 16)
                pool.dma_start(flat[0:E].rearrange("(p j) -> p j", p=P), dst_f).then_inc(s_est, 16)
                pool.wait_ge(s_est, 80)

            @block.vector
            def _(dve):
                dve.memset(xs[:, NB - 1, :], 0.0).then_inc(s_tail, 1)
                dve.wait_ge(s_x, 32)

                def moments(g, j):
                    b = 2 * g + j
                    dve.bn_stats(stats[:, bass.ds(b, 1), :].rearrange("p o c -> p (o c)"),
                                 xs[:, bass.ds(b, 1), :].rearrange("p o c -> p (o c)")).then_inc(s_bn, 1)
                drive(dve, moments, NB, 2)
                dve.wait_ge(s_bn, NB)
                even, odd, even_sq, odd_sq = (stats[:, :, n] for n in (1, 4, 2, 5))
                dve.tensor_tensor(mean[:, :], even, odd, ALU.add)
                dve.tensor_tensor(shift[:, :], even, odd, ALU.subtract)
                dve.tensor_tensor(rstd[:, :], even_sq, odd_sq, ALU.add).then_inc(s_bn, 1)
                dve.wait_ge(s_bn, NB + 1)
                dve.scalar_tensor_tensor(shift[:, :], shift[:, :], 0.25, shift[:, :], ALU.mult, ALU.mult)
                dve.tensor_scalar(rstd[:, :], rstd[:, :], 1.0 / C, 1e-5, ALU.mult, ALU.add).then_inc(s_bn, 1)
                dve.wait_ge(s_bn, NB + 2)
                dve.tensor_tensor(rstd[:, :], rstd[:, :], shift[:, :], ALU.add).then_inc(s_rstd, 1)
                dve.wait_ge(s_std, 1)
                dve.reciprocal(rstd[:, :], rstd[:, :]).then_inc(s_rstd, 1)
                dve.wait_ge(s_rstd, 2)
                dve.scalar_tensor_tensor(shift[:, :], mean[:, :], -0.5, rstd[:, :], ALU.mult, ALU.mult).then_inc(s_rstd, 1)
                dve.wait_ge(s_w, 48)

                def rows(g, j):
                    b = 2 * g + j
                    dve.wait_ge(s_hT, b + 1)
                    need(dve, s_mm, b - 1)
                    dve.tensor_copy(hT[:, j, :], PS[j][:, 0:C]).then_inc(s_hTs, 1)
                    dve.wait_ge(s_mm, b + 1)
                    need(dve, s_nst[j], 32 * g)
                    dve.tensor_tensor(node_out[:, j, 0:C], PS[2 + j][:, 0:C], bsrc[:, :], ALU.add).then_inc(s_no, 1)
                    dve.tensor_copy(node_out[:, j, C:2 * C], PS[2 + j][:, C:2 * C]).then_inc(s_no, 1)
                drive(dve, rows, NB, 2)

            @block.scalar
            def _(act):
                act.wait_ge(s_rstd, 1)
                act.activation(rstd[:, :], rstd[:, :], ACT.Sqrt).then_inc(s_std, 1)
                act.wait_ge(s_rstd, 3)

                def store(g, j):
                    b = 2 * g + j
                    act.wait_ge(s_no, 2 * b + 2)
                    act.dma_start(msg_src[bass.ds(b * P, P), :], node_out[:, j, 0:C]).then_inc(s_nst[j], 16)
                    act.dma_start(msg_dst[bass.ds(b, 1), :, :].rearrange("o p c -> p (o c)"),
                                  node_out[:, j, C:2 * C]).then_inc(s_nst[j], 16)

                def norm(g, j):
                    b = 2 * g + j
                    need(act, s_hT, b - 1)
                    act.activation(h[:, j, :], xs[:, bass.ds(b, 1), :].rearrange("p o c -> p (o c)"), ACT.Relu,
                                   bias=shift[:, bass.ds(b, 1)], scale=rstd[:, bass.ds(b, 1)]).then_inc(s_h, 1)
                    if isinstance(b, int) and b < 2:
                        return
                    store(g - 1, j)
                drive(act, norm, NB, 2)
                store(NB // 2 - 1, 0)
                store(NB // 2 - 1, 1)
                for j in range(2):
                    act.wait_ge(s_nst[j], 32 * (NB // 2))

            @block.tensor
            def _(pe):
                pe.wait_ge(s_const, 2)
                pe.wait_ge(s_w, 48)

                def product(g, j):
                    b = 2 * g + j
                    pe.wait_ge(s_h, b + 1)
                    need(pe, s_hTs, b - 1)
                    pe.transpose(PS[j][:, 0:C], h[:, j, :], ident[:, :]).then_inc(s_hT, 1)
                    pe.wait_ge(s_hTs, b + 1)
                    need(pe, s_no, 2 * b - 2)
                    pe.matmul(PS[2 + j][:, 0:2 * C], lhsT=hT[:, j, :], rhs=wnode[:, :], start=True, stop=True).then_inc(s_mm, 1)
                drive(pe, product, NB, 2)

        with ExitStack() as part, nc.Block() as block:
            def tb(name, shape, dt=f32):
                return part.enter_context(nc.sbuf_tensor(name, shape, dt))
            def ts(name):
                return part.enter_context(nc.semaphore(name))
            firsts_i = tb("firsts_i", [1, NT - 1], i32)
            firsts = tb("firsts", [1, NT - 1])
            ones = tb("ones", [P, P])
            begun_by = tb("begun_by", [P, 1])
            below = SC[:, 0:NT - 1]
            iota_w = SC[:, 1024:1024 + NI]
            begun = SC[:, 2048:2048 + NI]
            blocks = SC[:, 3072:3072 + NI]
            tiles = SC[:, 4096:4096 + NI]
            starts = SC[:, 5120:5120 + P]
            lasts = SC[:, 5248:5248 + P]
            s_wz, s_wl, s_f, s_io = ts("weights_cleared"), ts("weights_in"), ts("firsts_in"), ts("iota_made")
            s_v, s_p, s_st = ts("vector_steps"), ts("products"), ts("tables_stored")
            halves = [(0, 512), (512, NT - 1)]
            whalves = [(0, 512), (512, NI)]

            @block.sync
            def _(sp):
                sp.dma_start(firsts_i[:, :], bass.AP(tensor=dst.tensor, offset=dst.offset + TE, ap=[[0, 1], [TE, NT - 1]]),
                             allow_slow_non_contiguous=True).then_inc(s_f, 16)
                sp.wait_ge(s_wz, 1)
                loads = []
                for s in range(SUB):
                    loads.append((w1[RAD * s:RAD * (s + 1), s // 2, FC * (s % 2):FC * (s % 2 + 1)], fc_w1))
                for q in range(2):
                    rows = slice(FC * q, FC * (q + 1))
                    loads += [(w2[rows, FC * q:FC * (q + 1)], fc_w2), (w3[rows, q, :], fc_w3),
                              (b1[rows, :], column(fc_b1)), (b2[rows, :], column(fc_b2))]
                loads.append((b3[:, :], column(fc_b3)))
                for hd in range(H):
                    loads.append((adot[AH * hd:AH * (hd + 1), hd:hd + 1], alpha_dot[0, hd, :].rearrange("(k a) -> k a", a=1)))
                    loads.append((ba[AH * hd:AH * (hd + 1), :], column(b_sep[2 * AH * hd:2 * AH * hd + AH])))
                loads += [(wsep[:, :, :, :].rearrange("p h t k -> p (h t k)"), w_sep), (wproj[:, :], w_proj),
                          (bval[:, :, :, :].rearrange("p h t k -> p (h t k)"), spread(b_sep, P)),
                          (bproj[:, :], spread(b_proj, P))]
                for to, frm in loads:
                    sp.dma_start(to, frm).then_inc(s_wl, 16)
                sp.wait_ge(s_wl, 16 * len(loads))
                sp.wait_ge(s_v, 9)
                sp.dma_start(tile_of.rearrange("(a w) -> a w", a=1), steer[0:1, 0:NI]).then_inc(s_st, 16)
                sp.dma_start(base_of.rearrange("(a w) -> a w", a=1), base[0:1, :]).then_inc(s_st, 16)
                sp.wait_ge(s_st, 32)
            n_loads = SUB + 8 + 1 + 2 * H + 4

            @block.gpsimd
            def _(pool):
                pool.iota(iota_w, [[1, NI]], base=0, channel_multiplier=0,
                          allow_small_or_imprecise_dtypes=True).then_inc(s_io, 1)

            @block.vector
            def _(dve):
                for t in (w1, w2, w3, adot):
                    last = dve.memset(t[(slice(None),) * len(t.shape)], 0.0)
                last.then_inc(s_wz, 1)
                dve.memset(ones[:, :], 1.0).then_inc(s_v, 1)
                dve.wait_ge(s_f, 16)
                dve.tensor_copy(firsts[:, :], firsts_i[:, :]).then_inc(s_v, 1)
                dve.wait_ge(s_p, 1)
                for n, (a, z) in enumerate(halves):
                    dve.tensor_scalar(below[:, a:z], PS[n][:, 0:z - a], first_node[:, :], None, ALU.is_lt).then_inc(s_v, 1)
                dve.wait_ge(s_v, 4)
                dve.tensor_reduce(begun_by[:, :], below, mybir.AxisListType.X, ALU.add).then_inc(s_v, 1)
                dve.wait_ge(s_v, 5)
                dve.scalar_tensor_tensor(begun_by[:, :], first_node[:, :], 1.0 / P, begun_by[:, :], ALU.mult, ALU.add).then_inc(s_v, 1)
                dve.wait_ge(s_v, 6)
                dve.wait_ge(s_io, 1)
                dve.tensor_scalar(begun, iota_w, begun_by[:, :], None, ALU.is_ge).then_inc(s_v, 1)
                dve.wait_ge(s_p, 2)
                for n, (a, z) in enumerate(whalves):
                    dve.tensor_scalar(base[:, a:z], PS[2 + n][:, 0:z - a], -1.0, float(P), ALU.add, ALU.mult)
                    dve.tensor_scalar(blocks[:, a:z], PS[2 + n][:, 0:z - a], -1.0, None, ALU.add)
                last = dve.tensor_scalar(starts, PS[4][:, 0:P], -1.0, None, ALU.add)
                last.then_inc(s_v, 1)
                dve.wait_ge(s_v, 8)
                dve.tensor_tensor(tiles, iota_w, blocks, ALU.subtract).then_inc(s_io, 1)
                dve.tensor_tensor(keep[:, 1:NI], blocks[:, 1:NI], blocks[:, 0:NI - 1], ALU.is_equal)
                dve.memset(keep[:, 0:1], 0.0)
                dve.tensor_copy(steer[0:1, NI:2 * NI], blocks[0:1, :])
                dve.tensor_copy(last_item[0:1, 0:NB - 1], starts[0:1, 1:NB])
                dve.memset(last_item[0:1, NB - 1:NB], NT - 1 + NB - 1)
                dve.wait_ge(s_io, 2)
                dve.tensor_copy(steer[0:1, 0:NI], tiles[0:1, :]).then_inc(s_v, 1)
                dve.wait_ge(s_wl, 16 * n_loads)
                dve.tensor_copy(wa[:, :].rearrange("p (h k) -> p h k", h=H), wsep[:, :, 0, :])
                dve.tensor_copy(wv[:, :].rearrange("p (h k) -> p h k", h=H), wsep[:, :, 1, :])
                dve.tensor_scalar(adot[:, :], adot[:, :], 0.8, None, ALU.mult).then_inc(s_v, 1)
                dve.wait_ge(s_p, 3)
                dve.tensor_scalar(score_bias[:, :], PS[5][:, 0:H], 0.25, None, ALU.mult)

            @block.tensor
            def _(pe):
                pe.wait_ge(s_v, 2)
                for n, (a, z) in enumerate(halves):
                    last = pe.matmul(PS[n][:, 0:z - a], lhsT=ones[0:1, :], rhs=firsts[:, a:z], start=True, stop=True)
                last.then_inc(s_p, 1)
                pe.wait_ge(s_v, 7)
                for n, (a, z) in enumerate(whalves):
                    pe.matmul(PS[2 + n][:, 0:z - a], lhsT=ones[0:NB, :], rhs=begun[0:NB, a:z], start=True, stop=True)
                pe.matmul(PS[4][:, 0:P], lhsT=begun_by[:, :].broadcast_to((P, P)), rhs=ident[:, :],
                          start=True, stop=True).then_inc(s_p, 1)
                pe.wait_ge(s_v, 10)
                pe.matmul(PS[5][:, 0:H], lhsT=ba[:, :].broadcast_to((P, P)), rhs=adot[:, :], start=True, stop=True).then_inc(s_p, 1)

        with ExitStack() as part, nc.Block() as block:
            def tb(name, shape, dt=f32):
                return part.enter_context(nc.sbuf_tensor(name, shape, dt))
            def ts(name):
                return part.enter_context(nc.semaphore(name))
            U = 4
            rec = tb("rec", [P, U, SUB, RW])
            attr = tb("attr", [P, U, SUB * RAD])
            win = tb("win", [P, U, C])
            cut = [0]

            def carve(n, pattern, **dims):
                cut[0] += n
                return AR[:, cut[0] - n:cut[0]].rearrange(pattern, **dims)
            gath = carve(U * SUB * C, "p (j s c) -> p j s c", j=U, s=SUB)
            vout = carve(U * SUB * VW, "p (j s c) -> p j s c", j=U, s=SUB)
            hot = carve(2 * TE, "p (j s c) -> p j s c", j=2, s=SUB)
            hotT = carve(2 * TE, "p (j n) -> p j n", j=2)
            recT = tb("recT", [P, 2, P])
            h1 = tb("h1", [P, 2, 2 * P])
            h2 = tb("h2", [P, 2, 2 * P])
            xe = carve(2 * TE, "p (j s c) -> p j s c", j=2, s=SUB)
            rads, msgT, sil = (carve(2 * TE, "p (j n) -> p j n", j=2) for _ in range(3))
            s_rec = [ts(f"rec_in{j}") for j in range(U)]
            s_win = [ts(f"window_in{j}") for j in range(U)]
            s_gath = [ts(f"gathered{j}") for j in range(U)]
            s_vst = [ts(f"values_stored{j}") for j in range(U)]
            s_rel, s_hot, s_recT, s_hotT = ts("relative_done"), ts("hot_done"), ts("recT_done"), ts("hotT_done")
            s_recTs, s_hotTs = ts("recT_copied"), ts("hotT_copied")
            s_z1, s_h1, s_z2, s_h2, s_rad, s_rads = ts("z1_done"), ts("h1_done"), ts("z2_done"), ts("h2_done"), ts("rad_done"), ts("rad_copied")
            s_D, s_x, s_xT, s_msg = ts("dst_rows_done"), ts("summed"), ts("xT_done"), ts("message_done")
            s_a, s_v, s_sil, s_al, s_sc = ts("alpha_in_done"), ts("values_done"), ts("silu_done"), ts("alpha_done"), ts("scores_done")
            s_vout, s_scout, s_go = ts("values_copied"), ts("scores_copied"), ts("gathers_begun")
            recT_ps, z1_ps = PS[1][:, 0:P], PS[1][:, 2 * P:4 * P]
            z2_ps = z1_ps
            sc_ps = PS[0][:, 0:SUB * H]
            rad_ps, hotT_ps, d_ps, xT_ps, a_ps, v_ps = (PS[n][:, :] for n in range(2, 8))
            rec_v = records.rearrange("(t p s) f -> t p (s f)", p=P, s=SUB)
            attr_v = attrs.rearrange("(t p s) f -> t p (s f)", p=P, s=SUB)
            sc_v = SC[:, :].rearrange("p (k s m) -> p k s m", s=SUB, m=CH * H)

            @block.sync
            def _(sp):
                def store(g, j):
                    i = U * g + j
                    sp.wait_ge(s_vout, i + 1)
                    sp.dma_start(values[bass.ds(i, 1)].rearrange("o p c -> p (o c)"),
                                 vout[:, j].rearrange("p s c -> p (s c)")).then_inc(s_vst[j], 16)

                def load(g, j):
                    i = U * g + j
                    t = sp.value_load(steer[0:1, bass.ds(i, 1)], min_val=0, max_val=TPAD - 1)
                    b = sp.value_load(steer[0:1, bass.ds(NI + i, 1)], min_val=0, max_val=NB - 1)
                    need(sp, s_x, i - U + 1)
                    sp.dma_start(rec[:, j].rearrange("p s f -> p (s f)"),
                                 rec_v[bass.ds(t, 1)].rearrange("o p f -> p (o f)")).then_inc(s_rec[j], 16)
                    sp.dma_start(attr[:, j], attr_v[bass.ds(t, 1)].rearrange("o p f -> p (o f)")).then_inc(s_rec[j], 16)
                    sp.dma_start(win[:, j], msg_dst[bass.ds(b, 1)].rearrange("o p c -> p (o c)")).then_inc(s_win[j], 16)
                    if not (isinstance(g, int) and g == 0):
                        store(g - 1, j)
                drive(sp, load, NI, U)
                for j in range(U):
                    store(NI // U - 1, j)
                for j in range(U):
                    sp.wait_ge(s_vst[j], 16 * (NI // U))

            @block.gpsimd
            def _(pool):
                def gather(g, j):
                    i = U * g + j
                    need(pool, s_x, i - U + 1)
                    pool.wait_ge(s_rec[j], 32 * g + 32)
                    pool.sem_inc(s_go, 1)
                    for s in range(SUB):
                        pool.indirect_dma_start(
                            gath[:, j, s], None, msg_src,
                            bass.IndirectOffsetOnAxis(ap=rec[:, j, s, RSRC:RSRC + 1].bitcast(i32), axis=0)
                        ).then_inc(s_gath[j], 16)
                drive(pool, gather, NI, U)

            @block.vector
            def _(dve):
                def prepare(g, j):
                    i = U * g + j
                    dve.wait_ge(s_rec[j], 32 * g + 32)
                    need(dve, s_vst[j], 16 * g)
                    rel = vout[:, j, :, C]
                    dve.tensor_scalar(rel, rec[:, j, :, RDST], base[:, bass.ds(i, 1)], None, ALU.subtract).then_inc(s_rel, 1)
                    dve.wait_ge(s_rel, i + 1)
                    need(dve, s_hotT, i - 1)
                    for s in range(SUB):
                        last = dve.tensor_scalar(hot[:, j % 2, s], iota_row[:, :], vout[:, j, s, C:C + 1],
                                                 rec[:, j, s, REA:REA + 1], ALU.is_equal, ALU.mult)
                    last.then_inc(s_hot, 1)

                def copy_recT(g, j):
                    i = U * g + j
                    dve.wait_ge(s_recT, i + 1)
                    need(dve, s_z1, i - 1)
                    dve.tensor_copy(recT[:, j % 2], recT_ps).then_inc(s_recTs, 1)

                def step(g, j):
                    i = U * g + j
                    q = j % 2
                    dve.wait_ge(s_D, i + 1)
                    dve.wait_ge(s_gath[j], 16 * SUB * (g + 1))
                    need(dve, s_xT, i - 1)
                    for s in range(SUB):
                        last = dve.scalar_tensor_tensor(xe[:, q, s], gath[:, j, s], rec[:, j, s, REA:REA + 1],
                                                        d_ps[:, s * C:(s + 1) * C], ALU.mult, ALU.add)
                    last.then_inc(s_x, 1)
                    if not (isinstance(i, int) and i + 1 >= NI):
                        copy_recT(g + (j + 1) // U, (j + 1) % U)
                    dve.wait_ge(s_xT, i + 1)
                    dve.wait_ge(s_rads, i + 1)
                    need(dve, s_v, i - 1)
                    dve.tensor_tensor(msgT[:, q], xT_ps, rads[:, q], ALU.mult).then_inc(s_msg, 1)
                    if not (isinstance(i, int) and i + 2 >= NI):
                        prepare(g + (j + 2) // U, (j + 2) % U)
                    dve.wait_ge(s_a, i + 1)
                    dve.wait_ge(s_sil, i + 1)
                    dve.scalar_tensor_tensor(sil[:, q], a_ps, 0.25, sil[:, q], ALU.mult, ALU.add).then_inc(s_al, 1)
                    dve.wait_ge(s_v, i + 1)
                    dve.tensor_copy(vout[:, j, :, 0:C], v_ps.rearrange("p (s c) -> p s c", s=SUB)).then_inc(s_vout, 1)
                    dve.wait_ge(s_sc, i + 1)
                    dve.tensor_tensor(sc_v[:, bass.ds(i % IPC, 1), :, bass.ds((i // IPC) * H, H)].rearrange("p o s h -> p (o s) h"),
                                      sc_ps.rearrange("p (s h) -> p s h", s=SUB),
                                      score_bias[:, :].unsqueeze(1).broadcast_to((P, SUB, H)), ALU.add).then_inc(s_scout, 1)
                prepare(0, 0)
                prepare(0, 1)
                copy_recT(0, 0)
                drive(dve, step, NI, U)

            @block.scalar
            def _(act):
                def copy_hotT(g, j):
                    i = U * g + j
                    act.wait_ge(s_hotT, i + 1)
                    need(act, s_D, i - 1)
                    act.activation(hotT[:, j % 2], hotT_ps, ACT.Copy).then_inc(s_hotTs, 1)

                def first(g, j):
                    i = U * g + j
                    act.wait_ge(s_z1, i + 1)
                    need(act, s_z2, i - 1)
                    act.activation(h1[:, j % 2], z1_ps, ACT.Silu, bias=b1[:, :]).then_inc(s_h1, 1)

                def second(g, j):
                    i = U * g + j
                    act.wait_ge(s_z2, i + 1)
                    need(act, s_rad, i - 1)
                    act.activation(h2[:, j % 2], z2_ps, ACT.Silu, bias=b2[:, :]).then_inc(s_h2, 1)

                def radial(g, j):
                    i = U * g + j
                    act.wait_ge(s_rad, i + 1)
                    need(act, s_msg, i - 1)
                    act.activation(rads[:, j % 2].rearrange("f (p q e) -> f p q e", p=2, q=2),
                                   rad_ps.rearrange("f (q p e) -> f p q e", p=2, q=2),
                                   ACT.Identity, bias=b3[:, :]).then_inc(s_rads, 1)

                def step(g, j):
                    i = U * g + j
                    more = not (isinstance(i, int) and i + 1 >= NI)
                    n = (g + (j + 1) // U, (j + 1) % U)
                    if more:
                        copy_hotT(*n)
                        first(*n)
                    act.wait_ge(s_a, i + 1)
                    need(act, s_sc, i - 1)
                    act.activation(sil[:, j % 2], a_ps, ACT.Silu, bias=ba[:, :]).then_inc(s_sil, 1)
                    if more:
                        second(*n)
                        radial(*n)
                copy_hotT(0, 0)
                first(0, 0)
                second(0, 0)
                radial(0, 0)
                drive(act, step, NI, U)

            @block.tensor
            def _(pe):
                def transposes(g, j):
                    i = U * g + j
                    pe.wait_ge(s_rec[j], 32 * g + 32)
                    need(pe, s_h2, i)
                    pe.transpose(recT_ps, attr[:, j], ident[:, :]).then_inc(s_recT, 1)
                    pe.wait_ge(s_hot, i + 1)
                    need(pe, s_hotTs, i)
                    for s in range(SUB):
                        last = pe.transpose(hotT_ps[:, s * P:(s + 1) * P], hot[:, j % 2, s], ident[:, :])
                    last.then_inc(s_hotT, 1)

                def z1(g, j):
                    i = U * g + j
                    pe.wait_ge(s_recTs, i + 1)
                    for p in range(2):
                        last = pe.matmul(z1_ps[:, p * P:(p + 1) * P], lhsT=w1[:, p], rhs=recT[:, j % 2], start=True, stop=True)
                    last.then_inc(s_z1, 1)

                def z2(g, j):
                    i = U * g + j
                    pe.wait_ge(s_h1, i + 1)
                    pe.matmul(z2_ps, lhsT=w2[:, :], rhs=h1[:, j % 2], start=True, stop=True).then_inc(s_z2, 1)

                def dst_part(g, j):
                    i = U * g + j
                    pe.wait_ge(s_win[j], 16 * g + 16)
                    pe.wait_ge(s_hotTs, i + 1)
                    need(pe, s_x, i)
                    for s in range(SUB):
                        last = pe.matmul(d_ps[:, s * C:(s + 1) * C], lhsT=hotT[:, j % 2, s * P:(s + 1) * P],
                                         rhs=win[:, j], start=True, stop=True)
                    last.then_inc(s_D, 1)

                def radial(g, j):
                    i = U * g + j
                    pe.wait_ge(s_h2, i + 1)
                    need(pe, s_rads, i)
                    for q in range(2):
                        last = pe.matmul(rad_ps[:, q * 2 * P:(q + 1) * 2 * P], lhsT=w3[:, q], rhs=h2[:, j % 2], start=True, stop=True)
                    last.then_inc(s_rad, 1)

                def step(g, j):
                    i = U * g + j
                    q = j % 2
                    more = not (isinstance(i, int) and i + 1 >= NI)
                    n = (g + (j + 1) // U, (j + 1) % U)
                    if more:
                        transposes(*n)
                    pe.wait_ge(s_x, i + 1)
                    need(pe, s_msg, i)
                    for s in range(SUB):
                        last = pe.transpose(xT_ps[:, s * P:(s + 1) * P], xe[:, q, s], ident[:, :])
                    last.then_inc(s_xT, 1)
                    if more:
                        z1(*n)
                    pe.wait_ge(s_msg, i + 1)
                    need(pe, s_al, i)
                    pe.matmul(a_ps, lhsT=wa[:, :], rhs=msgT[:, q], start=True, stop=True).then_inc(s_a, 1)
                    need(pe, s_vout, i)
                    for s in range(SUB):
                        last = pe.matmul(v_ps[:, s * C:(s + 1) * C], lhsT=msgT[:, q, s * P:(s + 1) * P], rhs=wv[:, :], start=True, stop=True)
                    last.then_inc(s_v, 1)
                    if more:
                        z2(*n)
                        dst_part(*n)
                    pe.wait_ge(s_al, i + 1)
                    need(pe, s_scout, i)
                    for s in range(SUB):
                        last = pe.matmul(sc_ps[:, s * H:(s + 1) * H], lhsT=sil[:, q, s * P:(s + 1) * P], rhs=adot[:, :], start=True, stop=True)
                    last.then_inc(s_sc, 1)
                    if more:
                        radial(*n)
                transposes(0, 0)
                z1(0, 0)
                z2(0, 0)
                dst_part(0, 0)
                radial(0, 0)
                drive(pe, step, NI, U)

        with ExitStack() as part, nc.Block() as block:
            def tb(name, shape, dt=f32):
                return part.enter_context(nc.sbuf_tensor(name, shape, dt))
            def ts(name):
                return part.enter_context(nc.semaphore(name))
            L = IPC * TE
            change = AR[:, :].bitcast(bf16)[:, 0:L + 1]
            tiles_c = tb("tiles_c", [P, IPC], i32)
            lowest = tb("lowest", [P, IPC])
            highest = tb("highest", [P, IPC])
            index = tb("index", [P, 2], i32)
            drow = tb("drow", [P, 2, TE + 1])
            off = tb("off", [P, 2, TE])
            raw = tb("raw", [P, 2, TE])
            stage = tb("stage", [P, 2, TE])
            dfirst = tb("dfirst", [P, 1])
            edge = tb("edge", [P, 4])
            flags = tb("flags", [P, 4])
            small = tb("small", [H, 6, CH])
            back = tb("back", [P, 1])
            s_t, s_idx, s_pre = ts("chunk_tables_in"), ts("index_ready"), ts("table_steps")
            s_g = [ts(f"dst_gathered{j}") for j in range(2)]
            s_tr, s_col, s_row, s_masked = ts("scores_transposed"), ts("before_copied"), ts("changes_made"), ts("scores_masked")
            s_off = ts("offsets_steps")
            s_staged, s_go = ts("scores_staged"), ts("gathers_begun")
            s_c, s_cd, s_dump = ts("chain"), ts("chain_dma"), ts("scores_dumped")
            s_raw = [ts(f"raw_in{j}") for j in range(2)]
            s_sub, s_exp, s_wt, s_wc = ts("subtracted"), ts("exp_done"), ts("weights_transposed"), ts("weights_copied")
            sc_k = SC[:, :].rearrange("p (k n) -> p k n", n=TE)

            @block.sync
            def _(sp):
                for c in range(CH):
                    rows = slice(c * H, (c + 1) * H)
                    sp.dma_start(tiles_c[rows, :], spread(tile_of[c * IPC:(c + 1) * IPC], H)).then_inc(s_t, 16)
                    sp.dma_start(lowest[rows, :], spread(base_of[c * IPC:(c + 1) * IPC], H)).then_inc(s_t, 16)
                sp.wait_ge(s_masked, IPC)
                sp.dma_start(raw_scores, SC[:, :]).then_inc(s_dump, 16)
                sp.wait_ge(s_c, 1)
                sp.dma_start(column(edge_col[0]), drow[:, (IPC - 1) % 2, TE:TE + 1]).then_inc(s_cd, 16)
                sp.wait_ge(s_cd, 16)
                sp.dma_start(edge[H:P, 0:1], column(edge_col[0, 0:P - H])).then_inc(s_cd, 16)
                sp.wait_ge(s_c, 2)
                sp.dma_start(column(edge_col[1]), flags[:, 0:1]).then_inc(s_cd, 16)
                sp.wait_ge(s_cd, 48)
                sp.dma_start(edge[0:P - H, 1:2], column(edge_col[1, H:P])).then_inc(s_cd, 16)
                by_head = [edge_col[n].rearrange("(c h) -> h c", h=H) for n in range(4)]
                n = 64
                for way in range(2):
                    sp.wait_ge(s_c, 4 + 3 * way)
                    sp.dma_start(column(edge_col[2]), edge[:, 2:3]).then_inc(s_cd, 16)
                    sp.dma_start(column(edge_col[3]), flags[:, 1:2]).then_inc(s_cd, 16)
                    sp.wait_ge(s_cd, n + 32)
                    sp.dma_start(small[:, 0], by_head[2], allow_slow_non_contiguous=True).then_inc(s_cd, 16)
                    sp.dma_start(small[:, 1], by_head[3], allow_slow_non_contiguous=True).then_inc(s_cd, 16)
                    sp.wait_ge(s_cd, n + 64)
                    sp.wait_ge(s_c, 5 + 3 * way)
                    sp.dma_start(by_head[0], small[:, 2], allow_slow_non_contiguous=True).then_inc(s_cd, 16)
                    sp.wait_ge(s_cd, n + 80)
                    sp.dma_start(edge[:, 3:4], column(edge_col[0])).then_inc(s_cd, 16)
                    n += 96

                def load(g, j):
                    k = 2 * g + j
                    need(sp, s_sub, k - 1)
                    sp.dma_start(raw[:, j], raw_scores[:, bass.ds(k * TE, TE)]).then_inc(s_raw[j], 16)
                sp.wait_ge(s_dump, 16)
                drive(sp, load, IPC, 2)

            @block.gpsimd
            def _(pool):
                def gather(g, j):
                    k = 2 * g + j
                    pool.wait_ge(s_idx, k + 1)
                    pool.sem_inc(s_go, 1)
                    pool.indirect_dma_start(drow[:, j, 1:TE + 1], None, dst_rows,
                                            bass.IndirectOffsetOnAxis(ap=index[:, j:j + 1], axis=0)).then_inc(s_g[j], 16)
                drive(pool, gather, IPC, 2)

            @block.vector
            def _(dve):
                dve.memset(drow[:, 0, 0:1], 2 * FAR)
                dve.memset(edge[:, :], 2 * FAR)
                dve.memset(flags[:, :], 0.0)
                dve.memset(small[:, :, :], -BIG).then_inc(s_pre, 1)
                dve.wait_ge(s_t, 32 * CH)
                dve.tensor_scalar(highest[:, :], lowest[:, :], P - 1.0, None, ALU.add).then_inc(s_pre, 1)
                dve.wait_ge(s_pre, 2)

                def pick(g, j):
                    k = 2 * g + j
                    need(dve, s_off, 2 * (k - 1))
                    need(dve, s_row, k - 1)
                    need(dve, s_col, k - 1)
                    dve.tensor_copy(index[:, j:j + 1], tiles_c[:, bass.ds(k, 1)]).then_inc(s_idx, 1)

                def step(g, j):
                    k = 2 * g + j
                    dve.wait_ge(s_g[j], 16 * g + 16)
                    if not (isinstance(k, int) and k + 1 >= IPC):
                        need(dve, s_row, k)
                        dve.tensor_copy(drow[:, 1 - j, 0:1], drow[:, j, TE:TE + 1]).then_inc(s_col, 1)
                    if not (isinstance(k, int) and k == 0):
                        dve.wait_ge(s_col, k)
                    dve.tensor_tensor(change[:, bass.ds(k * TE, TE)], drow[:, j, 1:TE + 1], drow[:, j, 0:TE],
                                      ALU.not_equal).then_inc(s_row, 1)
                    need(dve, s_masked, k - 1)
                    dve.tensor_scalar(off[:, j], drow[:, j, 1:TE + 1], lowest[:, bass.ds(k, 1)], highest[:, bass.ds(k, 1)],
                                      ALU.max, ALU.min).then_inc(s_off, 1)
                    dve.wait_ge(s_off, 2 * k + 1)
                    dve.tensor_tensor(off[:, j], off[:, j], drow[:, j, 1:TE + 1], ALU.not_equal).then_inc(s_off, 1)
                    if isinstance(k, int) and k == 0:
                        dve.tensor_copy(dfirst[:, :], drow[:, 0, 1:2])
                    dve.wait_ge(s_off, 2 * k + 2)
                    dve.wait_ge(s_tr, k + 1)
                    dve.scalar_tensor_tensor(sc_k[:, bass.ds(k, 1)].rearrange("q o (p s) -> q s (o p)", s=SUB),
                                             off[:, j].rearrange("q (p s) -> q s p", s=SUB), -BIG,
                                             PS[j][:, :].rearrange("q (s p) -> q s p", s=SUB),
                                             ALU.mult, ALU.add).then_inc(s_masked, 1)
                    if not (isinstance(k, int) and k + 2 >= IPC):
                        pick(g + 1, j)
                pick(0, 0)
                pick(0, 1)
                drive(dve, step, IPC, 2)
                dve.wait_ge(s_row, IPC)
                dve.engine_nop().then_inc(s_c, 1)
                dve.wait_ge(s_cd, 32)
                dve.tensor_tensor(flags[:, 0:1], dfirst[:, :], edge[:, 0:1], ALU.not_equal).then_inc(s_c, 1)
                dve.wait_ge(s_c, 2)
                dve.tensor_copy(change[:, 0:1], flags[:, 0:1])
                dve.memset(back[:, :], 1.0)
                dve.wait_ge(s_cd, 64)
                dve.tensor_scalar(change[:, L:L + 1], edge[:, 1:2], 0.0, None, ALU.not_equal).then_inc(s_c, 1)
                dve.wait_ge(s_c, 3)
                dve.tensor_scalar(change[:, :], change[:, :], -BIG, None, ALU.mult).then_inc(s_row, 1)
                dve.wait_ge(s_dump, 16)
                dve.wait_ge(s_row, IPC + 1)
                for way in range(2):
                    run = slice(None) if way == 0 else slice(None, None, -1)
                    pen = change[:, way:L + way][:, run]
                    val = SC[:, :][:, run]
                    end = L - 1 if way == 0 else 0
                    b = 4 + 3 * way
                    dve.tensor_tensor_scan(val, pen, val, -BIG, ALU.add, ALU.max).then_inc(s_pre, 1)
                    dve.tensor_reduce(flags[:, 1:2], pen, mybir.AxisListType.X, ALU.min).then_inc(s_pre, 1)
                    dve.wait_ge(s_pre, 4 + 3 * way)
                    dve.tensor_copy(edge[:, 2:3], SC[:, end:end + 1]).then_inc(s_c, 1)
                    dve.wait_ge(s_cd, 128 + 96 * way)
                    inner = slice(0, CH - 1) if way == 0 else slice(CH - 1, 0, -1)
                    carry = slice(1, CH) if way == 0 else slice(CH - 2, None, -1)
                    if way == 1:
                        dve.memset(small[:, 2], -BIG).then_inc(s_pre, 1)
                        dve.wait_ge(s_pre, 8)
                    dve.tensor_tensor_scan(small[:, 2, carry], small[:, 1, inner], small[:, 0, inner], -BIG,
                                           ALU.add, ALU.max).then_inc(s_c, 1)
                    dve.wait_ge(s_cd, 160 + 96 * way)
                    dve.tensor_tensor_scan(val, pen, val, edge[:, 3:4], ALU.add, ALU.max).then_inc(s_c, 1)
                    if way == 0:
                        dve.engine_nop().then_inc(s_pre, 1)
                        dve.wait_ge(s_c, b + 2)
                dve.wait_ge(s_c, 9)

                def subtract(g, j):
                    k = 2 * g + j
                    dve.wait_ge(s_raw[j], 16 * g + 16)
                    dve.tensor_tensor(sc_k[:, bass.ds(k, 1)].rearrange("q o n -> q (o n)"), raw[:, j],
                                      sc_k[:, bass.ds(k, 1)].rearrange("q o n -> q (o n)"), ALU.subtract).then_inc(s_sub, 1)
                    if not (isinstance(k, int) and k < 2):
                        copy(g - 1, j)

                def copy(g, j):
                    k = 2 * g + j
                    dve.wait_ge(s_wt, k + 1)
                    dve.tensor_copy(sc_k[:, bass.ds(k, 1)].rearrange("q o n -> q (o n)"), PS[2 + j][:, :]).then_inc(s_wc, 1)
                drive(dve, subtract, IPC, 2)
                for k in range(IPC - 2, IPC):
                    copy(k // 2, k % 2)

            @block.scalar
            def _(act):
                def copy(g, j):
                    k = 2 * g + j
                    need(act, s_tr, k - 1)
                    act.activation(stage[:, j], sc_k[:, bass.ds(k, 1)].rearrange("q o n -> q (o n)"), ACT.Copy).then_inc(s_staged, 1)
                drive(act, copy, IPC, 2)

                def weigh(g, j):
                    k = 2 * g + j
                    act.wait_ge(s_sub, k + 1)
                    need(act, s_wt, k - 1)
                    row = sc_k[:, bass.ds(k, 1)].rearrange("q o n -> q (o n)")
                    act.activation(stage[:, j], row, ACT.Exp).then_inc(s_exp, 1)
                drive(act, weigh, IPC, 2)

            @block.tensor
            def _(pe):
                def to_rows(g, j):
                    k = 2 * g + j
                    pe.wait_ge(s_staged, k + 1)
                    need(pe, s_masked, k - 1)
                    for s in range(SUB):
                        last = pe.transpose(PS[j][:, s * P:(s + 1) * P], stage[:, j, s * P:(s + 1) * P], ident[:, :])
                    last.then_inc(s_tr, 1)
                drive(pe, to_rows, IPC, 2)

                def to_edges(g, j):
                    k = 2 * g + j
                    pe.wait_ge(s_exp, k + 1)
                    need(pe, s_wc, k - 1)
                    for s in range(SUB):
                        last = pe.transpose(PS[2 + j][:, s * P:(s + 1) * P], stage[:, j, s:TE:SUB], ident[:, :])
                    last.then_inc(s_wt, 1)
                drive(pe, to_edges, IPC, 2)

        with ExitStack() as part, nc.Block() as block:
            def tb(name, shape, dt=f32):
                return part.enter_context(nc.sbuf_tensor(name, shape, dt))
            def ts(name):
                return part.enter_context(nc.semaphore(name))
            U = 4
            vin = tb("vin", [P, U, SUB, VW])
            hot = tb("hot2", [P, 2, SUB, P])
            wval = tb("wval", [P, 2, SUB, AW])
            run = tb("run", [P, U, AW])
            s_vin = [ts(f"values_in{j}") for j in range(U)]
            s_hot, s_w, s_wv, s_mm, s_run, s_clear = ts("hot2_done"), ts("weights_out"), ts("weighted"), ts("aggregated"), ts("run_done"), ts("run_cleared")
            s_rst = [ts(f"run_stored{j}") for j in range(U)]
            sc_v = SC[:, :].rearrange("p (k s m) -> p k s m", s=SUB, m=CH * H)

            @block.sync
            def _(sp):
                def load(g, j):
                    i = U * g + j
                    need(sp, s_mm, i - U + 1)
                    sp.dma_start(vin[:, j].rearrange("p s c -> p (s c)"),
                                 values[bass.ds(i, 1)].rearrange("o p c -> p (o c)")).then_inc(s_vin[j], 16)
                    if not (isinstance(g, int) and g == 0):
                        store(g - 1, j)

                def store(g, j):
                    i = U * g + j
                    sp.wait_ge(s_run, i + 1)
                    sp.dma_start(sums[bass.ds(i, 1)].rearrange("o p c -> p (o c)"), run[:, j]).then_inc(s_rst[j], 16)
                drive(sp, load, NI, U)
                for j in range(U):
                    store(NI // U - 1, j)
                for j in range(U):
                    sp.wait_ge(s_rst[j], 16 * (NI // U))

            @block.vector
            def _(dve):
                dve.memset(run[:, U - 1], 0.0).then_inc(s_clear, 1)
                dve.wait_ge(s_clear, 1)

                def weigh(g, j):
                    i = U * g + j
                    q = j % 2
                    dve.wait_ge(s_vin[j], 16 * g + 16)
                    need(dve, s_mm, i - 1)
                    dve.tensor_copy(wval[:, q, :, C:AW],
                                    sc_v[:, bass.ds(i % IPC, 1), :, bass.ds((i // IPC) * H, H)].rearrange("p o s h -> p (o s) h")).then_inc(s_w, 1)
                    for s in range(SUB):
                        last = dve.tensor_scalar(hot[:, q, s], iota_row[:, :], vin[:, j, s, C:C + 1], None, ALU.is_equal)
                    last.then_inc(s_hot, 1)
                    dve.wait_ge(s_w, i + 1)
                    dve.tensor_tensor(wval[:, q, :, 0:C].rearrange("p s (h k) -> p s h k", h=H),
                                      vin[:, j, :, 0:C].rearrange("p s (h k) -> p s h k", h=H),
                                      wval[:, q, :, C:AW].unsqueeze(3).broadcast_to((P, SUB, H, AH)), ALU.mult).then_inc(s_wv, 1)

                def add(g, j):
                    i = U * g + j
                    dve.wait_ge(s_mm, i + 1)
                    need(dve, s_run, i)
                    need(dve, s_rst[j], 16 * g)
                    dve.scalar_tensor_tensor(run[:, j], run[:, (j - 1) % U], keep[:, bass.ds(i, 1)], PS[j % 2][:, 0:AW],
                                             ALU.mult, ALU.add).then_inc(s_run, 1)

                def step(g, j):
                    weigh(g, j)
                    if not (isinstance(g, int) and g == 0 and j == 0):
                        add(g - (1 if j == 0 else 0), (j - 1) % U)
                drive(dve, step, NI, U)
                add(NI // U - 1, U - 1)

            @block.tensor
            def _(pe):
                def aggregate(g, j):
                    i = U * g + j
                    pe.wait_ge(s_hot, i + 1)
                    pe.wait_ge(s_wv, i + 1)
                    need(pe, s_run, i - 1)
                    for s in range(SUB):
                        last = pe.matmul(PS[j % 2][:, 0:AW], lhsT=hot[:, j % 2, s], rhs=wval[:, j % 2, s],
                                         start=(s == 0), stop=(s == SUB - 1))
                    last.then_inc(s_mm, 1)
                drive(pe, aggregate, NI, U)

        with ExitStack() as part, nc.Block() as block:
            def tb(name, shape, dt=f32):
                return part.enter_context(nc.sbuf_tensor(name, shape, dt))
            def ts(name):
                return part.enter_context(nc.semaphore(name))
            agg = tb("agg", [P, 2, AW])
            xin = tb("xin", [P, 2, C])
            den = tb("den", [P, 2, H])
            mean = tb("mean", [P, 2, C])
            meanT = tb("meanT", [P, 2, C])
            fin = tb("fin", [P, 2, C])
            s_in = [ts(f"sums_in{j}") for j in range(2)]
            s_out = [ts(f"out_stored{j}") for j in range(2)]
            s_d, s_mean, s_T, s_Ts, s_mm, s_res, s_fin = ts("node_steps"), ts("mean_done"), ts("meanT_done"), ts("meanT_copied"), ts("projected"), ts("residual"), ts("out_ready")
            tail = N - (NB - 1) * P

            def nodes(v, b):
                return v[bass.ds(b * P, P), :]

            @block.sync
            def _(sp):
                def load(g, j):
                    b = 2 * g + j
                    last = sp.value_load(last_item[0:1, bass.ds(b, 1)], min_val=0, max_val=NI - 1)
                    need(sp, s_fin, b - 1)
                    sp.dma_start(agg[:, j], sums[bass.ds(last, 1)].rearrange("o p c -> p (o c)")).then_inc(s_in[j], 16)
                    if isinstance(b, int) and b == NB - 1:
                        sp.dma_start(xin[0:tail, j], x[b * P:N, :]).then_inc(s_in[j], 16)
                    else:
                        sp.dma_start(xin[:, j], nodes(x, b)).then_inc(s_in[j], 16)
                    if not (isinstance(g, int) and g == 0):
                        store(g - 1, j)

                def store(g, j):
                    b = 2 * g + j
                    sp.wait_ge(s_fin, b + 1)
                    if isinstance(b, int) and b == NB - 1:
                        sp.dma_start(out[b * P:N, :], fin[0:tail, j]).then_inc(s_out[j], 16)
                    else:
                        sp.dma_start(nodes(out, b), fin[:, j]).then_inc(s_out[j], 16)
                drive(sp, load, NB, 2)
                for j in range(2):
                    store(NB // 2 - 1, j)
                for j in range(2):
                    sp.wait_ge(s_out[j], 16 * (NB // 2))

            @block.vector
            def _(dve):
                def divide(g, j):
                    b = 2 * g + j
                    dve.wait_ge(s_in[j], 32 * g + 32)
                    need(dve, s_T, b - 1)
                    w = agg[:, j, C:AW]
                    heads = mean[:, j].rearrange("p (h k) -> p h k", h=H)
                    dve.tensor_scalar(den[:, j], w, 1e-16, None, ALU.add)
                    dve.tensor_tensor(heads, bval[:, :, 1, :], w.unsqueeze(2).broadcast_to((P, H, AH)), ALU.mult).then_inc(s_d, 1)
                    dve.wait_ge(s_d, 3 * b + 1)
                    dve.reciprocal(den[:, j], den[:, j])
                    dve.tensor_tensor(mean[:, j], mean[:, j], agg[:, j, 0:C], ALU.add).then_inc(s_d, 1)
                    dve.wait_ge(s_d, 3 * b + 2)
                    dve.tensor_tensor(heads, heads, den[:, j].unsqueeze(2).broadcast_to((P, H, AH)), ALU.mult).then_inc(s_mean, 1)
                    need(dve, s_out[j], 16 * g)
                    dve.tensor_tensor(fin[:, j], xin[:, j], bproj[:, :], ALU.add).then_inc(s_d, 1)
                    dve.wait_ge(s_T, b + 1)
                    need(dve, s_mm, b - 1)
                    dve.tensor_copy(meanT[:, j], PS[j][:, 0:P]).then_inc(s_Ts, 1)
                    dve.wait_ge(s_mm, b + 1)
                    dve.wait_ge(s_d, 3 * b + 3)
                    dve.tensor_tensor(fin[:, j], PS[2 + j][:, 0:C], fin[:, j], ALU.add).then_inc(s_fin, 1)
                drive(dve, divide, NB, 2)

            @block.tensor
            def _(pe):
                def project(g, j):
                    b = 2 * g + j
                    pe.wait_ge(s_mean, b + 1)
                    need(pe, s_Ts, b - 1)
                    pe.transpose(PS[j][:, 0:P], mean[:, j], ident[:, :]).then_inc(s_T, 1)
                    pe.wait_ge(s_Ts, b + 1)
                    need(pe, s_fin, b - 1)
                    pe.matmul(PS[2 + j][:, 0:C], lhsT=meanT[:, j], rhs=wproj[:, :], start=True, stop=True).then_inc(s_mm, 1)
                drive(pe, project, NB, 2)


_INS = ["x", "src", "dst", "edge_attr_32", "edge_weight1", "L0_gnn_w_src", "L0_gnn_b_src", "L0_gnn_w_dst",
        "L0_gnn_fc_w1", "L0_gnn_fc_b1", "L0_gnn_fc_w2", "L0_gnn_fc_b2", "L0_gnn_fc_w3", "L0_gnn_fc_b3",
        "L0_gnn_w_sep", "L0_gnn_b_sep", "L0_gnn_alpha_dot", "L0_gnn_w_proj", "L0_gnn_b_proj"]


def kernel(**inputs):
    import numpy as _np
    import concourse.bacc as _bacc
    from concourse import mybir as _mybir
    from concourse.bass_utils import run_bass_kernel_spmd as _run

    nc = _bacc.Bacc("TRN2", target_bir_lowering=False, num_devices=1)
    arrays, args = {}, []
    for name in _INS:
        a = _np.ascontiguousarray(inputs[name])
        if name == "edge_weight1":
            a = a.reshape(-1)
        arrays[f"in_{name}"] = a
        args.append(nc.dram_tensor(f"in_{name}", a.shape, _mybir.dt.from_np(a.dtype), kind="ExternalInput").ap())
    out = nc.dram_tensor("out", (N, C), _mybir.dt.float32, kind="ExternalOutput").ap()
    gnn_kernel(nc, *args, out)
    r = _run(nc, [arrays], core_ids=[0])
    return r.results[0]["out"]
```

```python
import concourse.bass as bass
from concourse import mybir
from contextlib import ExitStack

P = 128
N, E, C = 12500, 400000, 128
RAD, FC = 32, 64
H, AH = 8, 16
SUB = 4
TE = SUB * P
NB = -(-N // P)
NT = -(-E // TE)
CH = P // H
IPC = -(-(NT + NB - 1) // CH)
NI = CH * IPC
TPAD = NI - NB + 1
EPAD = TPAD * TE
RW = 4
RSRC, RDST, REA = 0, 1, 2
VW = C + 1
AW = C + H
EC = E // P
PADC = EPAD // P - EC
BIG = 1e30
PARTS = 3
FAR = -1e6
SS = 5
NS = E // (SS * P)


def need(eng, sem, count):
    if isinstance(count, int) and count <= 0:
        return
    eng.wait_ge(sem, count)


def drive(eng, body, total, unroll):
    last = total // unroll - 1
    for j in range(unroll):
        body(0, j)
    with eng.Fori(1, last) as g:
        for j in range(unroll):
            body(g, j)
    for i in range(last * unroll, total):
        body(i // unroll, i % unroll)


def gnn_kernel(nc, x, src, dst, edge_attr, edge_weight, w_src, b_src, w_dst, fc_w1, fc_b1, fc_w2, fc_b2,
               fc_w3, fc_b3, w_sep, b_sep, alpha_dot, w_proj, b_proj, out):
    f32, i32, bf16 = mybir.dt.float32, mybir.dt.int32, mybir.dt.bfloat16
    ALU = mybir.AluOpType
    ACT = mybir.ActivationFunctionType
    ctx = ExitStack()

    def sb(name, shape, dt=f32):
        return ctx.enter_context(nc.sbuf_tensor(name, shape, dt))

    def sem(name):
        return ctx.enter_context(nc.semaphore(name))

    def dram(name, shape, dt=f32):
        return nc.dram_tensor(name, shape, dt, kind="Internal").ap()

    def column(v):
        return v.rearrange("(p a) -> p a", a=1)

    def spread(v, n):
        return bass.AP(tensor=v.tensor, offset=v.offset, ap=[[0, n], [1, v.shape[0]]])

    msg_src = dram("msg_src", (NB * P, C))
    msg_dst = dram("msg_dst", (NB, P, PARTS * C), bf16)
    records = dram("records", (EPAD, RW))
    attrs = dram("attrs", (EPAD, RAD))
    dst_rows = dram("dst_rows", (TPAD, TE))
    records_by_low = dram("records_by_low", (E, RW))
    attrs_by_low = dram("attrs_by_low", (E, RAD))
    tile_of = dram("tile_of", (NI,), i32)
    base_of = dram("base_of", (NI,))
    values = dram("values", (NI, P, SUB * VW))
    scores = dram("scores", (NI, P, P))
    masked_scores = dram("masked_scores", (P, IPC * TE))
    edge_col = dram("edge_col", (4, P))
    sums = dram("sums", (NI, P, AW))

    with ctx:
        SC = sb("SC", [P, IPC * TE])
        AR = sb("AR", [P, IPC * TE // 2 + 2])
        PS = [ctx.enter_context(nc.psum_tensor(f"PS{i}", [P, TE], f32)) for i in range(8)]
        ident = sb("ident", [P, P])
        ident_h = sb("ident_h", [P, P], bf16)
        iota_row = sb("iota_row", [P, P])
        first_node = sb("first_node", [P, 1])
        base = sb("base", [P, NI])
        keep = sb("keep", [P, NI])
        steer = sb("steer", [1, 2 * NI], i32)
        last_item = sb("last_item", [1, P], i32)
        unsorted = sb("unsorted", [1, 1], i32)
        w1 = sb("w1", [P, 2, P])
        w2 = sb("w2", [P, P])
        w3 = sb("w3", [P, 2, P])
        wsep = sb("wsep", [P, H, 2, AH])
        wa = sb("wa", [P, C])
        wv = sb("wv", [P, C])
        wnode = sb("wnode", [P, 2 * C])
        wproj = sb("wproj", [P, C])
        adot = sb("adot", [P, 32])
        b1 = sb("b1", [P, 1])
        b2 = sb("b2", [P, 1])
        b3 = sb("b3", [P, 1])
        ba = sb("ba", [P, 1])
        bsrc = sb("bsrc", [P, C])
        bval = sb("bval", [P, H, 2, AH])
        bproj = sb("bproj", [P, C])
        score_bias = sb("score_bias", [P, 1])

        with ExitStack() as part, nc.Block() as block:
            def tb(name, shape, dt=f32):
                return part.enter_context(nc.sbuf_tensor(name, shape, dt))
            def ts(name):
                return part.enter_context(nc.semaphore(name))
            xs = AR[:, 0:NB * C].rearrange("p (b c) -> p b c", b=NB)
            at = [0]

            def region(n):
                at[0] += n
                return SC[:, at[0] - n:at[0]]
            src_in, dst_in = region(EC).bitcast(i32), region(EC).bitcast(i32)
            dst_next, ea_in = region(EC + 1), region(EC)
            dst_f = dst_next[:, 0:EC]
            rec_out, rec_pad = region(EC * RW), region(PADC * RW)
            attr_pad = region(PADC * RAD)
            stats = tb("stats", [P, NB, 6])
            mean = tb("mean_x2", [P, NB])
            rstd = tb("rstd", [P, NB])
            shift = tb("shift", [P, NB])
            h = tb("h", [P, 2, C])
            bsrc2 = tb("bsrc2", [P, 2 * C])
            hT = tb("hT", [P, 2, C])
            node_out = tb("node_out", [P, 2, 2 * C])
            dst_parts = tb("dst_parts", [P, 2, PARTS, C], bf16)
            tail = N - (NB - 1) * P
            s_x, s_w, s_const, s_pad = ts("x_in"), ts("node_weights_in"), ts("ident_made"), ts("pad_made")
            s_tail = ts("x_tail_cleared")
            s_bn, s_std, s_rstd = ts("moments"), ts("std_done"), ts("rstd_done")
            s_h, s_hT, s_hTs, s_mm, s_no = ts("h_done"), ts("hT_done"), ts("hT_copied"), ts("node_mm"), ts("node_rows")
            s_part = ts("parts_made")
            s_nst = [ts(f"node_stored{i}") for i in range(2)]
            s_ein, s_cp, s_est, s_attr = ts("edges_in"), ts("edge_copies"), ts("records_stored"), ts("attrs_copied")
            rec3 = rec_out.rearrange("p (j f) -> p j f", f=RW)
            pad3 = rec_pad.rearrange("p (j f) -> p j f", f=RW)
            flat = dst_rows.rearrange("t e -> (t e)")

            @block.sync
            def _(sp):
                sp.dma_start(wnode[:, 0:C], w_src).then_inc(s_w, 16)
                sp.dma_start(wnode[:, C:2 * C], w_dst).then_inc(s_w, 16)
                sp.dma_start(bsrc[:, :], spread(b_src, P)).then_inc(s_w, 16)
                sp.dma_start(xs[:, 0:NB - 1, :], x[0:(NB - 1) * P, :].rearrange("(b p) c -> p b c", p=P)).then_inc(s_x, 16)
                sp.wait_ge(s_tail, 1)
                sp.dma_start(xs[0:tail, NB - 1, :], x[(NB - 1) * P:N, :]).then_inc(s_x, 16)

                for to, frm in ((src_in, src), (dst_in, dst), (ea_in, edge_weight)):
                    sp.dma_start(to, frm.rearrange("(p j) -> p j", p=P)).then_inc(s_ein, 16)
                sp.dma_start(attrs[0:E, :].rearrange("(p j) f -> p (j f)", p=P),
                             edge_attr.rearrange("(p j) f -> p (j f)", p=P)).then_inc(s_attr, 16)
                sp.wait_ge(s_attr, 16)

            @block.gpsimd
            def _(pool):
                pool.memset(ident[:, :], 0.0).then_inc(s_const, 1)
                pool.wait_ge(s_const, 1)
                pool.affine_select(out=ident[:, :], in_=ident[:, :], compare_op=ALU.not_equal, fill=1.0,
                                   base=0, pattern=[[-1, P]], channel_multiplier=1).then_inc(s_const, 1)
                pool.iota(iota_row[:, :], [[1, P]], base=0, channel_multiplier=0,
                          allow_small_or_imprecise_dtypes=True)
                pool.iota(first_node[:, :], [[0, 1]], base=0, channel_multiplier=P,
                          allow_small_or_imprecise_dtypes=True)
                pool.memset(rec_pad, 0.0).then_inc(s_pad, 1)
                pool.memset(attr_pad, 0.0).then_inc(s_pad, 1)
                pool.memset(rec3[:, :, RW - 1:RW], 0.0).then_inc(s_pad, 1)
                pool.wait_ge(s_pad, 3)
                pool.memset(pad3[:, :, RDST:RDST + 1], FAR).then_inc(s_pad, 1)
                pool.wait_ge(s_pad, 4)
                pool.dma_start(records[E:EPAD, :].rearrange("(p j) f -> p (j f)", p=P), rec_pad).then_inc(s_est, 16)
                pool.dma_start(attrs[E:EPAD, :].rearrange("(p j) f -> p (j f)", p=P), attr_pad).then_inc(s_est, 16)
                pool.dma_start(flat[E:EPAD].rearrange("(p j) -> p j", p=P), pad3[:, :, RDST],
                               allow_slow_non_contiguous=True).then_inc(s_est, 16)
                pool.wait_ge(s_ein, 48)
                pool.tensor_copy(dst_f, dst_in).then_inc(s_cp, 1)
                pool.tensor_copy(rec3[:, :, RSRC].bitcast(i32), src_in).then_inc(s_cp, 1)
                pool.tensor_copy(rec3[:, :, RDST], dst_in).then_inc(s_cp, 1)
                pool.tensor_copy(rec3[:, :, REA], ea_in).then_inc(s_cp, 1)
                pool.wait_ge(s_cp, 4)
                pool.dma_start(records[0:E, :].rearrange("(p j) f -> p (j f)", p=P), rec_out).then_inc(s_est, 16)
                pool.dma_start(flat[0:E].rearrange("(p j) -> p j", p=P), dst_f).then_inc(s_est, 16)
                pool.wait_ge(s_est, 80)

            @block.vector
            def _(dve):
                dve.memset(xs[:, NB - 1, :], 0.0).then_inc(s_tail, 1)
                dve.wait_ge(s_x, 32)

                def moments(g, j):
                    b = 2 * g + j
                    dve.bn_stats(stats[:, bass.ds(b, 1), :].rearrange("p o c -> p (o c)"),
                                 xs[:, bass.ds(b, 1), :].rearrange("p o c -> p (o c)")).then_inc(s_bn, 1)
                drive(dve, moments, NB, 2)
                dve.wait_ge(s_bn, NB)
                even, odd, even_sq, odd_sq = (stats[:, :, n] for n in (1, 4, 2, 5))
                dve.tensor_tensor(mean[:, :], even, odd, ALU.add)
                dve.tensor_tensor(shift[:, :], even, odd, ALU.subtract)
                dve.tensor_tensor(rstd[:, :], even_sq, odd_sq, ALU.add).then_inc(s_bn, 1)
                dve.wait_ge(s_bn, NB + 1)
                dve.scalar_tensor_tensor(shift[:, :], shift[:, :], 0.25, shift[:, :], ALU.mult, ALU.mult)
                dve.tensor_scalar(rstd[:, :], rstd[:, :], 1.0 / C, 1e-5, ALU.mult, ALU.add).then_inc(s_bn, 1)
                dve.wait_ge(s_bn, NB + 2)
                dve.tensor_tensor(rstd[:, :], rstd[:, :], shift[:, :], ALU.add).then_inc(s_rstd, 1)
                dve.wait_ge(s_std, 1)
                dve.reciprocal(rstd[:, :], rstd[:, :]).then_inc(s_rstd, 1)
                dve.wait_ge(s_rstd, 2)
                dve.scalar_tensor_tensor(shift[:, :], mean[:, :], -0.5, rstd[:, :], ALU.mult, ALU.mult).then_inc(s_rstd, 1)
                dve.wait_ge(s_w, 48)

                def copy_hT(g, j):
                    b = 2 * g + j
                    dve.wait_ge(s_hT, b + 1)
                    need(dve, s_mm, b - 1)
                    dve.tensor_copy(hT[:, j, :], PS[j][:, 0:C]).then_inc(s_hTs, 1)

                def rows(g, j):
                    b = 2 * g + j
                    if not isinstance(b, int) or b + 1 < NB:
                        copy_hT(g + j, 1 - j)
                    dve.wait_ge(s_mm, b + 1)
                    need(dve, s_nst[j], 32 * g)
                    dve.tensor_tensor(node_out[:, j, :], PS[2 + j][:, 0:2 * C], bsrc2[:, :], ALU.add).then_inc(s_no, 1)
                    rest = node_out[:, j, C:2 * C]
                    for n in range(PARTS):
                        dve.wait_ge(s_no, b + 1) if n == 0 else dve.wait_ge(s_part, (2 * PARTS - 1) * b + 2 * n)
                        dve.tensor_copy(dst_parts[:, j, n], rest).then_inc(s_part, 1)
                        if n + 1 < PARTS:
                            dve.wait_ge(s_part, (2 * PARTS - 1) * b + 2 * n + 1)
                            dve.tensor_tensor(rest, rest, dst_parts[:, j, n], ALU.subtract).then_inc(s_part, 1)
                dve.memset(bsrc2[:, C:2 * C], 0.0)
                dve.tensor_copy(bsrc2[:, 0:C], bsrc[:, :]).then_inc(s_rstd, 1)
                dve.wait_ge(s_const, 2)
                dve.tensor_copy(ident_h[:, :], ident[:, :])
                dve.wait_ge(s_rstd, 4)
                copy_hT(0, 0)
                drive(dve, rows, NB, 2)

            @block.scalar
            def _(act):
                act.wait_ge(s_rstd, 1)
                act.activation(rstd[:, :], rstd[:, :], ACT.Sqrt).then_inc(s_std, 1)
                act.wait_ge(s_rstd, 3)

                def store(g, j):
                    b = 2 * g + j
                    act.wait_ge(s_part, (2 * PARTS - 1) * (b + 1))
                    act.dma_start(msg_src[bass.ds(b * P, P), :], node_out[:, j, 0:C]).then_inc(s_nst[j], 16)
                    act.dma_start(msg_dst[bass.ds(b, 1), :, :].rearrange("o p c -> p (o c)"),
                                  dst_parts[:, j].rearrange("p n c -> p (n c)")).then_inc(s_nst[j], 16)

                def norm(g, j):
                    b = 2 * g + j
                    need(act, s_hT, b - 1)
                    act.activation(h[:, j, :], xs[:, bass.ds(b, 1), :].rearrange("p o c -> p (o c)"), ACT.Relu,
                                   bias=shift[:, bass.ds(b, 1)], scale=rstd[:, bass.ds(b, 1)]).then_inc(s_h, 1)
                    if isinstance(b, int) and b < 2:
                        return
                    store(g - 1, j)
                drive(act, norm, NB, 2)
                store(NB // 2 - 1, 0)
                store(NB // 2 - 1, 1)
                for j in range(2):
                    act.wait_ge(s_nst[j], 32 * (NB // 2))

            @block.tensor
            def _(pe):
                pe.wait_ge(s_const, 2)
                pe.wait_ge(s_w, 48)

                def transpose(g, j):
                    b = 2 * g + j
                    pe.wait_ge(s_h, b + 1)
                    need(pe, s_hTs, b - 1)
                    pe.transpose(PS[j][:, 0:C], h[:, j, :], ident[:, :]).then_inc(s_hT, 1)

                def product(g, j):
                    b = 2 * g + j
                    if not isinstance(b, int) or b + 1 < NB:
                        transpose(g + j, 1 - j)
                    pe.wait_ge(s_hTs, b + 1)
                    need(pe, s_no, b - 1)
                    pe.matmul(PS[2 + j][:, 0:2 * C], lhsT=hT[:, j, :], rhs=wnode[:, :], start=True, stop=True).then_inc(s_mm, 1)
                transpose(0, 0)
                drive(pe, product, NB, 2)

        with ExitStack() as part, nc.Block() as block:
            def tb(name, shape, dt=f32):
                return part.enter_context(nc.sbuf_tensor(name, shape, dt))
            def ts(name):
                return part.enter_context(nc.semaphore(name))
            following = tb("following", [P, 1], i32)
            steps_down = tb("steps_down", [P, 1])
            ones = tb("ones_check", [P, 1])
            s_clear, s_f, s_v, s_p = ts("following_cleared"), ts("following_in"), ts("check_steps"), ts("check_summed")

            @block.sync
            def _(sp):
                sp.wait_ge(s_clear, 1)
                sp.dma_start(following[0:P - 1, :], bass.AP(tensor=dst.tensor, offset=dst.offset + EC, ap=[[EC, P - 1], [1, 1]]),
                             allow_slow_non_contiguous=True).then_inc(s_f, 16)

            @block.vector
            def _(dve):
                dve.memset(following[:, :], 2 ** 24)
                dve.memset(ones[:, :], 1.0).then_inc(s_clear, 1)
                dve.wait_ge(s_f, 16)
                dve.tensor_copy(dst_next[:, EC:EC + 1], following[:, :]).then_inc(s_v, 1)
                dve.wait_ge(s_v, 1)
                dve.tensor_tensor(ea_in, dst_next[:, 0:EC], dst_next[:, 1:EC + 1], ALU.is_gt).then_inc(s_v, 1)
                dve.wait_ge(s_v, 2)
                dve.tensor_reduce(steps_down[:, :], ea_in, mybir.AxisListType.X, ALU.add).then_inc(s_v, 1)
                dve.wait_ge(s_p, 1)
                dve.tensor_scalar(unsorted[:, :], PS[0][0:1, 0:1], 0.5, None, ALU.is_gt)

            @block.tensor
            def _(pe):
                pe.wait_ge(s_v, 3)
                pe.matmul(PS[0][0:1, 0:1], lhsT=steps_down[:, :], rhs=ones[:, :], start=True, stop=True).then_inc(s_p, 1)

        with ExitStack() as part, nc.Block() as block:
            def tb(name, shape, dt=f32):
                return part.enter_context(nc.sbuf_tensor(name, shape, dt))
            def ts(name):
                return part.enter_context(nc.semaphore(name))
            keys = tb("keys", [P, SS, RW])
            moved = tb("moved", [P, SS, RAD])
            bounds = tb("bounds", [P, P + 1])
            reached = tb("reached", [P, P + 1])
            quotient = tb("quotient", [P, 1])
            digit = tb("digit", [P, P])
            total = tb("total", [P, P])
            place = tb("place", [P, P])
            ranked = tb("ranked", [P, P])
            where_f = tb("where_f", [P, 1])
            where = tb("where", [P, SS], i32)
            ones = tb("ones_sort", [P, P])
            before = tb("before", [P, P])
            s_c, s_c2 = ts("sort_constants"), ts("sort_ones")
            loops = []
            for n, (frm, to) in enumerate((((records, attrs), (records_by_low, attrs_by_low)),
                                           ((records_by_low, attrs_by_low), (records, attrs)))):
                for moving in (False, True):
                    tag = f"{n}{int(moving)}"
                    n_digit = 4 if n == 0 else 2
                    loops.append((n, moving, frm, to, n_digit, n_digit + (5 if moving else 1),
                                  ts("free" + tag), ts("loaded" + tag), ts("vector" + tag), ts("product" + tag),
                                  [ts(f"scattered{tag}{s}") for s in range(SS)] if moving else [], ts("base" + tag), ts("go" + tag)))

            def subtiles(v):
                return v[0:E].rearrange("(t s p) f -> t p s f", s=SS, p=P)

            @block.sync
            def _(sp):
                flag = sp.value_load(unsorted[0:1, 0:1], min_val=0, max_val=1)
                with sp.If(flag == 1):
                    for n, moving, frm, to, n_digit, n_ops, free, loaded, vec, prod, scat, base_s, go in loops:
                        with sp.Fori(0, NS) as t:
                            sp.wait_ge(free, t + 1)
                            sp.dma_start(keys[:, :, :], subtiles(frm[0])[bass.ds(t, 1)].rearrange("o p s f -> p (o s) f")).then_inc(loaded, 16)
                            if moving:
                                sp.dma_start(moved[:, :, :], subtiles(frm[1])[bass.ds(t, 1)].rearrange("o p s f -> p (o s) f")).then_inc(loaded, 16)

            @block.gpsimd
            def _(pool):
                flag = pool.value_load(unsorted[0:1, 0:1], min_val=0, max_val=1)
                with pool.If(flag == 1):
                    pool.iota(bounds[:, :], [[P, P + 1]], base=0, channel_multiplier=0, allow_small_or_imprecise_dtypes=True).then_inc(s_c, 1)
                    pool.wait_ge(s_c2, 1)
                    pool.affine_select(out=before[:, :], in_=ones[:, :], compare_op=ALU.is_gt, fill=0.0,
                                       base=0, pattern=[[1, P]], channel_multiplier=-1).then_inc(s_c, 1)
                    for n, moving, frm, to, n_digit, n_ops, free, loaded, vec, prod, scat, base_s, go in loops:
                        if not moving:
                            continue
                        with pool.Fori(0, NS) as t:
                            for s in range(SS):
                                pool.wait_ge(vec, (t * SS + s + 1) * n_ops)
                                pool.sem_inc(go, 1)
                                at = bass.IndirectOffsetOnAxis(ap=where[:, s:s + 1], axis=0)
                                pool.indirect_dma_start(to[0][0:E], at, keys[:, s], None).then_inc(scat[s], 16)
                                pool.indirect_dma_start(to[1][0:E], at, moved[:, s], None).then_inc(scat[s], 16)
                                if n == 1:
                                    pool.indirect_dma_start(flat[0:E].rearrange("(e a) -> e a", a=1), at,
                                                            keys[:, s, RDST:RDST + 1], None).then_inc(scat[s], 16)
                            for s in range(SS):
                                pool.wait_ge(scat[s], (t + 1) * (48 if n == 1 else 32))
                            pool.sem_inc(free, 1)
                        if n == 0:
                            pool.sem_inc(loops[2][6], 1)

            @block.vector
            def _(dve):
                flag = dve.value_load(unsorted[0:1, 0:1], min_val=0, max_val=1)
                with dve.If(flag == 1):
                    dve.memset(ones[:, :], 1.0).then_inc(s_c2, 1)
                    dve.wait_ge(s_c, 2)
                    dve.sem_inc(loops[0][6], 1)
                    for at, (n, moving, frm, to, n_digit, n_ops, free, loaded, vec, prod, scat, base_s, go) in enumerate(loops):
                        if not moving:
                            dve.memset(total[:, :], 0.0).then_inc(base_s, 1)
                            dve.wait_ge(base_s, 1)
                        else:
                            dve.tensor_tensor_scan(place[:, :], ones[:, :], total[:, :], 0.0, ALU.mult, ALU.add).then_inc(base_s, 1)
                            dve.wait_ge(base_s, 1)
                            dve.tensor_tensor(place[:, :], place[:, :], total[:, :], ALU.subtract).then_inc(base_s, 1)
                            dve.wait_ge(base_s, 2)
                            dve.sem_inc(free, 1)
                        with dve.Fori(0, NS) as t:
                            dve.wait_ge(loaded, (t + 1) * (32 if moving else 16))
                            for s in range(SS):
                                def done(ins, k):
                                    ins.then_inc(vec, 1)
                                    dve.wait_ge(vec, (t * SS + s) * n_ops + k)
                                key = keys[:, s, RDST:RDST + 1]
                                done(dve.tensor_scalar(reached[:, :], bounds[:, :], key, None, ALU.is_le), 1)
                                if n == 0:
                                    done(dve.tensor_reduce(quotient[:, :], reached[:, 1:P + 1], mybir.AxisListType.X, ALU.add), 2)
                                    done(dve.scalar_tensor_tensor(quotient[:, :], quotient[:, :], -float(P), key, ALU.mult, ALU.add), 3)
                                    done(dve.tensor_scalar(digit[:, :], iota_row[:, :], quotient[:, :], None, ALU.is_equal), 4)
                                else:
                                    done(dve.tensor_tensor(digit[:, :], reached[:, 0:P], reached[:, 1:P + 1], ALU.subtract), 2)
                                dve.wait_ge(prod, t * SS + s + 1)
                                if not moving:
                                    done(dve.tensor_tensor(total[:, :], total[:, :], PS[1][:, 0:P], ALU.add), n_digit + 1)
                                    continue
                                done(dve.tensor_tensor(ranked[:, :], place[:, :], PS[0][:, 0:P], ALU.add), n_digit + 1)
                                done(dve.tensor_tensor(ranked[:, :], ranked[:, :], digit[:, :], ALU.mult), n_digit + 2)
                                done(dve.tensor_reduce(where_f[:, :], ranked[:, :], mybir.AxisListType.X, ALU.add), n_digit + 3)
                                done(dve.tensor_tensor(place[:, :], place[:, :], PS[1][:, 0:P], ALU.add), n_digit + 4)
                                done(dve.tensor_copy(where[:, s:s + 1], where_f[:, :]), n_digit + 5)
                            if not moving:
                                dve.sem_inc(free, 1)

            @block.tensor
            def _(pe):
                flag = pe.value_load(unsorted[0:1, 0:1], min_val=0, max_val=1)
                with pe.If(flag == 1):
                    pe.wait_ge(s_c, 2)
                    for n, moving, frm, to, n_digit, n_ops, free, loaded, vec, prod, scat, base_s, go in loops:
                        with pe.Fori(0, NS) as t:
                            for s in range(SS):
                                pe.wait_ge(vec, (t * SS + s) * n_ops + n_digit)
                                if moving:
                                    pe.matmul(PS[0][:, 0:P], lhsT=before[:, :], rhs=digit[:, :], start=True, stop=True)
                                pe.matmul(PS[1][:, 0:P], lhsT=ones[:, :], rhs=digit[:, :], start=True, stop=True).then_inc(prod, 1)

        with ExitStack() as part, nc.Block() as block:
            def tb(name, shape, dt=f32):
                return part.enter_context(nc.sbuf_tensor(name, shape, dt))
            def ts(name):
                return part.enter_context(nc.semaphore(name))
            firsts = tb("firsts", [1, NT - 1])
            ones = tb("ones", [P, P])
            begun_by = tb("begun_by", [P, 1])
            below = SC[:, 0:NT - 1]
            iota_w = SC[:, 1024:1024 + NI]
            begun = SC[:, 2048:2048 + NI]
            blocks = SC[:, 3072:3072 + NI]
            tiles = SC[:, 4096:4096 + NI]
            starts = SC[:, 5120:5120 + P]
            lasts = SC[:, 5248:5248 + P]
            s_wz, s_wl, s_f, s_io = ts("weights_cleared"), ts("weights_in"), ts("firsts_in"), ts("iota_made")
            s_v, s_p, s_st = ts("vector_steps"), ts("products"), ts("tables_stored")
            halves = [(0, 512), (512, NT - 1)]
            whalves = [(0, 512), (512, NI)]

            @block.sync
            def _(sp):
                sp.dma_start(firsts[:, :], dst_rows[1:NT, 0:1].rearrange("t a -> a t"),
                             allow_slow_non_contiguous=True).then_inc(s_f, 16)
                sp.wait_ge(s_wz, 1)
                loads = []
                for s in range(SUB):
                    loads.append((w1[RAD * s:RAD * (s + 1), s // 2, FC * (s % 2):FC * (s % 2 + 1)], fc_w1))
                for q in range(2):
                    rows = slice(FC * q, FC * (q + 1))
                    loads += [(w2[rows, FC * q:FC * (q + 1)], fc_w2), (w3[rows, q, :], fc_w3),
                              (b1[rows, :], column(fc_b1)), (b2[rows, :], column(fc_b2))]
                loads.append((b3[:, :], column(fc_b3)))
                for hd in range(H):
                    loads.append((adot[AH * hd:AH * (hd + 1), hd:hd + 1], alpha_dot[0, hd, :].rearrange("(k a) -> k a", a=1)))
                    loads.append((ba[AH * hd:AH * (hd + 1), :], column(b_sep[2 * AH * hd:2 * AH * hd + AH])))
                loads += [(wsep[:, :, :, :].rearrange("p h t k -> p (h t k)"), w_sep), (wproj[:, :], w_proj),
                          (bval[:, :, :, :].rearrange("p h t k -> p (h t k)"), spread(b_sep, P)),
                          (bproj[:, :], spread(b_proj, P))]
                for to, frm in loads:
                    sp.dma_start(to, frm).then_inc(s_wl, 16)
                sp.wait_ge(s_wl, 16 * len(loads))
                sp.wait_ge(s_v, 9)
                sp.dma_start(tile_of.rearrange("(a w) -> a w", a=1), steer[0:1, 0:NI]).then_inc(s_st, 16)
                sp.dma_start(base_of.rearrange("(a w) -> a w", a=1), base[0:1, :]).then_inc(s_st, 16)
                sp.wait_ge(s_st, 32)
            n_loads = SUB + 8 + 1 + 2 * H + 4

            @block.gpsimd
            def _(pool):
                pool.iota(iota_w, [[1, NI]], base=0, channel_multiplier=0,
                          allow_small_or_imprecise_dtypes=True).then_inc(s_io, 1)

            @block.vector
            def _(dve):
                for t in (w1, w2, w3, adot):
                    last = dve.memset(t[(slice(None),) * len(t.shape)], 0.0)
                last.then_inc(s_wz, 1)
                dve.memset(ones[:, :], 1.0).then_inc(s_v, 1)
                dve.wait_ge(s_f, 16)
                dve.engine_nop().then_inc(s_v, 1)
                dve.wait_ge(s_p, 1)
                for n, (a, z) in enumerate(halves):
                    dve.tensor_scalar(below[:, a:z], PS[n][:, 0:z - a], first_node[:, :], None, ALU.is_lt).then_inc(s_v, 1)
                dve.wait_ge(s_v, 4)
                dve.tensor_reduce(begun_by[:, :], below, mybir.AxisListType.X, ALU.add).then_inc(s_v, 1)
                dve.wait_ge(s_v, 5)
                dve.scalar_tensor_tensor(begun_by[:, :], first_node[:, :], 1.0 / P, begun_by[:, :], ALU.mult, ALU.add).then_inc(s_v, 1)
                dve.wait_ge(s_v, 6)
                dve.wait_ge(s_io, 1)
                dve.tensor_scalar(begun, iota_w, begun_by[:, :], None, ALU.is_ge).then_inc(s_v, 1)
                dve.wait_ge(s_p, 2)
                for n, (a, z) in enumerate(whalves):
                    dve.tensor_scalar(base[:, a:z], PS[2 + n][:, 0:z - a], -1.0, float(P), ALU.add, ALU.mult)
                    dve.tensor_scalar(blocks[:, a:z], PS[2 + n][:, 0:z - a], -1.0, None, ALU.add)
                last = dve.tensor_scalar(starts, PS[4][:, 0:P], -1.0, None, ALU.add)
                last.then_inc(s_v, 1)
                dve.wait_ge(s_v, 8)
                dve.tensor_tensor(tiles, iota_w, blocks, ALU.subtract).then_inc(s_io, 1)
                dve.tensor_tensor(keep[:, 1:NI], blocks[:, 1:NI], blocks[:, 0:NI - 1], ALU.is_equal)
                dve.memset(keep[:, 0:1], 0.0)
                dve.tensor_copy(steer[0:1, NI:2 * NI], blocks[0:1, :])
                dve.tensor_copy(last_item[0:1, 0:NB - 1], starts[0:1, 1:NB])
                dve.memset(last_item[0:1, NB - 1:NB], NT - 1 + NB - 1)
                dve.wait_ge(s_io, 2)
                dve.tensor_copy(steer[0:1, 0:NI], tiles[0:1, :]).then_inc(s_v, 1)
                dve.wait_ge(s_wl, 16 * n_loads)
                dve.tensor_copy(wa[:, :].rearrange("p (h k) -> p h k", h=H), wsep[:, :, 0, :])
                dve.tensor_copy(wv[:, :].rearrange("p (h k) -> p h k", h=H), wsep[:, :, 1, :])
                dve.tensor_scalar(adot[:, :], adot[:, :], 0.8, None, ALU.mult).then_inc(s_v, 1)
                dve.wait_ge(s_p, 3)
                dve.tensor_scalar(score_bias[:, :], PS[5][:, 0:1], 0.25, None, ALU.mult)

            @block.tensor
            def _(pe):
                pe.wait_ge(s_v, 2)
                for n, (a, z) in enumerate(halves):
                    last = pe.matmul(PS[n][:, 0:z - a], lhsT=ones[0:1, :], rhs=firsts[:, a:z], start=True, stop=True)
                last.then_inc(s_p, 1)
                pe.wait_ge(s_v, 7)
                for n, (a, z) in enumerate(whalves):
                    pe.matmul(PS[2 + n][:, 0:z - a], lhsT=ones[0:NB, :], rhs=begun[0:NB, a:z], start=True, stop=True)
                pe.matmul(PS[4][:, 0:P], lhsT=begun_by[:, :].broadcast_to((P, P)), rhs=ident[:, :],
                          start=True, stop=True).then_inc(s_p, 1)
                pe.wait_ge(s_v, 10)
                for s in range(SUB):
                    last = pe.matmul(PS[5][32 * s:32 * s + 32, 0:1], lhsT=adot[:, :], rhs=ba[:, :], start=True, stop=True,
                                     tile_position=(0, 32 * s))
                last.then_inc(s_p, 1)

        with ExitStack() as part, nc.Block() as block:
            def tb(name, shape, dt=f32):
                return part.enter_context(nc.sbuf_tensor(name, shape, dt))
            def ts(name):
                return part.enter_context(nc.semaphore(name))
            U = 4
            rec = tb("rec", [P, U, SUB, RW])
            attr = tb("attr", [P, U, SUB * RAD])
            win = tb("win", [P, U, PARTS, C], bf16)
            cut = [0]

            def carve(n, pattern, **dims):
                cut[0] += n
                return AR[:, cut[0] - n:cut[0]].rearrange(pattern, **dims)
            gath = carve(U * SUB * C, "p (j s c) -> p j s c", j=U, s=SUB)
            vout = carve(U * SUB * VW, "p (j s c) -> p j s c", j=U, s=SUB)
            hot = tb("hot", [P, 2, SUB, P], bf16)
            hotT = tb("hotT", [P, 2, TE], bf16)
            recT = tb("recT", [P, 2, P])
            h1 = tb("h1", [P, 2, 2 * P])
            h2 = tb("h2", [P, 2, 2 * P])
            sout = carve(U * P, "p (j n) -> p j n", j=U)
            xe = carve(2 * TE, "p (j s c) -> p j s c", j=2, s=SUB)
            rads, msgT, sil = (carve(2 * TE, "p (j n) -> p j n", j=2) for _ in range(3))
            s_rec = [ts(f"rec_in{j}") for j in range(U)]
            s_win = [ts(f"window_in{j}") for j in range(U)]
            s_gath = [ts(f"gathered{j}") for j in range(U)]
            s_vst = [ts(f"values_stored{j}") for j in range(U)]
            s_rel, s_hot, s_recT, s_hotT = ts("relative_done"), ts("hot_done"), ts("recT_done"), ts("hotT_done")
            s_recTs, s_hotTs = ts("recT_copied"), ts("hotT_copied")
            s_z1, s_h1, s_z2, s_h2, s_rad, s_rads = ts("z1_done"), ts("h1_done"), ts("z2_done"), ts("h2_done"), ts("rad_done"), ts("rad_copied")
            s_D, s_x, s_xT, s_msg = ts("dst_rows_done"), ts("summed"), ts("xT_done"), ts("message_done")
            s_a, s_v, s_sil, s_al, s_sc = ts("alpha_in_done"), ts("values_done"), ts("silu_done"), ts("alpha_done"), ts("scores_done")
            s_sum = ts("parts_added")
            s_vout, s_scout, s_go = ts("values_copied"), ts("scores_copied"), ts("gathers_begun")
            recT_ps, z1_ps = PS[1][:, 0:P], PS[1][:, 2 * P:4 * P]
            z2_ps = z1_ps
            sc_ps = PS[0][:, 0:P]
            rad_ps, hotT_ps, d_ps, xT_ps, a_ps, v_ps = (PS[n][:, :] for n in range(2, 8))
            hotT_ps = hotT_ps.bitcast(bf16)[:, 0:TE]
            rec_v = records.rearrange("(t p s) f -> t p (s f)", p=P, s=SUB)
            attr_v = attrs.rearrange("(t p s) f -> t p (s f)", p=P, s=SUB)

            def there(i):
                return not isinstance(i, int) or 0 <= i < NI

            def later(g, j, d):
                return g + (j + d) // U, (j + d) % U

            @block.sync
            def _(sp):
                def store(g, j):
                    i = U * g + j
                    sp.wait_ge(s_vout, i + 1)
                    sp.dma_start(values[bass.ds(i, 1)].rearrange("o p c -> p (o c)"),
                                 vout[:, j].rearrange("p s c -> p (s c)")).then_inc(s_vst[j], 16)
                    sp.wait_ge(s_scout, i + 1)
                    sp.dma_start(scores[bass.ds(i, 1)].rearrange("o q n -> q (o n)"), sout[:, j]).then_inc(s_vst[j], 16)

                def load(g, j):
                    i = U * g + j
                    t = sp.value_load(steer[0:1, bass.ds(i, 1)], min_val=0, max_val=TPAD - 1)
                    b = sp.value_load(steer[0:1, bass.ds(NI + i, 1)], min_val=0, max_val=NB - 1)
                    need(sp, s_x, i - U + 1)
                    sp.dma_start(rec[:, j].rearrange("p s f -> p (s f)"),
                                 rec_v[bass.ds(t, 1)].rearrange("o p f -> p (o f)")).then_inc(s_rec[j], 16)
                    sp.dma_start(attr[:, j], attr_v[bass.ds(t, 1)].rearrange("o p f -> p (o f)")).then_inc(s_rec[j], 16)
                    sp.dma_start(win[:, j].rearrange("p n c -> p (n c)"), msg_dst[bass.ds(b, 1)].rearrange("o p c -> p (o c)")).then_inc(s_win[j], 16)
                    if not (isinstance(g, int) and g == 0):
                        store(g - 1, j)
                drive(sp, load, NI, U)
                for j in range(U):
                    store(NI // U - 1, j)
                for j in range(U):
                    sp.wait_ge(s_vst[j], 32 * (NI // U))

            @block.gpsimd
            def _(pool):
                def gather(g, j):
                    i = U * g + j
                    need(pool, s_x, i - U + 1)
                    pool.wait_ge(s_rec[j], 32 * g + 32)
                    pool.sem_inc(s_go, 1)
                    for s in range(SUB):
                        pool.indirect_dma_start(
                            gath[:, j, s], None, msg_src,
                            bass.IndirectOffsetOnAxis(ap=rec[:, j, s, RSRC:RSRC + 1].bitcast(i32), axis=0)
                        ).then_inc(s_gath[j], 16)
                drive(pool, gather, NI, U)

            @block.vector
            def _(dve):
                def prepare(g, j):
                    i = U * g + j
                    dve.wait_ge(s_rec[j], 32 * g + 32)
                    need(dve, s_vst[j], 32 * g)
                    rel = vout[:, j, :, C]
                    dve.tensor_scalar(rel, rec[:, j, :, RDST], base[:, bass.ds(i, 1)], None, ALU.subtract).then_inc(s_rel, 1)
                    dve.wait_ge(s_rel, i + 1)
                    need(dve, s_hotT, i - 1)
                    dve.tensor_tensor(hot[:, j % 2], iota_row[:, :].unsqueeze(1).broadcast_to((P, SUB, P)),
                                      rel.unsqueeze(2).broadcast_to((P, SUB, P)), ALU.is_equal).then_inc(s_hot, 1)

                def copy_recT(g, j):
                    i = U * g + j
                    dve.wait_ge(s_recT, i + 1)
                    need(dve, s_z1, i - 1)
                    dve.tensor_copy(recT[:, j % 2], recT_ps).then_inc(s_recTs, 1)

                def add_parts(g, j):
                    i = U * g + j
                    dve.wait_ge(s_D, i + 1)
                    dve.wait_ge(s_gath[j], 16 * SUB * (g + 1))
                    dve.tensor_tensor(gath[:, j], gath[:, j], d_ps.rearrange("p (s c) -> p s c", s=SUB), ALU.add).then_inc(s_sum, 1)
                    need(dve, s_xT, i - 1)
                    dve.wait_ge(s_sum, i + 1)
                    dve.tensor_tensor(xe[:, j % 2], gath[:, j], rec[:, j, :, REA].unsqueeze(2).broadcast_to((P, SUB, C)),
                                      ALU.mult).then_inc(s_x, 1)

                def copy_out(g, j):
                    i = U * g + j
                    dve.wait_ge(s_v, i + 1)
                    dve.tensor_copy(vout[:, j, :, 0:C], v_ps.rearrange("p (s c) -> p s c", s=SUB)).then_inc(s_vout, 1)
                    dve.wait_ge(s_sc, i + 1)
                    dve.tensor_scalar(sout[:, j], sc_ps, score_bias[:, :], None, ALU.add).then_inc(s_scout, 1)

                def step(g, j):
                    i = U * g + j
                    q = j % 2
                    if there(i + 1):
                        copy_recT(*later(g, j, 1))
                    dve.wait_ge(s_xT, i + 1)
                    dve.wait_ge(s_rads, i + 1)
                    need(dve, s_v, i - 1)
                    dve.tensor_tensor(msgT[:, q], xT_ps, rads[:, q], ALU.mult).then_inc(s_msg, 1)
                    if there(i - 1):
                        copy_out(*later(g, j, -1))
                    if there(i + 1):
                        add_parts(*later(g, j, 1))
                    dve.wait_ge(s_a, i + 1)
                    dve.wait_ge(s_sil, i + 1)
                    dve.scalar_tensor_tensor(sil[:, q], a_ps, 0.25, sil[:, q], ALU.mult, ALU.add).then_inc(s_al, 1)
                    if there(i + 2):
                        prepare(*later(g, j, 2))
                prepare(0, 0)
                prepare(0, 1)
                copy_recT(0, 0)
                add_parts(0, 0)
                drive(dve, step, NI, U)
                copy_out(NI // U - 1, U - 1)

            @block.scalar
            def _(act):
                def copy_hotT(g, j):
                    i = U * g + j
                    act.wait_ge(s_hotT, i + 1)
                    need(act, s_D, i - 1)
                    act.activation(hotT[:, j % 2], hotT_ps, ACT.Copy).then_inc(s_hotTs, 1)

                def first(g, j):
                    i = U * g + j
                    act.wait_ge(s_z1, i + 1)
                    need(act, s_z2, i - 1)
                    act.activation(h1[:, j % 2], z1_ps, ACT.Silu, bias=b1[:, :]).then_inc(s_h1, 1)

                def second(g, j):
                    i = U * g + j
                    act.wait_ge(s_z2, i + 1)
                    need(act, s_rad, i - 1)
                    act.activation(h2[:, j % 2], z2_ps, ACT.Silu, bias=b2[:, :]).then_inc(s_h2, 1)

                def radial(g, j):
                    i = U * g + j
                    act.wait_ge(s_rad, i + 1)
                    need(act, s_msg, i - 1)
                    act.activation(rads[:, j % 2].rearrange("f (p q e) -> f p q e", p=2, q=2),
                                   rad_ps.rearrange("f (q p e) -> f p q e", p=2, q=2),
                                   ACT.Identity, bias=b3[:, :]).then_inc(s_rads, 1)

                def step(g, j):
                    i = U * g + j
                    following = later(g, j, 1)
                    if there(i + 1):
                        copy_hotT(*following)
                        first(*following)
                    act.wait_ge(s_a, i + 1)
                    need(act, s_sc, i - 1)
                    act.activation(sil[:, j % 2], a_ps, ACT.Silu, bias=ba[:, :]).then_inc(s_sil, 1)
                    if there(i + 1):
                        second(*following)
                        radial(*following)
                copy_hotT(0, 0)
                first(0, 0)
                second(0, 0)
                radial(0, 0)
                drive(act, step, NI, U)

            @block.tensor
            def _(pe):
                def transposes(g, j):
                    i = U * g + j
                    pe.wait_ge(s_rec[j], 32 * g + 32)
                    need(pe, s_h2, i)
                    pe.transpose(recT_ps, attr[:, j], ident[:, :]).then_inc(s_recT, 1)
                    pe.wait_ge(s_hot, i + 1)
                    need(pe, s_hotTs, i)
                    for s in range(SUB):
                        last = pe.transpose(hotT_ps[:, s * P:(s + 1) * P], hot[:, j % 2, s], ident_h[:, :])
                    last.then_inc(s_hotT, 1)

                def z1(g, j):
                    i = U * g + j
                    pe.wait_ge(s_recTs, i + 1)
                    for p in range(2):
                        last = pe.matmul(z1_ps[:, p * P:(p + 1) * P], lhsT=w1[:, p], rhs=recT[:, j % 2], start=True, stop=True)
                    last.then_inc(s_z1, 1)

                def z2(g, j):
                    i = U * g + j
                    pe.wait_ge(s_h1, i + 1)
                    pe.matmul(z2_ps, lhsT=w2[:, :], rhs=h1[:, j % 2], start=True, stop=True).then_inc(s_z2, 1)

                def dst_part(g, j):
                    i = U * g + j
                    pe.wait_ge(s_win[j], 16 * g + 16)
                    pe.wait_ge(s_hotTs, i + 1)
                    need(pe, s_sum, i)
                    for s in range(SUB):
                        for n in range(PARTS):
                            last = pe.matmul(d_ps[:, s * C:(s + 1) * C], lhsT=hotT[:, j % 2, s * P:(s + 1) * P],
                                             rhs=win[:, j, n], start=(n == 0), stop=(n == PARTS - 1))
                    last.then_inc(s_D, 1)

                def radial(g, j):
                    i = U * g + j
                    pe.wait_ge(s_h2, i + 1)
                    need(pe, s_rads, i)
                    for q in range(2):
                        last = pe.matmul(rad_ps[:, q * 2 * P:(q + 1) * 2 * P], lhsT=w3[:, q], rhs=h2[:, j % 2], start=True, stop=True)
                    last.then_inc(s_rad, 1)

                def scores(g, j):
                    i = U * g + j
                    pe.wait_ge(s_al, i + 1)
                    need(pe, s_scout, i)
                    for s in range(SUB):
                        last = pe.matmul(sc_ps[32 * s:32 * s + 32, :], lhsT=adot[:, :], rhs=sil[:, j % 2, s * P:(s + 1) * P],
                                         start=True, stop=True, tile_position=(0, 32 * s))
                    last.then_inc(s_sc, 1)

                def step(g, j):
                    i = U * g + j
                    q = j % 2
                    following = later(g, j, 1)
                    if there(i - 1):
                        scores(*later(g, j, -1))
                    if there(i + 1):
                        transposes(*following)
                    pe.wait_ge(s_x, i + 1)
                    need(pe, s_msg, i)
                    for s in range(SUB):
                        last = pe.transpose(xT_ps[:, s * P:(s + 1) * P], xe[:, q, s], ident[:, :])
                    last.then_inc(s_xT, 1)
                    if there(i + 1):
                        z1(*following)
                        dst_part(*following)
                    pe.wait_ge(s_msg, i + 1)
                    need(pe, s_al, i)
                    pe.matmul(a_ps, lhsT=wa[:, :], rhs=msgT[:, q], start=True, stop=True).then_inc(s_a, 1)
                    if there(i + 1):
                        z2(*following)
                    need(pe, s_vout, i)
                    for s in range(SUB):
                        last = pe.matmul(v_ps[:, s * C:(s + 1) * C], lhsT=msgT[:, q, s * P:(s + 1) * P], rhs=wv[:, :], start=True, stop=True)
                    last.then_inc(s_v, 1)
                    if there(i + 1):
                        radial(*following)
                transposes(0, 0)
                z1(0, 0)
                z2(0, 0)
                dst_part(0, 0)
                radial(0, 0)
                drive(pe, step, NI, U)
                scores(NI // U - 1, U - 1)

        with ExitStack() as part, nc.Block() as block:
            def tb(name, shape, dt=f32):
                return part.enter_context(nc.sbuf_tensor(name, shape, dt))
            def ts(name):
                return part.enter_context(nc.semaphore(name))
            L = IPC * TE
            change = AR[:, :].bitcast(bf16)[:, 0:L + 1]
            tiles_c = tb("tiles_c", [P, IPC], i32)
            lowest = tb("lowest", [P, IPC])
            highest = tb("highest", [P, IPC])
            index = tb("index", [P, 2], i32)
            drow = tb("drow", [P, 2, TE + 1])
            off = tb("off", [P, 2, TE])
            raw = tb("raw", [P, 2, TE])
            stage = tb("stage", [P, 2, TE])
            dfirst = tb("dfirst", [P, 1])
            edge = tb("edge", [P, 4])
            flags = tb("flags", [P, 4])
            small = tb("small", [H, 6, CH])
            back = tb("back", [P, 1])
            s_t, s_idx, s_pre = ts("chunk_tables_in"), ts("index_ready"), ts("table_steps")
            s_g = [ts(f"dst_gathered{j}") for j in range(2)]
            s_col, s_row, s_masked = ts("before_copied"), ts("changes_made"), ts("scores_masked")
            s_off = ts("offsets_steps")
            s_scin = ts("scores_in")
            s_staged, s_go = ts("scores_staged"), ts("gathers_begun")
            s_c, s_cd, s_dump = ts("chain"), ts("chain_dma"), ts("scores_dumped")
            s_raw = [ts(f"raw_in{j}") for j in range(2)]
            s_sub, s_exp, s_wt, s_wc = ts("subtracted"), ts("exp_done"), ts("weights_transposed"), ts("weights_copied")
            sc_k = SC[:, :].rearrange("p (k n) -> p k n", n=TE)

            @block.sync
            def _(sp):
                for c in range(CH):
                    rows = slice(c * H, (c + 1) * H)
                    sp.dma_start(tiles_c[rows, :], spread(tile_of[c * IPC:(c + 1) * IPC], H)).then_inc(s_t, 16)
                    sp.dma_start(lowest[rows, :], spread(base_of[c * IPC:(c + 1) * IPC], H)).then_inc(s_t, 16)
                by_chunk = scores.rearrange("(c k) (s m) n -> c m (k s) n", c=CH, s=SUB)
                for c in range(CH):
                    sp.dma_start(SC[c * H:(c + 1) * H, :].rearrange("q (k n) -> q k n", n=P), by_chunk[c, 0:H]).then_inc(s_scin, 16)
                sp.wait_ge(s_masked, IPC)
                sp.dma_start(masked_scores, SC[:, :]).then_inc(s_dump, 16)
                sp.wait_ge(s_c, 1)
                sp.dma_start(column(edge_col[0]), drow[:, (IPC - 1) % 2, TE:TE + 1]).then_inc(s_cd, 16)
                sp.wait_ge(s_cd, 16)
                sp.dma_start(edge[H:P, 0:1], column(edge_col[0, 0:P - H])).then_inc(s_cd, 16)
                sp.wait_ge(s_c, 2)
                sp.dma_start(column(edge_col[1]), flags[:, 0:1]).then_inc(s_cd, 16)
                sp.wait_ge(s_cd, 48)
                sp.dma_start(edge[0:P - H, 1:2], column(edge_col[1, H:P])).then_inc(s_cd, 16)
                by_head = [edge_col[n].rearrange("(c h) -> h c", h=H) for n in range(4)]
                n = 64
                for way in range(2):
                    sp.wait_ge(s_c, 4 + 3 * way)
                    sp.dma_start(column(edge_col[2]), edge[:, 2:3]).then_inc(s_cd, 16)
                    sp.dma_start(column(edge_col[3]), flags[:, 1:2]).then_inc(s_cd, 16)
                    sp.wait_ge(s_cd, n + 32)
                    sp.dma_start(small[:, 0], by_head[2], allow_slow_non_contiguous=True).then_inc(s_cd, 16)
                    sp.dma_start(small[:, 1], by_head[3], allow_slow_non_contiguous=True).then_inc(s_cd, 16)
                    sp.wait_ge(s_cd, n + 64)
                    sp.wait_ge(s_c, 5 + 3 * way)
                    sp.dma_start(by_head[0], small[:, 2], allow_slow_non_contiguous=True).then_inc(s_cd, 16)
                    sp.wait_ge(s_cd, n + 80)
                    sp.dma_start(edge[:, 3:4], column(edge_col[0])).then_inc(s_cd, 16)
                    n += 96

                def load(g, j):
                    k = 2 * g + j
                    need(sp, s_sub, k - 1)
                    sp.dma_start(raw[:, j], masked_scores[:, bass.ds(k * TE, TE)]).then_inc(s_raw[j], 16)
                sp.wait_ge(s_dump, 16)
                drive(sp, load, IPC, 2)

            @block.gpsimd
            def _(pool):
                def gather(g, j):
                    k = 2 * g + j
                    pool.wait_ge(s_idx, k + 1)
                    pool.sem_inc(s_go, 1)
                    pool.indirect_dma_start(drow[:, j, 1:TE + 1], None, dst_rows,
                                            bass.IndirectOffsetOnAxis(ap=index[:, j:j + 1], axis=0)).then_inc(s_g[j], 16)
                drive(pool, gather, IPC, 2)

            @block.vector
            def _(dve):
                dve.memset(drow[:, 0, 0:1], 2 * FAR)
                dve.memset(edge[:, :], 2 * FAR)
                dve.memset(flags[:, :], 0.0)
                dve.memset(small[:, :, :], -BIG).then_inc(s_pre, 1)
                dve.wait_ge(s_t, 32 * CH)
                dve.tensor_scalar(highest[:, :], lowest[:, :], P - 1.0, None, ALU.add).then_inc(s_pre, 1)
                dve.wait_ge(s_pre, 2)

                def pick(g, j):
                    k = 2 * g + j
                    need(dve, s_off, 2 * (k - 1))
                    need(dve, s_row, k - 1)
                    need(dve, s_col, k - 1)
                    dve.tensor_copy(index[:, j:j + 1], tiles_c[:, bass.ds(k, 1)]).then_inc(s_idx, 1)

                def step(g, j):
                    k = 2 * g + j
                    dve.wait_ge(s_g[j], 16 * g + 16)
                    if not (isinstance(k, int) and k + 1 >= IPC):
                        need(dve, s_row, k)
                        dve.tensor_copy(drow[:, 1 - j, 0:1], drow[:, j, TE:TE + 1]).then_inc(s_col, 1)
                    if not (isinstance(k, int) and k == 0):
                        dve.wait_ge(s_col, k)
                    dve.tensor_tensor(change[:, bass.ds(k * TE, TE)], drow[:, j, 1:TE + 1], drow[:, j, 0:TE],
                                      ALU.not_equal).then_inc(s_row, 1)
                    need(dve, s_masked, k - 1)
                    dve.tensor_scalar(off[:, j], drow[:, j, 1:TE + 1], lowest[:, bass.ds(k, 1)], highest[:, bass.ds(k, 1)],
                                      ALU.max, ALU.min).then_inc(s_off, 1)
                    dve.wait_ge(s_off, 2 * k + 1)
                    dve.tensor_tensor(off[:, j], off[:, j], drow[:, j, 1:TE + 1], ALU.not_equal).then_inc(s_off, 1)
                    if isinstance(k, int) and k == 0:
                        dve.tensor_copy(dfirst[:, :], drow[:, 0, 1:2])
                    dve.wait_ge(s_off, 2 * k + 2)
                    dve.wait_ge(s_staged, k + 1)
                    dve.scalar_tensor_tensor(sc_k[:, bass.ds(k, 1)].rearrange("q o (p s) -> q s (o p)", s=SUB),
                                             off[:, j].rearrange("q (p s) -> q s p", s=SUB), -BIG,
                                             stage[:, j].rearrange("q (s p) -> q s p", s=SUB),
                                             ALU.mult, ALU.add).then_inc(s_masked, 1)
                    if not (isinstance(k, int) and k + 2 >= IPC):
                        pick(g + 1, j)
                pick(0, 0)
                pick(0, 1)
                drive(dve, step, IPC, 2)
                dve.wait_ge(s_row, IPC)
                dve.engine_nop().then_inc(s_c, 1)
                dve.wait_ge(s_cd, 32)
                dve.tensor_tensor(flags[:, 0:1], dfirst[:, :], edge[:, 0:1], ALU.not_equal).then_inc(s_c, 1)
                dve.wait_ge(s_c, 2)
                dve.tensor_copy(change[:, 0:1], flags[:, 0:1])
                dve.memset(back[:, :], 1.0)
                dve.wait_ge(s_cd, 64)
                dve.tensor_scalar(change[:, L:L + 1], edge[:, 1:2], 0.0, None, ALU.not_equal).then_inc(s_c, 1)
                dve.wait_ge(s_c, 3)
                dve.tensor_scalar(change[:, :], change[:, :], -BIG, None, ALU.mult).then_inc(s_row, 1)
                dve.wait_ge(s_dump, 16)
                dve.wait_ge(s_row, IPC + 1)
                for way in range(2):
                    run = slice(None) if way == 0 else slice(None, None, -1)
                    pen = change[:, way:L + way][:, run]
                    val = SC[:, :][:, run]
                    end = L - 1 if way == 0 else 0
                    b = 4 + 3 * way
                    dve.tensor_tensor_scan(val, pen, val, -BIG, ALU.add, ALU.max).then_inc(s_pre, 1)
                    dve.tensor_reduce(flags[:, 1:2], pen, mybir.AxisListType.X, ALU.min).then_inc(s_pre, 1)
                    dve.wait_ge(s_pre, 4 + 3 * way)
                    dve.tensor_copy(edge[:, 2:3], SC[:, end:end + 1]).then_inc(s_c, 1)
                    dve.wait_ge(s_cd, 128 + 96 * way)
                    inner = slice(0, CH - 1) if way == 0 else slice(CH - 1, 0, -1)
                    carry = slice(1, CH) if way == 0 else slice(CH - 2, None, -1)
                    if way == 1:
                        dve.memset(small[:, 2], -BIG).then_inc(s_pre, 1)
                        dve.wait_ge(s_pre, 8)
                    dve.tensor_tensor_scan(small[:, 2, carry], small[:, 1, inner], small[:, 0, inner], -BIG,
                                           ALU.add, ALU.max).then_inc(s_c, 1)
                    dve.wait_ge(s_cd, 160 + 96 * way)
                    dve.tensor_tensor_scan(val, pen, val, edge[:, 3:4], ALU.add, ALU.max).then_inc(s_c, 1)
                    if way == 0:
                        dve.engine_nop().then_inc(s_pre, 1)
                        dve.wait_ge(s_c, b + 2)
                dve.wait_ge(s_c, 9)

                def subtract(g, j):
                    k = 2 * g + j
                    dve.wait_ge(s_raw[j], 16 * g + 16)
                    dve.tensor_tensor(sc_k[:, bass.ds(k, 1)].rearrange("q o n -> q (o n)"), raw[:, j],
                                      sc_k[:, bass.ds(k, 1)].rearrange("q o n -> q (o n)"), ALU.subtract).then_inc(s_sub, 1)
                    if not (isinstance(k, int) and k < 2):
                        copy(g - 1, j)

                def copy(g, j):
                    k = 2 * g + j
                    dve.wait_ge(s_wt, k + 1)
                    dve.tensor_copy(sc_k[:, bass.ds(k, 1)].rearrange("q o n -> q (o n)"), PS[2 + j][:, :]).then_inc(s_wc, 1)
                drive(dve, subtract, IPC, 2)
                for k in range(IPC - 2, IPC):
                    copy(k // 2, k % 2)

            @block.scalar
            def _(act):
                def copy(g, j):
                    k = 2 * g + j
                    need(act, s_masked, k - 1)
                    act.activation(stage[:, j], sc_k[:, bass.ds(k, 1)].rearrange("q o n -> q (o n)"), ACT.Copy).then_inc(s_staged, 1)
                act.wait_ge(s_scin, 16 * CH)
                drive(act, copy, IPC, 2)

                def weigh(g, j):
                    k = 2 * g + j
                    act.wait_ge(s_sub, k + 1)
                    need(act, s_wt, k - 1)
                    row = sc_k[:, bass.ds(k, 1)].rearrange("q o n -> q (o n)")
                    act.activation(stage[:, j], row, ACT.Exp).then_inc(s_exp, 1)
                drive(act, weigh, IPC, 2)

            @block.tensor
            def _(pe):
                def to_edges(g, j):
                    k = 2 * g + j
                    pe.wait_ge(s_exp, k + 1)
                    need(pe, s_wc, k - 1)
                    for s in range(SUB):
                        last = pe.transpose(PS[2 + j][:, s * P:(s + 1) * P], stage[:, j, s:TE:SUB], ident[:, :])
                    last.then_inc(s_wt, 1)
                drive(pe, to_edges, IPC, 2)

        with ExitStack() as part, nc.Block() as block:
            def tb(name, shape, dt=f32):
                return part.enter_context(nc.sbuf_tensor(name, shape, dt))
            def ts(name):
                return part.enter_context(nc.semaphore(name))
            U = 4
            vin = tb("vin", [P, U, SUB, VW])
            hot = tb("hot2", [P, 2, SUB, P])
            wval = tb("wval", [P, 2, SUB, AW])
            run = tb("run", [P, U, AW])
            s_vin = [ts(f"values_in{j}") for j in range(U)]
            s_hot, s_w, s_wv, s_mm, s_run, s_clear = ts("hot2_done"), ts("weights_out"), ts("weighted"), ts("aggregated"), ts("run_done"), ts("run_cleared")
            s_rst = [ts(f"run_stored{j}") for j in range(U)]
            sc_v = SC[:, :].rearrange("p (k s m) -> p k s m", s=SUB, m=CH * H)

            @block.sync
            def _(sp):
                def load(g, j):
                    i = U * g + j
                    need(sp, s_mm, i - U + 1)
                    sp.dma_start(vin[:, j].rearrange("p s c -> p (s c)"),
                                 values[bass.ds(i, 1)].rearrange("o p c -> p (o c)")).then_inc(s_vin[j], 16)
                    if not (isinstance(g, int) and g == 0):
                        store(g - 1, j)

                def store(g, j):
                    i = U * g + j
                    sp.wait_ge(s_run, i + 1)
                    sp.dma_start(sums[bass.ds(i, 1)].rearrange("o p c -> p (o c)"), run[:, j]).then_inc(s_rst[j], 16)
                drive(sp, load, NI, U)
                for j in range(U):
                    store(NI // U - 1, j)
                for j in range(U):
                    sp.wait_ge(s_rst[j], 16 * (NI // U))

            @block.gpsimd
            def _(pool):
                def weigh(g, j):
                    i = U * g + j
                    q = j % 2
                    pool.wait_ge(s_vin[j], 16 * g + 16)
                    pool.wait_ge(s_w, i + 1)
                    pool.tensor_tensor(wval[:, q, :, 0:C].rearrange("p s (h k) -> p s h k", h=H),
                                       vin[:, j, :, 0:C].rearrange("p s (h k) -> p s h k", h=H),
                                       wval[:, q, :, C:AW].unsqueeze(3).broadcast_to((P, SUB, H, AH)), ALU.mult).then_inc(s_wv, 1)
                drive(pool, weigh, NI, U)

            @block.vector
            def _(dve):
                dve.memset(run[:, U - 1], 0.0).then_inc(s_clear, 1)
                dve.wait_ge(s_clear, 1)

                def weigh(g, j):
                    i = U * g + j
                    q = j % 2
                    dve.wait_ge(s_vin[j], 16 * g + 16)
                    need(dve, s_mm, i - 1)
                    dve.tensor_copy(wval[:, q, :, C:AW],
                                    sc_v[:, bass.ds(i % IPC, 1), :, bass.ds((i // IPC) * H, H)].rearrange("p o s h -> p (o s) h")).then_inc(s_w, 1)
                    dve.tensor_tensor(hot[:, q], iota_row[:, :].unsqueeze(1).broadcast_to((P, SUB, P)),
                                      vin[:, j, :, C].unsqueeze(2).broadcast_to((P, SUB, P)), ALU.is_equal).then_inc(s_hot, 1)

                def add(g, j):
                    i = U * g + j
                    dve.wait_ge(s_mm, i + 1)
                    need(dve, s_run, i)
                    need(dve, s_rst[j], 16 * g)
                    dve.scalar_tensor_tensor(run[:, j], run[:, (j - 1) % U], keep[:, bass.ds(i, 1)], PS[j % 2][:, 0:AW],
                                             ALU.mult, ALU.add).then_inc(s_run, 1)

                def step(g, j):
                    weigh(g, j)
                    if not (isinstance(g, int) and g == 0 and j == 0):
                        add(g - (1 if j == 0 else 0), (j - 1) % U)
                drive(dve, step, NI, U)
                add(NI // U - 1, U - 1)

            @block.tensor
            def _(pe):
                def aggregate(g, j):
                    i = U * g + j
                    pe.wait_ge(s_hot, i + 1)
                    pe.wait_ge(s_wv, i + 1)
                    need(pe, s_run, i - 1)
                    for s in range(SUB):
                        last = pe.matmul(PS[j % 2][:, 0:AW], lhsT=hot[:, j % 2, s], rhs=wval[:, j % 2, s],
                                         start=(s == 0), stop=(s == SUB - 1))
                    last.then_inc(s_mm, 1)
                drive(pe, aggregate, NI, U)

        with ExitStack() as part, nc.Block() as block:
            def tb(name, shape, dt=f32):
                return part.enter_context(nc.sbuf_tensor(name, shape, dt))
            def ts(name):
                return part.enter_context(nc.semaphore(name))
            agg = tb("agg", [P, 2, AW])
            xin = tb("xin", [P, 2, C])
            den = tb("den", [P, 2, H])
            mean = tb("mean", [P, 2, C])
            meanT = tb("meanT", [P, 2, C])
            fin = tb("fin", [P, 2, C])
            s_in = [ts(f"sums_in{j}") for j in range(2)]
            s_out = [ts(f"out_stored{j}") for j in range(2)]
            s_d, s_mean, s_T, s_Ts, s_mm, s_res, s_fin = ts("node_steps"), ts("mean_done"), ts("meanT_done"), ts("meanT_copied"), ts("projected"), ts("residual"), ts("out_ready")
            tail = N - (NB - 1) * P

            def nodes(v, b):
                return v[bass.ds(b * P, P), :]

            @block.sync
            def _(sp):
                def load(g, j):
                    b = 2 * g + j
                    last = sp.value_load(last_item[0:1, bass.ds(b, 1)], min_val=0, max_val=NI - 1)
                    need(sp, s_fin, b - 1)
                    sp.dma_start(agg[:, j], sums[bass.ds(last, 1)].rearrange("o p c -> p (o c)")).then_inc(s_in[j], 16)
                    if isinstance(b, int) and b == NB - 1:
                        sp.dma_start(xin[0:tail, j], x[b * P:N, :]).then_inc(s_in[j], 16)
                    else:
                        sp.dma_start(xin[:, j], nodes(x, b)).then_inc(s_in[j], 16)
                    if not (isinstance(g, int) and g == 0):
                        store(g - 1, j)

                def store(g, j):
                    b = 2 * g + j
                    sp.wait_ge(s_fin, b + 1)
                    if isinstance(b, int) and b == NB - 1:
                        sp.dma_start(out[b * P:N, :], fin[0:tail, j]).then_inc(s_out[j], 16)
                    else:
                        sp.dma_start(nodes(out, b), fin[:, j]).then_inc(s_out[j], 16)
                drive(sp, load, NB, 2)
                for j in range(2):
                    store(NB // 2 - 1, j)
                for j in range(2):
                    sp.wait_ge(s_out[j], 16 * (NB // 2))

            @block.vector
            def _(dve):
                def divide(g, j):
                    b = 2 * g + j
                    dve.wait_ge(s_in[j], 32 * g + 32)
                    need(dve, s_T, b - 1)
                    w = agg[:, j, C:AW]
                    heads = mean[:, j].rearrange("p (h k) -> p h k", h=H)
                    dve.tensor_scalar(den[:, j], w, 1e-16, None, ALU.add)
                    dve.tensor_tensor(heads, bval[:, :, 1, :], w.unsqueeze(2).broadcast_to((P, H, AH)), ALU.mult).then_inc(s_d, 1)
                    dve.wait_ge(s_d, 3 * b + 1)
                    dve.reciprocal(den[:, j], den[:, j])
                    dve.tensor_tensor(mean[:, j], mean[:, j], agg[:, j, 0:C], ALU.add).then_inc(s_d, 1)
                    dve.wait_ge(s_d, 3 * b + 2)
                    dve.tensor_tensor(heads, heads, den[:, j].unsqueeze(2).broadcast_to((P, H, AH)), ALU.mult).then_inc(s_mean, 1)
                    need(dve, s_out[j], 16 * g)
                    dve.tensor_tensor(fin[:, j], xin[:, j], bproj[:, :], ALU.add).then_inc(s_d, 1)

                def finish(g, j):
                    b = 2 * g + j
                    dve.wait_ge(s_mm, b + 1)
                    dve.wait_ge(s_d, 3 * b + 3)
                    dve.tensor_tensor(fin[:, j], PS[2 + j][:, 0:C], fin[:, j], ALU.add).then_inc(s_fin, 1)

                def step(g, j):
                    divide(g, j)
                    if isinstance(g, int) and g == 0 and j == 0:
                        return
                    finish(g - (1 - j), 1 - j)
                drive(dve, step, NB, 2)
                finish(NB // 2 - 1, 1)

            @block.scalar
            def _(act):
                def copy(g, j):
                    b = 2 * g + j
                    act.wait_ge(s_T, b + 1)
                    need(act, s_mm, b - 1)
                    act.activation(meanT[:, j], PS[j][:, 0:P], ACT.Copy).then_inc(s_Ts, 1)
                drive(act, copy, NB, 2)

            @block.tensor
            def _(pe):
                def project(g, j):
                    b = 2 * g + j
                    pe.wait_ge(s_mean, b + 1)
                    need(pe, s_Ts, b - 1)
                    pe.transpose(PS[j][:, 0:P], mean[:, j], ident[:, :]).then_inc(s_T, 1)
                    pe.wait_ge(s_Ts, b + 1)
                    need(pe, s_fin, b - 1)
                    pe.matmul(PS[2 + j][:, 0:C], lhsT=meanT[:, j], rhs=wproj[:, :], start=True, stop=True).then_inc(s_mm, 1)
                drive(pe, project, NB, 2)


_INS = ["x", "src", "dst", "edge_attr_32", "edge_weight1", "L0_gnn_w_src", "L0_gnn_b_src", "L0_gnn_w_dst",
        "L0_gnn_fc_w1", "L0_gnn_fc_b1", "L0_gnn_fc_w2", "L0_gnn_fc_b2", "L0_gnn_fc_w3", "L0_gnn_fc_b3",
        "L0_gnn_w_sep", "L0_gnn_b_sep", "L0_gnn_alpha_dot", "L0_gnn_w_proj", "L0_gnn_b_proj"]


def kernel(**inputs):
    import numpy as _np
    import concourse.bacc as _bacc
    from concourse import mybir as _mybir
    from concourse.bass_utils import run_bass_kernel_spmd as _run

    nc = _bacc.Bacc("TRN2", target_bir_lowering=False, num_devices=1)
    arrays, args = {}, []
    for name in _INS:
        a = _np.ascontiguousarray(inputs[name])
        if name == "edge_weight1":
            a = a.reshape(-1)
        arrays[f"in_{name}"] = a
        args.append(nc.dram_tensor(f"in_{name}", a.shape, _mybir.dt.from_np(a.dtype), kind="ExternalInput").ap())
    out = nc.dram_tensor("out", (N, C), _mybir.dt.float32, kind="ExternalOutput").ap()
    gnn_kernel(nc, *args, out)
    r = _run(nc, [arrays], core_ids=[0])
    return r.results[0]["out"]
```

```python
import concourse.bass as bass
from concourse import mybir
from contextlib import ExitStack

P = 128
N, E, C = 12500, 400000, 128
RAD, FC = 32, 64
H, AH = 8, 16
SUB = 4
TE = SUB * P
NB = -(-N // P)
NT = -(-E // TE)
CH = P // H
IPC = -(-(NT + NB - 1) // CH)
NI = CH * IPC
TPAD = NI - NB + 1
EPAD = TPAD * TE
RW = 4
RSRC, RDST, REA = 0, 1, 2
VW = C + 1
AW = C + H
EC = E // P
PADC = EPAD // P - EC
BIG = 1e30
PARTS = 3
FAR = -1e6
SS = 5
NS = E // (SS * P)


def need(eng, sem, count):
    if isinstance(count, int) and count <= 0:
        return
    eng.wait_ge(sem, count)


def drive(eng, body, total, unroll):
    last = total // unroll - 1
    for j in range(unroll):
        body(0, j)
    with eng.Fori(1, last) as g:
        for j in range(unroll):
            body(g, j)
    for i in range(last * unroll, total):
        body(i // unroll, i % unroll)


def gnn_kernel(nc, x, src, dst, edge_attr, edge_weight, w_src, b_src, w_dst, fc_w1, fc_b1, fc_w2, fc_b2,
               fc_w3, fc_b3, w_sep, b_sep, alpha_dot, w_proj, b_proj, out):
    f32, i32, bf16 = mybir.dt.float32, mybir.dt.int32, mybir.dt.bfloat16
    ALU = mybir.AluOpType
    ACT = mybir.ActivationFunctionType
    ctx = ExitStack()

    def sb(name, shape, dt=f32):
        return ctx.enter_context(nc.sbuf_tensor(name, shape, dt))

    def sem(name):
        return ctx.enter_context(nc.semaphore(name))

    def dram(name, shape, dt=f32):
        return nc.dram_tensor(name, shape, dt, kind="Internal").ap()

    def column(v):
        return v.rearrange("(p a) -> p a", a=1)

    def spread(v, n):
        return bass.AP(tensor=v.tensor, offset=v.offset, ap=[[0, n], [1, v.shape[0]]])

    msg_src = dram("msg_src", (NB * P, C))
    msg_dst = dram("msg_dst", (NB, P, PARTS * C), bf16)
    records = dram("records", (EPAD, RW))
    attrs = dram("attrs", (EPAD, RAD))
    dst_rows = dram("dst_rows", (TPAD, TE))
    records_by_low = dram("records_by_low", (E, RW))
    attrs_by_low = dram("attrs_by_low", (E, RAD))
    tile_of = dram("tile_of", (NI,), i32)
    minus_base_of = dram("minus_base_of", (NI,))
    values = dram("values", (NI, P, SUB * VW))
    scores = dram("scores", (NI, P, P))
    masked_scores = dram("masked_scores", (P, IPC * TE))
    edge_col = dram("edge_col", (4, P))
    sums = dram("sums", (NI, P, AW))

    with ctx:
        SC = sb("SC", [P, IPC * TE])
        AR = sb("AR", [P, IPC * TE // 2 + 2])
        PS = [ctx.enter_context(nc.psum_tensor(f"PS{i}", [P, TE], f32)) for i in range(8)]
        ident = sb("ident", [P, P])
        iota_row = sb("iota_row", [P, P])
        first_node = sb("first_node", [P, 1])
        row_number = sb("row_number", [P, 1])
        minus_base = sb("minus_base", [P, NI])
        keep = sb("keep", [P, NI])
        steer = sb("steer", [1, 2 * NI], i32)
        last_item = sb("last_item", [1, P], i32)
        unsorted = sb("unsorted", [1, 1], i32)
        w1 = sb("w1", [P, 2, P])
        w2 = sb("w2", [P, P])
        w3 = sb("w3", [P, 2, P])
        wsep = sb("wsep", [P, H, 2, AH])
        wa = sb("wa", [P, C])
        wv = sb("wv", [P, C])
        wnode = sb("wnode", [P, 2 * C])
        wproj = sb("wproj", [P, C])
        adot = sb("adot", [P, 32])
        b1 = sb("b1", [P, 1])
        b2 = sb("b2", [P, 1])
        b3 = sb("b3", [P, 1])
        ba = sb("ba", [P, 1])
        bsrc = sb("bsrc", [P, C])
        bval = sb("bval", [P, H, 2, AH])
        bproj = sb("bproj", [P, C])
        score_bias = sb("score_bias", [P, 1])

        with ExitStack() as part, nc.Block() as block:
            def tb(name, shape, dt=f32):
                return part.enter_context(nc.sbuf_tensor(name, shape, dt))
            def ts(name):
                return part.enter_context(nc.semaphore(name))
            xs = AR[:, 0:NB * C].rearrange("p (b c) -> p b c", b=NB)
            U, S = 14, 7
            at = [0]

            def region(n):
                at[0] += n
                return SC[:, at[0] - n:at[0]]
            src_in, dst_in = region(EC).bitcast(i32), region(EC).bitcast(i32)
            dst_next, ea_in = region(EC + 1), region(EC)
            dst_f = dst_next[:, 0:EC]
            rec_out, rec_pad = region(EC * RW), region(PADC * RW)
            stats = tb("stats", [P, NB, 6])
            mean = tb("mean_x2", [P, NB])
            rstd = tb("rstd", [P, NB])
            shift = tb("shift", [P, NB])
            h = tb("h", [P, 2, C])
            bsrc2 = tb("bsrc2", [P, 2 * C])
            hT = tb("hT", [P, 2, C])
            node_out = tb("node_out", [P, S, 2 * C])
            dst_parts = AR[:, NB * C:NB * C + S * PARTS * C // 2].bitcast(bf16).rearrange("p (j n c) -> p j n c", j=S, n=PARTS)
            tail = N - (NB - 1) * P
            s_x, s_w, s_const = ts("x_in"), ts("node_weights_in"), ts("constants_made")
            s_bn, s_std, s_rstd = ts("moments"), ts("std_done"), ts("rstd_done")
            s_h, s_hT, s_hTs, s_mm, s_no = ts("h_done"), ts("hT_done"), ts("hT_copied"), ts("node_mm"), ts("node_rows")
            s_part = ts("parts_made")
            s_nst = [ts(f"node_stored{i}") for i in range(S)]
            s_ein, s_est = ts("edges_in"), ts("records_stored")
            rec3 = rec_out.rearrange("p (j f) -> p j f", f=RW)
            pad3 = rec_pad.rearrange("p (j f) -> p j f", f=RW)
            flat = dst_rows.rearrange("t e -> (t e)")

            @block.sync
            def _(sp):
                sp.dma_start(wnode[:, 0:C], w_src).then_inc(s_w, 16)
                sp.dma_start(wnode[:, C:2 * C], w_dst).then_inc(s_w, 16)
                sp.dma_start(bsrc[:, :], spread(b_src, P)).then_inc(s_w, 16)
                sp.dma_start(xs[:, 0:NB - 1, :], x[0:(NB - 1) * P, :].rearrange("(b p) c -> p b c", p=P)).then_inc(s_x, 16)
                sp.wait_ge(s_bn, 1)
                sp.dma_start(xs[0:tail, NB - 1, :], x[(NB - 1) * P:N, :]).then_inc(s_x, 16)

                for to, frm in ((src_in, src), (dst_in, dst), (ea_in, edge_weight)):
                    sp.dma_start(to, frm.rearrange("(p j) -> p j", p=P)).then_inc(s_ein, 16)
                sp.dma_start(attrs[E:EPAD, :], edge_attr[E:EPAD, :]).then_inc(s_ein, 16)
                sp.wait_ge(s_ein, 64)

            @block.gpsimd
            def _(pool):
                pool.memset(ident[:, :], 0.0).then_inc(s_const, 1)
                pool.wait_ge(s_const, 1)
                pool.affine_select(out=ident[:, :], in_=ident[:, :], compare_op=ALU.not_equal, fill=1.0,
                                   base=0, pattern=[[-1, P]], channel_multiplier=1).then_inc(s_const, 1)
                pool.iota(iota_row[:, :], [[1, P]], base=0, channel_multiplier=0,
                          allow_small_or_imprecise_dtypes=True)
                pool.iota(first_node[:, :], [[0, 1]], base=0, channel_multiplier=P,
                          allow_small_or_imprecise_dtypes=True)
                pool.iota(row_number[:, :], [[0, 1]], base=0, channel_multiplier=1,
                          allow_small_or_imprecise_dtypes=True)
                pool.memset(rec_pad, 0.0).then_inc(s_const, 1)
                pool.memset(rec3[:, :, RW - 1:RW], 0.0).then_inc(s_const, 1)
                pool.wait_ge(s_const, 4)
                pool.memset(pad3[:, :, RDST:RDST + 1], FAR).then_inc(s_const, 1)
                pool.wait_ge(s_const, 5)
                pool.dma_start(records[E:EPAD, :].rearrange("(p j) f -> p (j f)", p=P), rec_pad).then_inc(s_est, 16)
                pool.dma_start(flat[E:EPAD].rearrange("(p j) -> p j", p=P), pad3[:, :, RDST],
                               allow_slow_non_contiguous=True).then_inc(s_est, 16)

                pool.wait_ge(s_rstd, 8)
                pool.dma_start(records[0:E, :].rearrange("(p j) f -> p (j f)", p=P), rec_out).then_inc(s_est, 16)
                pool.dma_start(flat[0:E].rearrange("(p j) -> p j", p=P), dst_f).then_inc(s_est, 16)

                def parts(g, j):
                    b = U * g + j
                    rest = node_out[:, j % S, C:2 * C]
                    pool.wait_ge(s_no, 3 * b + 3)
                    for n in range(1, PARTS):
                        if n > 1:
                            pool.wait_ge(s_part, 3 * b + 1)
                            pool.tensor_tensor(rest, rest, dst_parts[:, j % S, n - 1], ALU.subtract).then_inc(s_part, 1)
                            pool.wait_ge(s_part, 3 * b + 2)
                        pool.tensor_tensor(dst_parts[:, j % S, n], rest, bsrc2[:, C:2 * C], ALU.add).then_inc(s_part, 1)
                drive(pool, parts, NB, U)
                pool.wait_ge(s_est, 64)

            @block.vector
            def _(dve):
                dve.memset(xs[:, NB - 1, :], 0.0).then_inc(s_bn, 1)
                dve.wait_ge(s_x, 32)

                def moments(g, j):
                    b = 2 * g + j
                    dve.bn_stats(stats[:, bass.ds(b, 1), :].rearrange("p o c -> p (o c)"),
                                 xs[:, bass.ds(b, 1), :].rearrange("p o c -> p (o c)")).then_inc(s_bn, 1)
                drive(dve, moments, NB, 2)
                dve.wait_ge(s_bn, NB + 1)
                even, odd, even_sq, odd_sq = (stats[:, :, n] for n in (1, 4, 2, 5))
                dve.tensor_tensor(mean[:, :], even, odd, ALU.add)
                dve.tensor_tensor(shift[:, :], even, odd, ALU.subtract)
                dve.tensor_tensor(rstd[:, :], even_sq, odd_sq, ALU.add).then_inc(s_bn, 1)
                dve.wait_ge(s_bn, NB + 2)
                dve.scalar_tensor_tensor(shift[:, :], shift[:, :], 0.25, shift[:, :], ALU.mult, ALU.mult)
                dve.tensor_scalar(rstd[:, :], rstd[:, :], 1.0 / C, 1e-5, ALU.mult, ALU.add).then_inc(s_bn, 1)
                dve.wait_ge(s_bn, NB + 3)
                dve.tensor_tensor(rstd[:, :], rstd[:, :], shift[:, :], ALU.add).then_inc(s_rstd, 1)
                dve.wait_ge(s_std, 1)
                dve.reciprocal(rstd[:, :], rstd[:, :]).then_inc(s_rstd, 1)
                dve.wait_ge(s_rstd, 2)
                dve.scalar_tensor_tensor(shift[:, :], mean[:, :], -0.5, rstd[:, :], ALU.mult, ALU.mult).then_inc(s_rstd, 1)
                dve.wait_ge(s_w, 48)

                def copy_hT(g, j):
                    b = U * g + j
                    dve.wait_ge(s_hT, b + 1)
                    need(dve, s_mm, b - 1)
                    dve.tensor_copy(hT[:, j % 2, :], PS[j % 2][:, 0:C]).then_inc(s_hTs, 1)

                def rows(g, j):
                    b = U * g + j
                    dve.wait_ge(s_mm, b + 1)
                    need(dve, s_nst[j % S], 32 * (U // S * g + j // S))
                    dve.tensor_tensor(node_out[:, j % S, :], PS[2 + j % 2][:, 0:2 * C], bsrc2[:, :], ALU.add).then_inc(s_no, 1)
                    if not isinstance(b, int) or b + 2 < NB:
                        copy_hT(g + (j + 2) // U, (j + 2) % U)
                    rest = node_out[:, j % S, C:2 * C]
                    dve.wait_ge(s_no, 3 * b + 1)
                    dve.tensor_copy(dst_parts[:, j % S, 0], rest).then_inc(s_no, 1)
                    dve.wait_ge(s_no, 3 * b + 2)
                    dve.tensor_tensor(rest, rest, dst_parts[:, j % S, 0], ALU.subtract).then_inc(s_no, 1)

                dve.memset(bsrc2[:, C:2 * C], 0.0)
                dve.tensor_copy(bsrc2[:, 0:C], bsrc[:, :]).then_inc(s_rstd, 1)
                dve.wait_ge(s_rstd, 4)
                dve.wait_ge(s_ein, 64)
                dve.tensor_copy(dst_f, dst_in).then_inc(s_rstd, 1)
                dve.tensor_copy(rec3[:, :, RSRC].bitcast(i32), src_in).then_inc(s_rstd, 1)
                dve.tensor_copy(rec3[:, :, RDST], dst_in).then_inc(s_rstd, 1)
                dve.tensor_copy(rec3[:, :, REA], ea_in).then_inc(s_rstd, 1)
                copy_hT(0, 0)
                copy_hT(0, 1)
                drive(dve, rows, NB, U)

            @block.scalar
            def _(act):
                act.wait_ge(s_rstd, 1)
                act.activation(rstd[:, :], rstd[:, :], ACT.Sqrt).then_inc(s_std, 1)
                act.wait_ge(s_rstd, 3)

                def store(g, j):
                    b = U * g + j
                    act.wait_ge(s_part, 3 * b + 3)
                    act.dma_start(msg_src[bass.ds(b * P, P), :], node_out[:, j % S, 0:C]).then_inc(s_nst[j % S], 16)
                    act.dma_start(msg_dst[bass.ds(b, 1), :, :].rearrange("o p c -> p (o c)"),
                                  dst_parts[:, j % S].rearrange("p n c -> p (n c)")).then_inc(s_nst[j % S], 16)

                def norm(g, j):
                    b = U * g + j
                    need(act, s_hT, b - 1)
                    act.activation(h[:, j % 2, :], xs[:, bass.ds(b, 1), :].rearrange("p o c -> p (o c)"), ACT.Relu,
                                   bias=shift[:, bass.ds(b, 1)], scale=rstd[:, bass.ds(b, 1)]).then_inc(s_h, 1)
                    if isinstance(b, int) and b < 4:
                        return
                    store(g + (j - 4) // U, (j - 4) % U)
                drive(act, norm, NB, U)
                for j in range(U - 4, U):
                    store(NB // U - 1, j)
                for j in range(S):
                    act.wait_ge(s_nst[j], 32 * (NB // S))

            @block.tensor
            def _(pe):
                pe.wait_ge(s_const, 2)
                pe.wait_ge(s_w, 48)

                def transpose(g, j):
                    b = U * g + j
                    pe.wait_ge(s_h, b + 1)
                    need(pe, s_hTs, b - 1)
                    pe.transpose(PS[j % 2][:, 0:C], h[:, j % 2, :], ident[:, :]).then_inc(s_hT, 1)

                def product(g, j):
                    b = U * g + j
                    pe.wait_ge(s_hTs, b + 1)
                    need(pe, s_no, 3 * b - 5)
                    pe.matmul(PS[2 + j % 2][:, 0:2 * C], lhsT=hT[:, j % 2, :], rhs=wnode[:, :], start=True, stop=True).then_inc(s_mm, 1)
                    if not isinstance(b, int) or b + 2 < NB:
                        transpose(g + (j + 2) // U, (j + 2) % U)
                transpose(0, 0)
                transpose(0, 1)
                drive(pe, product, NB, U)

        with ExitStack() as part, nc.Block() as block:
            def tb(name, shape, dt=f32):
                return part.enter_context(nc.sbuf_tensor(name, shape, dt))
            def ts(name):
                return part.enter_context(nc.semaphore(name))
            following = tb("following", [P, 1], i32)
            steps_down = tb("steps_down", [P, 1])
            ones = tb("ones_check", [P, 1])
            s_f, s_v, s_p = ts("following_in"), ts("check_steps"), ts("check_summed")

            @block.sync
            def _(sp):
                sp.wait_ge(s_v, 1)
                sp.dma_start(following[0:P - 1, :], bass.AP(tensor=dst.tensor, offset=dst.offset + EC, ap=[[EC, P - 1], [1, 1]]),
                             allow_slow_non_contiguous=True).then_inc(s_f, 16)

            @block.vector
            def _(dve):
                dve.memset(following[:, :], 2 ** 24)
                dve.memset(ones[:, :], 1.0).then_inc(s_v, 1)
                dve.wait_ge(s_f, 16)
                dve.tensor_copy(dst_next[:, EC:EC + 1], following[:, :]).then_inc(s_v, 1)
                dve.wait_ge(s_v, 2)
                dve.tensor_tensor(ea_in, dst_next[:, 0:EC], dst_next[:, 1:EC + 1], ALU.is_gt).then_inc(s_v, 1)
                dve.wait_ge(s_v, 3)
                dve.tensor_reduce(steps_down[:, :], ea_in, mybir.AxisListType.X, ALU.add).then_inc(s_v, 1)
                dve.wait_ge(s_p, 1)
                dve.tensor_scalar(unsorted[:, :], PS[0][0:1, 0:1], 0.5, None, ALU.is_gt)

            @block.tensor
            def _(pe):
                pe.wait_ge(s_v, 4)
                pe.matmul(PS[0][0:1, 0:1], lhsT=steps_down[:, :], rhs=ones[:, :], start=True, stop=True).then_inc(s_p, 1)

        with ExitStack() as part, nc.Block() as block:
            def tb(name, shape, dt=f32):
                return part.enter_context(nc.sbuf_tensor(name, shape, dt))
            def ts(name):
                return part.enter_context(nc.semaphore(name))
            keys = tb("keys", [P, SS, RW])
            moved = tb("moved", [P, SS, RAD])
            bounds = tb("bounds", [P, P + 1])
            reached = tb("reached", [P, P + 1])
            quotient = tb("quotient", [P, 1])
            digit = tb("digit", [P, P])
            total = tb("total", [P, P])
            place = tb("place", [P, P])
            ranked = tb("ranked", [P, P])
            where_f = tb("where_f", [P, 1])
            where = tb("where", [P, SS], i32)
            ones = tb("ones_sort", [P, P])
            before = tb("before", [P, P])
            s_c, s_c2, s_base = ts("sort_constants"), ts("sort_ones"), ts("places_begun")
            loops = []
            for n, (frm, to) in enumerate((((records, edge_attr), (records_by_low, attrs_by_low)),
                                           ((records_by_low, attrs_by_low), (records, attrs)))):
                for moving in (False, True):
                    tag = f"{n}{int(moving)}"
                    n_digit = 4 if n == 0 else 2
                    loops.append((n, moving, frm, to, n_digit, n_digit + (5 if moving else 1),
                                  ts("free" + tag), ts("loaded" + tag), ts("vector" + tag), ts("product" + tag),
                                  [[ts(f"scattered{tag}{m}") for m in range(2 + n)], ts("go" + tag)] if moving else [None, None]))

            def subtiles(v):
                return v[0:E].rearrange("(t s p) f -> t p s f", s=SS, p=P)

            @block.sync
            def _(sp):
                flag = sp.value_load(unsorted[0:1, 0:1], min_val=0, max_val=1)
                with sp.If(flag == 1):
                    for n, moving, frm, to, n_digit, n_ops, free, loaded, vec, prod, (scat, go) in loops:
                        with sp.Fori(0, NS) as t:
                            sp.wait_ge(free, t + 1)
                            sp.dma_start(keys[:, :, :], subtiles(frm[0])[bass.ds(t, 1)].rearrange("o p s f -> p (o s) f")).then_inc(loaded, 16)
                            if moving:
                                sp.dma_start(moved[:, :, :], subtiles(frm[1])[bass.ds(t, 1)].rearrange("o p s f -> p (o s) f")).then_inc(loaded, 16)

            @block.gpsimd
            def _(pool):
                flag = pool.value_load(unsorted[0:1, 0:1], min_val=0, max_val=1)
                with pool.If(flag == 1):
                    pool.iota(bounds[:, :], [[P, P + 1]], base=0, channel_multiplier=0, allow_small_or_imprecise_dtypes=True).then_inc(s_c, 1)
                    pool.wait_ge(s_c2, 1)
                    pool.affine_select(out=before[:, :], in_=ones[:, :], compare_op=ALU.is_gt, fill=0.0,
                                       base=0, pattern=[[1, P]], channel_multiplier=-1).then_inc(s_c, 1)
                    for n, moving, frm, to, n_digit, n_ops, free, loaded, vec, prod, (scat, go) in loops:
                        if not moving:
                            continue
                        with pool.Fori(0, NS) as t:
                            for s in range(SS):
                                pool.wait_ge(vec, (t * SS + s + 1) * n_ops)
                                pool.sem_inc(go, 1)
                                at = bass.IndirectOffsetOnAxis(ap=where[:, s:s + 1], axis=0)
                                pool.indirect_dma_start(to[0][0:E], at, keys[:, s], None).then_inc(scat[0], 16)
                                pool.indirect_dma_start(to[1][0:E], at, moved[:, s], None).then_inc(scat[1], 16)
                                if n == 1:
                                    pool.indirect_dma_start(flat[0:E].rearrange("(e a) -> e a", a=1), at,
                                                            keys[:, s, RDST:RDST + 1], None).then_inc(scat[2], 16)
                            for scattered in scat:
                                pool.wait_ge(scattered, 16 * SS * (t + 1))
                            pool.sem_inc(free, 1)
                        if n == 0:
                            pool.sem_inc(loops[2][6], 1)

            @block.vector
            def _(dve):
                flag = dve.value_load(unsorted[0:1, 0:1], min_val=0, max_val=1)
                with dve.If(flag == 1):
                    dve.memset(ones[:, :], 1.0).then_inc(s_c2, 1)
                    dve.wait_ge(s_c, 2)
                    dve.sem_inc(loops[0][6], 1)
                    for at, (n, moving, frm, to, n_digit, n_ops, free, loaded, vec, prod, (scat, go)) in enumerate(loops):
                        if not moving:
                            dve.memset(total[:, :], 0.0).then_inc(s_base, 1)
                            dve.wait_ge(s_base, 3 * n + 1)
                        else:
                            dve.tensor_tensor_scan(place[:, :], ones[:, :], total[:, :], 0.0, ALU.mult, ALU.add).then_inc(s_base, 1)
                            dve.wait_ge(s_base, 3 * n + 2)
                            dve.tensor_tensor(place[:, :], place[:, :], total[:, :], ALU.subtract).then_inc(s_base, 1)
                            dve.wait_ge(s_base, 3 * n + 3)
                            dve.sem_inc(free, 1)
                        with dve.Fori(0, NS) as t:
                            dve.wait_ge(loaded, (t + 1) * (32 if moving else 16))
                            for s in range(SS):
                                def done(ins, k):
                                    ins.then_inc(vec, 1)
                                    dve.wait_ge(vec, (t * SS + s) * n_ops + k)
                                key = keys[:, s, RDST:RDST + 1]
                                done(dve.tensor_scalar(reached[:, :], bounds[:, :], key, None, ALU.is_le), 1)
                                if n == 0:
                                    done(dve.tensor_reduce(quotient[:, :], reached[:, 1:P + 1], mybir.AxisListType.X, ALU.add), 2)
                                    done(dve.scalar_tensor_tensor(quotient[:, :], quotient[:, :], -float(P), key, ALU.mult, ALU.add), 3)
                                    done(dve.tensor_scalar(digit[:, :], iota_row[:, :], quotient[:, :], None, ALU.is_equal), 4)
                                else:
                                    done(dve.tensor_tensor(digit[:, :], reached[:, 0:P], reached[:, 1:P + 1], ALU.subtract), 2)
                                dve.wait_ge(prod, t * SS + s + 1)
                                if not moving:
                                    done(dve.tensor_tensor(total[:, :], total[:, :], PS[1][:, 0:P], ALU.add), n_digit + 1)
                                    continue
                                done(dve.tensor_tensor(ranked[:, :], place[:, :], PS[0][:, 0:P], ALU.add), n_digit + 1)
                                done(dve.tensor_tensor(ranked[:, :], ranked[:, :], digit[:, :], ALU.mult), n_digit + 2)
                                done(dve.tensor_reduce(where_f[:, :], ranked[:, :], mybir.AxisListType.X, ALU.add), n_digit + 3)
                                done(dve.tensor_tensor(place[:, :], place[:, :], PS[1][:, 0:P], ALU.add), n_digit + 4)
                                done(dve.tensor_copy(where[:, s:s + 1], where_f[:, :]), n_digit + 5)
                            if not moving:
                                dve.sem_inc(free, 1)

            @block.tensor
            def _(pe):
                flag = pe.value_load(unsorted[0:1, 0:1], min_val=0, max_val=1)
                with pe.If(flag == 1):
                    pe.wait_ge(s_c, 2)
                    for n, moving, frm, to, n_digit, n_ops, free, loaded, vec, prod, (scat, go) in loops:
                        with pe.Fori(0, NS) as t:
                            for s in range(SS):
                                pe.wait_ge(vec, (t * SS + s) * n_ops + n_digit)
                                if moving:
                                    pe.matmul(PS[0][:, 0:P], lhsT=before[:, :], rhs=digit[:, :], start=True, stop=True)
                                pe.matmul(PS[1][:, 0:P], lhsT=ones[:, :], rhs=digit[:, :], start=True, stop=True).then_inc(prod, 1)

        with ExitStack() as part, nc.Block() as block:
            def tb(name, shape, dt=f32):
                return part.enter_context(nc.sbuf_tensor(name, shape, dt))
            def ts(name):
                return part.enter_context(nc.semaphore(name))
            firsts = tb("firsts", [1, NT - 1])
            ones = tb("ones", [P, P])
            begun_by = tb("begun_by", [P, 1])
            below = SC[:, 0:NT - 1]
            iota_w = SC[:, 1024:1024 + NI]
            begun = SC[:, 2048:2048 + NI]
            blocks = SC[:, 3072:3072 + NI]
            tiles = SC[:, 4096:4096 + NI]
            starts = SC[:, 5120:5120 + P]
            s_wz, s_wl, s_f, s_io = ts("weights_cleared"), ts("weights_in"), ts("firsts_in"), ts("iota_made")
            s_v, s_p, s_st = ts("vector_steps"), ts("products"), ts("tables_stored")
            halves = [(0, 512), (512, NT - 1)]
            whalves = [(0, 512), (512, NI)]

            @block.sync
            def _(sp):
                sp.dma_start(firsts[:, :], dst_rows[1:NT, 0:1].rearrange("t a -> a t"),
                             allow_slow_non_contiguous=True).then_inc(s_f, 16)
                sp.wait_ge(s_wz, 1)
                loads = []
                for s in range(SUB):
                    loads.append((w1[RAD * s:RAD * (s + 1), s // 2, FC * (s % 2):FC * (s % 2 + 1)], fc_w1))
                for q in range(2):
                    rows = slice(FC * q, FC * (q + 1))
                    loads += [(w2[rows, FC * q:FC * (q + 1)], fc_w2), (w3[rows, q, :], fc_w3),
                              (b1[rows, :], column(fc_b1)), (b2[rows, :], column(fc_b2))]
                loads.append((b3[:, :], column(fc_b3)))
                for hd in range(H):
                    loads.append((adot[AH * hd:AH * (hd + 1), hd:hd + 1], alpha_dot[0, hd, :].rearrange("(k a) -> k a", a=1)))
                    loads.append((ba[AH * hd:AH * (hd + 1), :], column(b_sep[2 * AH * hd:2 * AH * hd + AH])))
                loads += [(wsep[:, :, :, :].rearrange("p h t k -> p (h t k)"), w_sep), (wproj[:, :], w_proj),
                          (bval[:, :, :, :].rearrange("p h t k -> p (h t k)"), spread(b_sep, P)),
                          (bproj[:, :], spread(b_proj, P))]
                for to, frm in loads:
                    sp.dma_start(to, frm).then_inc(s_wl, 16)
                sp.wait_ge(s_wl, 16 * len(loads))
                sp.wait_ge(s_v, 9)
                sp.dma_start(tile_of.rearrange("(a w) -> a w", a=1), steer[0:1, 0:NI]).then_inc(s_st, 16)
                sp.dma_start(minus_base_of.rearrange("(a w) -> a w", a=1), minus_base[0:1, :]).then_inc(s_st, 16)
                sp.wait_ge(s_st, 32)
            n_loads = SUB + 8 + 1 + 2 * H + 4

            @block.gpsimd
            def _(pool):
                pool.iota(iota_w, [[1, NI]], base=0, channel_multiplier=0,
                          allow_small_or_imprecise_dtypes=True).then_inc(s_io, 1)

            @block.vector
            def _(dve):
                for t in (w1, w2, w3, adot):
                    last = dve.memset(t[(slice(None),) * len(t.shape)], 0.0)
                last.then_inc(s_wz, 1)
                dve.memset(ones[:, :], 1.0).then_inc(s_v, 1)
                dve.wait_ge(s_f, 16)
                dve.engine_nop().then_inc(s_v, 1)
                dve.wait_ge(s_p, 1)
                for n, (a, z) in enumerate(halves):
                    dve.tensor_scalar(below[:, a:z], PS[n][:, 0:z - a], first_node[:, :], None, ALU.is_lt).then_inc(s_v, 1)
                dve.wait_ge(s_v, 4)
                dve.tensor_reduce(begun_by[:, :], below, mybir.AxisListType.X, ALU.add).then_inc(s_v, 1)
                dve.wait_ge(s_v, 5)
                dve.scalar_tensor_tensor(begun_by[:, :], first_node[:, :], 1.0 / P, begun_by[:, :], ALU.mult, ALU.add).then_inc(s_v, 1)
                dve.wait_ge(s_v, 6)
                dve.wait_ge(s_io, 1)
                dve.tensor_scalar(begun, iota_w, begun_by[:, :], None, ALU.is_ge).then_inc(s_v, 1)
                dve.wait_ge(s_p, 2)
                for n, (a, z) in enumerate(whalves):
                    dve.tensor_scalar(minus_base[:, a:z], PS[2 + n][:, 0:z - a], -1.0, -float(P), ALU.add, ALU.mult)
                    dve.tensor_scalar(blocks[:, a:z], PS[2 + n][:, 0:z - a], -1.0, None, ALU.add)
                last = dve.tensor_scalar(starts, PS[4][:, 0:P], -1.0, None, ALU.add)
                last.then_inc(s_v, 1)
                dve.wait_ge(s_v, 8)
                dve.tensor_tensor(tiles, iota_w, blocks, ALU.subtract).then_inc(s_io, 1)
                dve.tensor_tensor(keep[:, 1:NI], blocks[:, 1:NI], blocks[:, 0:NI - 1], ALU.is_equal)
                dve.memset(keep[:, 0:1], 0.0)
                dve.tensor_copy(steer[0:1, NI:2 * NI], blocks[0:1, :])
                dve.tensor_copy(last_item[0:1, 0:NB - 1], starts[0:1, 1:NB])
                dve.memset(last_item[0:1, NB - 1:NB], NT - 1 + NB - 1)
                dve.wait_ge(s_io, 2)
                dve.tensor_copy(steer[0:1, 0:NI], tiles[0:1, :]).then_inc(s_v, 1)
                dve.wait_ge(s_wl, 16 * n_loads)
                dve.tensor_copy(wa[:, :].rearrange("p (h k) -> p h k", h=H), wsep[:, :, 0, :])
                dve.tensor_copy(wv[:, :].rearrange("p (h k) -> p h k", h=H), wsep[:, :, 1, :])
                dve.tensor_scalar(adot[:, :], adot[:, :], 0.8, None, ALU.mult).then_inc(s_v, 1)
                dve.wait_ge(s_p, 3)
                dve.tensor_scalar(score_bias[:, :], PS[5][:, 0:1], 0.25, None, ALU.mult)

            @block.tensor
            def _(pe):
                pe.wait_ge(s_v, 2)
                for n, (a, z) in enumerate(halves):
                    last = pe.matmul(PS[n][:, 0:z - a], lhsT=ones[0:1, :], rhs=firsts[:, a:z], start=True, stop=True)
                last.then_inc(s_p, 1)
                pe.wait_ge(s_v, 7)
                for n, (a, z) in enumerate(whalves):
                    pe.matmul(PS[2 + n][:, 0:z - a], lhsT=ones[0:NB, :], rhs=begun[0:NB, a:z], start=True, stop=True)
                pe.matmul(PS[4][:, 0:P], lhsT=begun_by[:, :].broadcast_to((P, P)), rhs=ident[:, :],
                          start=True, stop=True).then_inc(s_p, 1)
                pe.wait_ge(s_v, 10)
                for s in range(SUB):
                    last = pe.matmul(PS[5][32 * s:32 * s + 32, 0:1], lhsT=adot[:, :], rhs=ba[:, :], start=True, stop=True,
                                     tile_position=(0, 32 * s))
                last.then_inc(s_p, 1)

        with ExitStack() as part, nc.Block() as block:
            def tb(name, shape, dt=f32):
                return part.enter_context(nc.sbuf_tensor(name, shape, dt))
            def ts(name):
                return part.enter_context(nc.semaphore(name))
            U = 4
            rec = tb("rec", [P, U, SUB, RW])
            attr = tb("attr", [P, U, SUB * RAD])
            win = tb("win", [P, U, PARTS, C], bf16)
            cut = [0]

            def carve(n, pattern, **dims):
                cut[0] += n
                return AR[:, cut[0] - n:cut[0]].rearrange(pattern, **dims)
            gath = carve(U * SUB * C, "p (j s c) -> p j s c", j=U, s=SUB)
            vout = carve(U * SUB * VW, "p (j s c) -> p j s c", j=U, s=SUB)
            hotT = tb("hotT", [P, 2, TE], bf16)
            recT = tb("recT", [P, 2, P])
            h1 = tb("h1", [P, 2, 2 * P])
            h2 = tb("h2", [P, 2, 2 * P])
            sout = carve(U * P, "p (j n) -> p j n", j=U)
            xe = carve(2 * TE, "p (j s c) -> p j s c", j=2, s=SUB)
            rads, msgT, sil = (carve(2 * TE, "p (j n) -> p j n", j=2) for _ in range(3))
            spread_dst = carve(U * TE, "p (j n) -> p j n", j=U)
            s_rec = [ts(f"rec_in{j}") for j in range(U)]
            s_win = [ts(f"window_in{j}") for j in range(U)]
            s_gath = [ts(f"gathered{j}") for j in range(U)]
            s_vst = [ts(f"values_stored{j}") for j in range(U)]
            s_recT, s_recTs, s_hotT = ts("recT_done"), ts("recT_copied"), ts("hotT_done")
            s_rel = ts("places_done")
            s_z1, s_h1, s_z2, s_h2, s_rad, s_rads = ts("z1_done"), ts("h1_done"), ts("z2_done"), ts("h2_done"), ts("rad_done"), ts("rad_copied")
            s_D, s_x, s_xT, s_msg = ts("dst_rows_done"), ts("summed"), ts("xT_done"), ts("message_done")
            s_a, s_v, s_sil, s_al, s_sc = ts("alpha_in_done"), ts("values_done"), ts("silu_done"), ts("alpha_done"), ts("scores_done")
            s_sum = ts("parts_added")
            s_vout, s_scout, s_go = ts("values_copied"), ts("scores_copied"), ts("gathers_begun")
            recT_ps = PS[3][:, 0:P]
            z1_ps = z2_ps = PS[1][:, 0:2 * P]
            sc_ps = PS[0][:, 0:P]
            rad_ps, d_ps, xT_ps, a_ps, v_ps = (PS[n][:, :] for n in (2, 4, 5, 6, 7))
            rec_v = records.rearrange("(t p s) f -> t p (s f)", p=P, s=SUB)
            given_v, sorted_v = (v.rearrange("(t p s) f -> t p (s f)", p=P, s=SUB) for v in (edge_attr, attrs))

            def there(i):
                return not isinstance(i, int) or 0 <= i < NI

            def later(g, j, d):
                return g + (j + d) // U, (j + d) % U

            @block.sync
            def _(sp):
                def store(g, j):
                    i = U * g + j
                    sp.wait_ge(s_rel, i + 1)
                    sp.wait_ge(s_vout, i + 1)
                    sp.dma_start(values[bass.ds(i, 1)].rearrange("o p c -> p (o c)"),
                                 vout[:, j].rearrange("p s c -> p (s c)")).then_inc(s_vst[j], 16)
                    sp.wait_ge(s_scout, i + 1)
                    sp.dma_start(scores[bass.ds(i, 1)].rearrange("o q n -> q (o n)"), sout[:, j]).then_inc(s_vst[j], 16)

                def load(g, j, attr_v):
                    i = U * g + j
                    t = sp.value_load(steer[0:1, bass.ds(i, 1)], min_val=0, max_val=TPAD - 1)
                    b = sp.value_load(steer[0:1, bass.ds(NI + i, 1)], min_val=0, max_val=NB - 1)
                    need(sp, s_x, i - U + 1)
                    need(sp, s_rel, i - U + 1)
                    sp.dma_start(rec[:, j].rearrange("p s f -> p (s f)"),
                                 rec_v[bass.ds(t, 1)].rearrange("o p f -> p (o f)")).then_inc(s_rec[j], 16)
                    sp.dma_start(attr[:, j], attr_v[bass.ds(t, 1)].rearrange("o p f -> p (o f)")).then_inc(s_rec[j], 16)
                    sp.dma_start(win[:, j].rearrange("p n c -> p (n c)"), msg_dst[bass.ds(b, 1)].rearrange("o p c -> p (o c)")).then_inc(s_win[j], 16)
                    sp.dma_start(spread_dst[:, j], dst_rows[bass.ds(t, 1), :].broadcast_to((P, TE))).then_inc(s_win[j], 16)
                    if not (isinstance(g, int) and g == 0):
                        store(g - 1, j)
                flag = sp.value_load(unsorted[0:1, 0:1], min_val=0, max_val=1)
                with sp.If(flag == 0):
                    drive(sp, lambda g, j: load(g, j, given_v), NI, U)
                with sp.Else():
                    drive(sp, lambda g, j: load(g, j, sorted_v), NI, U)
                for j in range(U):
                    store(NI // U - 1, j)
                for j in range(U):
                    sp.wait_ge(s_vst[j], 32 * (NI // U))

            @block.gpsimd
            def _(pool):
                def gather(g, j):
                    i = U * g + j
                    need(pool, s_x, i - U + 1)
                    pool.wait_ge(s_rec[j], 32 * g + 32)
                    pool.sem_inc(s_go, 1)
                    for s in range(SUB):
                        pool.indirect_dma_start(
                            gath[:, j, s], None, msg_src,
                            bass.IndirectOffsetOnAxis(ap=rec[:, j, s, RSRC:RSRC + 1].bitcast(i32), axis=0)
                        ).then_inc(s_gath[j], 16)
                drive(pool, gather, NI, U)

            @block.vector
            def _(dve):
                def prepare(g, j):
                    i = U * g + j
                    dve.wait_ge(s_win[j], 32 * g + 32)
                    need(dve, s_D, i - 1)
                    dve.tensor_scalar(hotT[:, j % 2], spread_dst[:, j], minus_base[:, bass.ds(i, 1)], row_number[:, :],
                                      ALU.add, ALU.is_equal).then_inc(s_hotT, 1)

                def copy_recT(g, j):
                    i = U * g + j
                    dve.wait_ge(s_recT, i + 1)
                    need(dve, s_z1, i - 1)
                    dve.tensor_copy(recT[:, j % 2], recT_ps).then_inc(s_recTs, 1)

                def add_parts(g, j):
                    i = U * g + j
                    dve.wait_ge(s_D, i + 1)
                    dve.wait_ge(s_gath[j], 16 * SUB * (g + 1))
                    dve.tensor_tensor(gath[:, j], gath[:, j], d_ps.rearrange("p (s c) -> p s c", s=SUB), ALU.add).then_inc(s_sum, 1)
                    need(dve, s_xT, i - 1)
                    dve.wait_ge(s_sum, i + 1)
                    dve.tensor_tensor(xe[:, j % 2], gath[:, j], rec[:, j, :, REA].unsqueeze(2).broadcast_to((P, SUB, C)),
                                      ALU.mult).then_inc(s_x, 1)

                def copy_scores(g, j):
                    i = U * g + j
                    dve.wait_ge(s_sc, i + 1)
                    need(dve, s_vst[j], 32 * g)
                    dve.tensor_scalar(sout[:, j], sc_ps, score_bias[:, :], None, ALU.add).then_inc(s_scout, 1)

                def step(g, j):
                    i = U * g + j
                    q = j % 2
                    dve.wait_ge(s_xT, i + 1)
                    dve.wait_ge(s_rads, i + 1)
                    need(dve, s_v, i - 1)
                    dve.tensor_tensor(msgT[:, q], xT_ps, rads[:, q], ALU.mult).then_inc(s_msg, 1)
                    if there(i - 1):
                        copy_scores(*later(g, j, -1))
                    if there(i + 1):
                        add_parts(*later(g, j, 1))
                    dve.wait_ge(s_a, i + 1)
                    dve.wait_ge(s_sil, i + 1)
                    dve.scalar_tensor_tensor(sil[:, q], a_ps, 0.25, sil[:, q], ALU.mult, ALU.add).then_inc(s_al, 1)
                    if there(i + 2):
                        copy_recT(*later(g, j, 2))
                        prepare(*later(g, j, 2))
                prepare(0, 0)
                prepare(0, 1)
                copy_recT(0, 0)
                copy_recT(0, 1)
                add_parts(0, 0)
                drive(dve, step, NI, U)
                copy_scores(NI // U - 1, U - 1)

            @block.scalar
            def _(act):
                def places(g, j):
                    i = U * g + j
                    need(act, s_vst[j], 32 * g)
                    act.wait_ge(s_rec[j], 32 * g + 32)
                    act.activation(vout[:, j, :, C], rec[:, j, :, RDST], ACT.Identity,
                                   bias=minus_base[:, bass.ds(i, 1)]).then_inc(s_rel, 1)

                def copy_values(g, j):
                    i = U * g + j
                    act.wait_ge(s_v, i + 1)
                    act.activation(vout[:, j, :, 0:C], v_ps.rearrange("p (s c) -> p s c", s=SUB), ACT.Copy).then_inc(s_vout, 1)

                def first(g, j):
                    i = U * g + j
                    act.wait_ge(s_z1, i + 1)
                    need(act, s_z2, i - 1)
                    act.activation(h1[:, j % 2], z1_ps, ACT.Silu, bias=b1[:, :]).then_inc(s_h1, 1)

                def second(g, j):
                    i = U * g + j
                    act.wait_ge(s_z2, i + 1)
                    need(act, s_rad, i - 1)
                    act.activation(h2[:, j % 2], z2_ps, ACT.Silu, bias=b2[:, :]).then_inc(s_h2, 1)

                def radial(g, j):
                    i = U * g + j
                    act.wait_ge(s_rad, i + 1)
                    need(act, s_msg, i - 1)
                    act.activation(rads[:, j % 2].rearrange("f (p q e) -> f p q e", p=2, q=2),
                                   rad_ps.rearrange("f (q p e) -> f p q e", p=2, q=2),
                                   ACT.Identity, bias=b3[:, :]).then_inc(s_rads, 1)

                def step(g, j):
                    i = U * g + j
                    following = later(g, j, 1)
                    if there(i + 1):
                        first(*following)
                        places(*following)
                    if there(i - 1):
                        copy_values(*later(g, j, -1))
                    act.wait_ge(s_a, i + 1)
                    need(act, s_sc, i - 1)
                    act.activation(sil[:, j % 2], a_ps, ACT.Silu, bias=ba[:, :]).then_inc(s_sil, 1)
                    if there(i + 1):
                        second(*following)
                        radial(*following)
                first(0, 0)
                places(0, 0)
                second(0, 0)
                radial(0, 0)
                drive(act, step, NI, U)
                copy_values(NI // U - 1, U - 1)

            @block.tensor
            def _(pe):
                def attributes(g, j):
                    i = U * g + j
                    pe.wait_ge(s_rec[j], 32 * g + 32)
                    need(pe, s_recTs, i)
                    pe.transpose(recT_ps, attr[:, j], ident[:, :]).then_inc(s_recT, 1)

                def z1(g, j):
                    i = U * g + j
                    pe.wait_ge(s_recTs, i + 1)
                    need(pe, s_h2, i)
                    for p in range(2):
                        last = pe.matmul(z1_ps[:, p * P:(p + 1) * P], lhsT=w1[:, p], rhs=recT[:, j % 2], start=True, stop=True)
                    last.then_inc(s_z1, 1)

                def z2(g, j):
                    i = U * g + j
                    pe.wait_ge(s_h1, i + 1)
                    pe.matmul(z2_ps, lhsT=w2[:, :], rhs=h1[:, j % 2], start=True, stop=True).then_inc(s_z2, 1)

                def dst_part(g, j):
                    i = U * g + j
                    pe.wait_ge(s_win[j], 32 * g + 32)
                    pe.wait_ge(s_hotT, i + 1)
                    need(pe, s_sum, i)
                    for s in range(SUB):
                        for n in range(PARTS):
                            last = pe.matmul(d_ps[:, s * C:(s + 1) * C], lhsT=hotT[:, j % 2, s:TE:SUB],
                                             rhs=win[:, j, n], start=(n == 0), stop=(n == PARTS - 1))
                    last.then_inc(s_D, 1)

                def radial(g, j):
                    i = U * g + j
                    pe.wait_ge(s_h2, i + 1)
                    need(pe, s_rads, i)
                    for q in range(2):
                        last = pe.matmul(rad_ps[:, q * 2 * P:(q + 1) * 2 * P], lhsT=w3[:, q], rhs=h2[:, j % 2], start=True, stop=True)
                    last.then_inc(s_rad, 1)

                def scores(g, j):
                    i = U * g + j
                    pe.wait_ge(s_al, i + 1)
                    need(pe, s_scout, i)
                    for s in range(SUB):
                        last = pe.matmul(sc_ps[32 * s:32 * s + 32, :], lhsT=adot[:, :], rhs=sil[:, j % 2, s * P:(s + 1) * P],
                                         start=True, stop=True, tile_position=(0, 32 * s))
                    last.then_inc(s_sc, 1)

                def step(g, j):
                    i = U * g + j
                    q = j % 2
                    following = later(g, j, 1)
                    if there(i - 1):
                        scores(*later(g, j, -1))
                    pe.wait_ge(s_x, i + 1)
                    need(pe, s_msg, i)
                    for s in range(SUB):
                        last = pe.transpose(xT_ps[:, s * P:(s + 1) * P], xe[:, q, s], ident[:, :])
                    last.then_inc(s_xT, 1)
                    if there(i + 1):
                        z1(*following)
                        dst_part(*following)
                    pe.wait_ge(s_msg, i + 1)
                    need(pe, s_al, i)
                    pe.matmul(a_ps, lhsT=wa[:, :], rhs=msgT[:, q], start=True, stop=True).then_inc(s_a, 1)
                    if there(i + 1):
                        z2(*following)
                    need(pe, s_vout, i)
                    for s in range(SUB):
                        last = pe.matmul(v_ps[:, s * C:(s + 1) * C], lhsT=msgT[:, q, s * P:(s + 1) * P], rhs=wv[:, :], start=True, stop=True)
                    last.then_inc(s_v, 1)
                    if there(i + 2):
                        attributes(*later(g, j, 2))
                    if there(i + 1):
                        radial(*following)
                attributes(0, 0)
                attributes(0, 1)
                z1(0, 0)
                z2(0, 0)
                dst_part(0, 0)
                radial(0, 0)
                drive(pe, step, NI, U)
                scores(NI // U - 1, U - 1)

        with ExitStack() as part, nc.Block() as block:
            def tb(name, shape, dt=f32):
                return part.enter_context(nc.sbuf_tensor(name, shape, dt))
            def ts(name):
                return part.enter_context(nc.semaphore(name))
            L = IPC * TE
            change = AR[:, :].bitcast(bf16)[:, 0:L + 1]
            tiles_c = tb("tiles_c", [P, IPC], i32)
            lowest = tb("lowest", [P, IPC])
            highest = tb("highest", [P, IPC])
            index = tb("index", [P, 2], i32)
            drow = tb("drow", [P, 2, TE + 1])
            off = tb("off", [P, 4, TE])
            raw = off
            stage = tb("stage", [P, 2, TE])
            dfirst = tb("dfirst", [P, 1])
            edge = tb("edge", [P, 4])
            flags = tb("flags", [P, 4])
            changes = tb("changes", [P, IPC])
            small = tb("small", [H, 6, CH])
            back = tb("back", [P, 1])
            s_t, s_idx, s_pre = ts("chunk_tables_in"), ts("index_ready"), ts("table_steps")
            s_g = [ts(f"dst_gathered{j}") for j in range(2)]
            s_col, s_row, s_masked = ts("before_copied"), ts("changes_made"), ts("scores_masked")
            s_off = ts("offsets_steps")
            s_scin = ts("scores_in")
            s_staged, s_go = ts("scores_staged"), ts("gathers_begun")
            s_c, s_cd, s_dump = ts("chain"), ts("chain_dma"), ts("scores_dumped")
            s_raw = [ts(f"raw_in{j}") for j in range(4)]
            s_sub, s_exp, s_wt, s_wc = ts("subtracted"), ts("exp_done"), ts("weights_transposed"), ts("weights_copied")
            sc_k = SC[:, :].rearrange("p (k n) -> p k n", n=TE)

            @block.sync
            def _(sp):
                for c in range(CH):
                    rows = slice(c * H, (c + 1) * H)
                    sp.dma_start(tiles_c[rows, :], spread(tile_of[c * IPC:(c + 1) * IPC], H)).then_inc(s_t, 16)
                    sp.dma_start(lowest[rows, :], spread(minus_base_of[c * IPC:(c + 1) * IPC], H)).then_inc(s_t, 16)
                by_chunk = scores.rearrange("(c k) (s m) n -> c m (k s) n", c=CH, s=SUB)
                for c in range(CH):
                    sp.dma_start(SC[c * H:(c + 1) * H, :].rearrange("q (k n) -> q k n", n=P), by_chunk[c, 0:H]).then_inc(s_scin, 16)
                def keep_masked(g, j):
                    k = 2 * g + j
                    sp.wait_ge(s_masked, k + 1)
                    sp.dma_start(masked_scores[:, bass.ds(k * TE, TE)], SC[:, bass.ds(k * TE, TE)]).then_inc(s_dump, 16)
                drive(sp, keep_masked, IPC, 2)
                sp.wait_ge(s_c, 1)
                sp.dma_start(column(edge_col[0]), drow[:, (IPC - 1) % 2, TE:TE + 1]).then_inc(s_cd, 16)
                sp.wait_ge(s_cd, 16)
                sp.dma_start(edge[H:P, 0:1], column(edge_col[0, 0:P - H])).then_inc(s_cd, 16)
                sp.wait_ge(s_c, 2)
                sp.dma_start(column(edge_col[1]), flags[:, 0:1]).then_inc(s_cd, 16)
                sp.wait_ge(s_cd, 48)
                sp.dma_start(edge[0:P - H, 1:2], column(edge_col[1, H:P])).then_inc(s_cd, 16)
                by_head = [edge_col[n].rearrange("(c h) -> h c", h=H) for n in range(4)]
                n = 64
                for way in range(2):
                    sp.wait_ge(s_c, 4 + 3 * way)
                    sp.dma_start(column(edge_col[2]), edge[:, 2:3]).then_inc(s_cd, 16)
                    sp.dma_start(column(edge_col[3]), flags[:, 1 + way:2 + way]).then_inc(s_cd, 16)
                    sp.wait_ge(s_cd, n + 32)
                    sp.dma_start(small[:, 0], by_head[2], allow_slow_non_contiguous=True).then_inc(s_cd, 16)
                    sp.dma_start(small[:, 1], by_head[3], allow_slow_non_contiguous=True).then_inc(s_cd, 16)
                    sp.wait_ge(s_cd, n + 64)
                    sp.wait_ge(s_c, 5 + 3 * way)
                    sp.dma_start(by_head[0], small[:, 2], allow_slow_non_contiguous=True).then_inc(s_cd, 16)
                    sp.wait_ge(s_cd, n + 80)
                    sp.dma_start(edge[:, 3:4], column(edge_col[0])).then_inc(s_cd, 16)
                    n += 96

                def load(g, j):
                    k = 4 * g + j
                    need(sp, s_sub, k - 3)
                    sp.dma_start(raw[:, j], masked_scores[:, bass.ds(k * TE, TE)]).then_inc(s_raw[j], 16)
                sp.wait_ge(s_dump, 16 * IPC)
                drive(sp, load, IPC, 4)

            @block.gpsimd
            def _(pool):
                def gather(g, j):
                    k = 2 * g + j
                    pool.wait_ge(s_idx, k + 1)
                    pool.sem_inc(s_go, 1)
                    pool.indirect_dma_start(drow[:, j, 1:TE + 1], None, dst_rows,
                                            bass.IndirectOffsetOnAxis(ap=index[:, j:j + 1], axis=0)).then_inc(s_g[j], 16)
                drive(pool, gather, IPC, 2)

            @block.vector
            def _(dve):
                dve.memset(drow[:, 0, 0:1], 2 * FAR)
                dve.memset(edge[:, :], 2 * FAR)
                dve.memset(flags[:, :], 0.0)
                dve.memset(small[:, :, :], -BIG).then_inc(s_pre, 1)
                dve.wait_ge(s_t, 32 * CH)
                dve.tensor_scalar(highest[:, :], lowest[:, :], -1.0, P - 1.0, ALU.mult, ALU.add).then_inc(s_pre, 1)
                dve.wait_ge(s_pre, 2)
                dve.tensor_scalar(lowest[:, :], lowest[:, :], -1.0, None, ALU.mult).then_inc(s_pre, 1)
                dve.wait_ge(s_pre, 3)

                def pick(g, j):
                    k = 2 * g + j
                    need(dve, s_off, 2 * (k - 1))
                    need(dve, s_row, k - 1)
                    need(dve, s_col, k - 1)
                    dve.tensor_copy(index[:, j:j + 1], tiles_c[:, bass.ds(k, 1)]).then_inc(s_idx, 1)

                def step(g, j):
                    k = 2 * g + j
                    dve.wait_ge(s_g[j], 16 * g + 16)
                    if not (isinstance(k, int) and k + 1 >= IPC):
                        need(dve, s_row, k)
                        dve.tensor_copy(drow[:, 1 - j, 0:1], drow[:, j, TE:TE + 1]).then_inc(s_col, 1)
                    if not (isinstance(k, int) and k == 0):
                        dve.wait_ge(s_col, k)
                    dve.tensor_tensor(change[:, bass.ds(k * TE, TE)], drow[:, j, 1:TE + 1], drow[:, j, 0:TE],
                                      ALU.not_equal).then_inc(s_row, 1)
                    need(dve, s_masked, k - 1)
                    dve.tensor_scalar(off[:, j], drow[:, j, 1:TE + 1], lowest[:, bass.ds(k, 1)], highest[:, bass.ds(k, 1)],
                                      ALU.max, ALU.min).then_inc(s_off, 1)
                    dve.wait_ge(s_off, 2 * k + 1)
                    dve.tensor_tensor(off[:, j], off[:, j], drow[:, j, 1:TE + 1], ALU.not_equal).then_inc(s_off, 1)
                    if isinstance(k, int) and k == 0:
                        dve.tensor_copy(dfirst[:, :], drow[:, 0, 1:2])
                    if not (isinstance(k, int) and k + 2 >= IPC):
                        pick(g + 1, j)
                    dve.wait_ge(s_off, 2 * k + 2)
                    dve.wait_ge(s_staged, k + 1)
                    dve.scalar_tensor_tensor(sc_k[:, bass.ds(k, 1)].rearrange("q o (p s) -> q s (o p)", s=SUB),
                                             off[:, j].rearrange("q (p s) -> q s p", s=SUB), -BIG,
                                             stage[:, j].rearrange("q (s p) -> q s p", s=SUB),
                                             ALU.mult, ALU.add).then_inc(s_masked, 1)
                    dve.wait_ge(s_row, k + 1)
                    dve.tensor_reduce(changes[:, bass.ds(k, 1)], change[:, bass.ds(k * TE, TE)], mybir.AxisListType.X,
                                      ALU.add).then_inc(s_pre, 1)
                pick(0, 0)
                pick(0, 1)
                drive(dve, step, IPC, 2)
                dve.wait_ge(s_row, IPC)
                dve.wait_ge(s_pre, IPC + 3)
                dve.tensor_reduce(flags[:, 1:2], changes[:, :], mybir.AxisListType.X, ALU.add).then_inc(s_pre, 1)
                dve.engine_nop().then_inc(s_c, 1)
                dve.wait_ge(s_cd, 32)
                dve.tensor_tensor(flags[:, 0:1], dfirst[:, :], edge[:, 0:1], ALU.not_equal).then_inc(s_c, 1)
                dve.wait_ge(s_c, 2)
                dve.tensor_copy(change[:, 0:1], flags[:, 0:1])
                dve.memset(back[:, :], 1.0)
                dve.wait_ge(s_cd, 64)
                dve.tensor_scalar(flags[:, 3:4], edge[:, 1:2], 0.0, None, ALU.not_equal)
                dve.tensor_scalar(change[:, L:L + 1], edge[:, 1:2], 0.0, None, ALU.not_equal).then_inc(s_c, 1)
                dve.wait_ge(s_c, 3)
                dve.wait_ge(s_pre, IPC + 4)
                dve.scalar_tensor_tensor(flags[:, 2:3], flags[:, 1:2], -1.0, flags[:, 3:4], ALU.add, ALU.add)
                dve.scalar_tensor_tensor(flags[:, 1:2], flags[:, 1:2], -1.0, flags[:, 0:1], ALU.add, ALU.add).then_inc(s_pre, 1)
                dve.wait_ge(s_pre, IPC + 5)
                dve.tensor_scalar(flags[:, 1:3], flags[:, 1:3], 0.5, -BIG, ALU.is_gt, ALU.mult).then_inc(s_pre, 1)
                dve.wait_ge(s_pre, IPC + 6)
                dve.tensor_scalar(change[:, :], change[:, :], -BIG, None, ALU.mult).then_inc(s_row, 1)
                dve.wait_ge(s_dump, 16 * IPC)
                dve.wait_ge(s_row, IPC + 1)
                for way in range(2):
                    run = slice(None) if way == 0 else slice(None, None, -1)
                    pen = change[:, way:L + way][:, run]
                    val = SC[:, :][:, run]
                    end = L - 1 if way == 0 else 0
                    b = 4 + 3 * way
                    dve.tensor_tensor_scan(val, pen, val, -BIG, ALU.add, ALU.max).then_inc(s_pre, 1)
                    dve.wait_ge(s_pre, IPC + 7 + 2 * way)
                    dve.tensor_copy(edge[:, 2:3], SC[:, end:end + 1]).then_inc(s_c, 1)
                    dve.wait_ge(s_cd, 128 + 96 * way)
                    inner = slice(0, CH - 1) if way == 0 else slice(CH - 1, 0, -1)
                    carry = slice(1, CH) if way == 0 else slice(CH - 2, None, -1)
                    if way == 1:
                        dve.memset(small[:, 2], -BIG).then_inc(s_pre, 1)
                        dve.wait_ge(s_pre, IPC + 10)
                    dve.tensor_tensor_scan(small[:, 2, carry], small[:, 1, inner], small[:, 0, inner], -BIG,
                                           ALU.add, ALU.max).then_inc(s_c, 1)
                    dve.wait_ge(s_cd, 160 + 96 * way)
                    dve.tensor_tensor_scan(val, pen, val, edge[:, 3:4], ALU.add, ALU.max).then_inc(s_c, 1)
                    if way == 0:
                        dve.engine_nop().then_inc(s_pre, 1)
                        dve.wait_ge(s_c, b + 2)
                dve.wait_ge(s_c, 9)

                def subtract(g, j):
                    k = 4 * g + j
                    dve.wait_ge(s_raw[j], 16 * g + 16)
                    dve.tensor_tensor(sc_k[:, bass.ds(k, 1)].rearrange("q o n -> q (o n)"), raw[:, j],
                                      sc_k[:, bass.ds(k, 1)].rearrange("q o n -> q (o n)"), ALU.subtract).then_inc(s_sub, 1)
                    if not (isinstance(k, int) and k < 2):
                        copy(k - 2, j % 2)

                def copy(k, bank):
                    dve.wait_ge(s_wt, k + 1)
                    dve.tensor_scalar(sc_k[:, bass.ds(k, 1)].rearrange("q o n -> q (o n)"), PS[2 + bank][:, :], 1.0, None,
                                      ALU.mult).then_inc(s_wc, 1)
                drive(dve, subtract, IPC, 4)
                for k in range(IPC - 2, IPC):
                    copy(k, k % 2)

            @block.scalar
            def _(act):
                def copy(g, j):
                    k = 2 * g + j
                    need(act, s_masked, k - 1)
                    act.activation(stage[:, j], sc_k[:, bass.ds(k, 1)].rearrange("q o n -> q (o n)"), ACT.Copy).then_inc(s_staged, 1)
                act.wait_ge(s_scin, 16 * CH)
                drive(act, copy, IPC, 2)

                def weigh(g, j):
                    k = 2 * g + j
                    act.wait_ge(s_sub, k + 1)
                    need(act, s_wt, k - 1)
                    row = sc_k[:, bass.ds(k, 1)].rearrange("q o n -> q (o n)")
                    act.activation(stage[:, j], row, ACT.Exp).then_inc(s_exp, 1)
                drive(act, weigh, IPC, 2)

            @block.tensor
            def _(pe):
                def to_edges(g, j):
                    k = 2 * g + j
                    pe.wait_ge(s_exp, k + 1)
                    need(pe, s_wc, k - 1)
                    for s in range(SUB):
                        last = pe.transpose(PS[2 + j][:, s * P:(s + 1) * P], stage[:, j, s:TE:SUB], ident[:, :])
                    last.then_inc(s_wt, 1)
                drive(pe, to_edges, IPC, 2)

        with ExitStack() as part, nc.Block() as block:
            def tb(name, shape, dt=f32):
                return part.enter_context(nc.sbuf_tensor(name, shape, dt))
            def ts(name):
                return part.enter_context(nc.semaphore(name))
            U, R = 8, 4
            cut = [0]

            def carve(n):
                cut[0] += U * SUB * n
                return AR[:, cut[0] - U * SUB * n:cut[0]].rearrange("p (j s c) -> p j s c", j=U, s=SUB)
            vin, hot, wval = carve(VW), carve(P), carve(AW)
            run = tb("run", [P, R, AW])
            s_vin = [ts(f"values_in{j}") for j in range(U)]
            s_hot, s_w, s_wv, s_mm, s_run, s_clear = ts("hot2_done"), ts("weights_out"), ts("weighted"), ts("aggregated"), ts("run_done"), ts("run_cleared")
            s_rst = [ts(f"run_stored{j}") for j in range(R)]
            sc_v = SC[:, :].rearrange("p (k s m) -> p k s m", s=SUB, m=CH * H)

            @block.sync
            def _(sp):
                def load(g, j):
                    i = U * g + j
                    need(sp, s_mm, i - U + 1)
                    sp.dma_start(vin[:, j].rearrange("p s c -> p (s c)"),
                                 values[bass.ds(i, 1)].rearrange("o p c -> p (o c)")).then_inc(s_vin[j], 16)
                drive(sp, load, NI, U)

            @block.scalar
            def _(act):
                def store(g, j):
                    i = U * g + j
                    act.wait_ge(s_run, i + 1)
                    act.dma_start(sums[bass.ds(i, 1)].rearrange("o p c -> p (o c)"), run[:, j % R]).then_inc(s_rst[j % R], 16)
                drive(act, store, NI, U)
                for j in range(R):
                    act.wait_ge(s_rst[j], 16 * (NI // R))

            @block.gpsimd
            def _(pool):
                def weigh(g, j):
                    i = U * g + j
                    pool.wait_ge(s_vin[j], 16 * g + 16)
                    pool.wait_ge(s_w, i + 1)
                    pool.tensor_tensor(wval[:, j, :, 0:C].rearrange("p s (h k) -> p s h k", h=H),
                                       vin[:, j, :, 0:C].rearrange("p s (h k) -> p s h k", h=H),
                                       wval[:, j, :, C:AW].unsqueeze(3).broadcast_to((P, SUB, H, AH)), ALU.mult).then_inc(s_wv, 1)
                drive(pool, weigh, NI, U)

            @block.vector
            def _(dve):
                dve.memset(run[:, R - 1], 0.0).then_inc(s_clear, 1)
                dve.wait_ge(s_clear, 1)

                def prepare(g, j):
                    i = U * g + j
                    dve.wait_ge(s_vin[j], 16 * g + 16)
                    need(dve, s_mm, i - U + 1)
                    dve.tensor_copy(wval[:, j, :, C:AW],
                                    sc_v[:, bass.ds(i % IPC, 1), :, bass.ds((i // IPC) * H, H)].rearrange("p o s h -> p (o s) h")).then_inc(s_w, 1)
                    dve.tensor_tensor(hot[:, j], iota_row[:, :].unsqueeze(1).broadcast_to((P, SUB, P)),
                                      vin[:, j, :, C].unsqueeze(2).broadcast_to((P, SUB, P)), ALU.is_equal).then_inc(s_hot, 1)

                def step(g, j):
                    i = U * g + j
                    if not isinstance(i, int) or i + 2 < NI:
                        prepare(g + (j + 2) // U, (j + 2) % U)
                    dve.wait_ge(s_mm, i + 1)
                    need(dve, s_run, i)
                    need(dve, s_rst[j % R], 16 * (U // R * g + j // R))
                    dve.scalar_tensor_tensor(run[:, j % R], run[:, (j - 1) % R], keep[:, bass.ds(i, 1)], PS[j][:, 0:AW],
                                             ALU.mult, ALU.add).then_inc(s_run, 1)
                prepare(0, 0)
                prepare(0, 1)
                drive(dve, step, NI, U)

            @block.tensor
            def _(pe):
                def aggregate(g, j):
                    i = U * g + j
                    pe.wait_ge(s_hot, i + 1)
                    pe.wait_ge(s_wv, i + 1)
                    need(pe, s_run, i - U + 1)
                    for s in range(SUB):
                        last = pe.matmul(PS[j][:, 0:AW], lhsT=hot[:, j, s], rhs=wval[:, j, s],
                                         start=(s == 0), stop=(s == SUB - 1))
                    last.then_inc(s_mm, 1)
                drive(pe, aggregate, NI, U)

        with ExitStack() as part, nc.Block() as block:
            def tb(name, shape, dt=f32):
                return part.enter_context(nc.sbuf_tensor(name, shape, dt))
            def ts(name):
                return part.enter_context(nc.semaphore(name))
            U, S = 14, 7
            cut = [0]

            def carve(n):
                cut[0] += S * n
                return AR[:, cut[0] - S * n:cut[0]].rearrange("p (j c) -> p j c", j=S)
            agg, xin, fin, den = carve(AW), carve(C), carve(C), carve(H)
            biased, mean, meanT = carve(C), carve(C), carve(C)
            s_in = [ts(f"sums_in{j}") for j in range(S)]
            s_out = [ts(f"out_stored{j}") for j in range(S)]
            s_bias = ts("biases_added")
            s_mean, s_T, s_Ts, s_mm, s_fin = ts("mean_steps"), ts("meanT_done"), ts("meanT_copied"), ts("projected"), ts("out_ready")
            tail = N - (NB - 1) * P

            def nodes(v, b):
                return v[bass.ds(b * P, P), :]

            @block.sync
            def _(sp):
                def load(g, j):
                    b = U * g + j
                    last = sp.value_load(last_item[0:1, bass.ds(b, 1)], min_val=0, max_val=NI - 1)
                    need(sp, s_fin, b - S + 1)
                    sp.dma_start(agg[:, j % S], sums[bass.ds(last, 1)].rearrange("o p c -> p (o c)")).then_inc(s_in[j % S], 16)
                    if isinstance(b, int) and b == NB - 1:
                        sp.dma_start(xin[0:tail, j % S], x[b * P:N, :]).then_inc(s_in[j % S], 16)
                    else:
                        sp.dma_start(xin[:, j % S], nodes(x, b)).then_inc(s_in[j % S], 16)
                drive(sp, load, NB, U)

            @block.gpsimd
            def _(pool):
                def biases(g, j):
                    b = U * g + j
                    pool.wait_ge(s_in[j % S], 32 * (U // S * g + j // S + 1))
                    need(pool, s_mean, 4 * (b - S + 1))
                    pool.tensor_tensor(biased[:, j % S].rearrange("p (h k) -> p h k", h=H), bval[:, :, 1, :],
                                       agg[:, j % S, C:AW].unsqueeze(2).broadcast_to((P, H, AH)), ALU.mult).then_inc(s_bias, 1)
                    need(pool, s_out[j % S], 16 * (U // S * g + j // S))
                    pool.tensor_tensor(fin[:, j % S], xin[:, j % S], bproj[:, :], ALU.add).then_inc(s_bias, 1)
                drive(pool, biases, NB, U)

            @block.vector
            def _(dve):
                def divide(g, j):
                    b = U * g + j
                    dve.wait_ge(s_in[j % S], 32 * (U // S * g + j // S + 1))
                    need(dve, s_T, b - S + 1)
                    heads = mean[:, j % S].rearrange("p (h k) -> p h k", h=H)
                    dve.tensor_scalar(den[:, j % S], agg[:, j % S, C:AW], 1e-16, None, ALU.add).then_inc(s_mean, 1)
                    dve.wait_ge(s_bias, 2 * b + 1)
                    dve.tensor_tensor(mean[:, j % S], biased[:, j % S], agg[:, j % S, 0:C], ALU.add).then_inc(s_mean, 1)
                    dve.wait_ge(s_mean, 4 * b + 1)
                    dve.reciprocal(den[:, j % S], den[:, j % S]).then_inc(s_mean, 1)
                    dve.wait_ge(s_mean, 4 * b + 3)
                    dve.tensor_tensor(heads, heads, den[:, j % S].unsqueeze(2).broadcast_to((P, H, AH)), ALU.mult).then_inc(s_mean, 1)

                def finish(g, j):
                    b = U * g + j
                    dve.wait_ge(s_mm, b + 1)
                    dve.wait_ge(s_bias, 2 * b + 2)
                    dve.tensor_tensor(fin[:, j % S], PS[2 + j % 2][:, 0:C], fin[:, j % S], ALU.add).then_inc(s_fin, 1)

                def step(g, j):
                    divide(g, j)
                    if isinstance(g, int) and g == 0 and j == 0:
                        return
                    finish(g + (j - 1) // U, (j - 1) % U)
                drive(dve, step, NB, U)
                finish(NB // U - 1, U - 1)

            @block.scalar
            def _(act):
                def store(g, j):
                    b = U * g + j
                    act.wait_ge(s_fin, b + 1)
                    if isinstance(b, int) and b == NB - 1:
                        act.dma_start(out[b * P:N, :], fin[0:tail, j % S]).then_inc(s_out[j % S], 16)
                    else:
                        act.dma_start(nodes(out, b), fin[:, j % S]).then_inc(s_out[j % S], 16)

                def copy(g, j):
                    b = U * g + j
                    act.wait_ge(s_T, b + 1)
                    need(act, s_mm, b - S + 1)
                    act.activation(meanT[:, j % S], PS[j % 2][:, 0:P], ACT.Copy).then_inc(s_Ts, 1)
                    if not (isinstance(b, int) and b < 2):
                        store(g + (j - 2) // U, (j - 2) % U)
                drive(act, copy, NB, U)
                for j in range(U - 2, U):
                    store(NB // U - 1, j)
                for j in range(S):
                    act.wait_ge(s_out[j], 16 * (NB // S))

            @block.tensor
            def _(pe):
                def project(g, j):
                    b = U * g + j
                    pe.wait_ge(s_mean, 4 * b + 4)
                    need(pe, s_Ts, b - 1)
                    pe.transpose(PS[j % 2][:, 0:P], mean[:, j % S], ident[:, :]).then_inc(s_T, 1)
                    pe.wait_ge(s_Ts, b + 1)
                    need(pe, s_fin, b - 1)
                    pe.matmul(PS[2 + j % 2][:, 0:C], lhsT=meanT[:, j % S], rhs=wproj[:, :], start=True, stop=True).then_inc(s_mm, 1)
                drive(pe, project, NB, U)


_INS = ["x", "src", "dst", "edge_attr_32", "edge_weight1", "L0_gnn_w_src", "L0_gnn_b_src", "L0_gnn_w_dst",
        "L0_gnn_fc_w1", "L0_gnn_fc_b1", "L0_gnn_fc_w2", "L0_gnn_fc_b2", "L0_gnn_fc_w3", "L0_gnn_fc_b3",
        "L0_gnn_w_sep", "L0_gnn_b_sep", "L0_gnn_alpha_dot", "L0_gnn_w_proj", "L0_gnn_b_proj"]


def kernel(**inputs):
    import numpy as _np
    import concourse.bacc as _bacc
    from concourse import mybir as _mybir
    from concourse.bass_utils import run_bass_kernel_spmd as _run

    nc = _bacc.Bacc("TRN2", target_bir_lowering=False, num_devices=1)
    arrays, args = {}, []
    for name in _INS:
        a = _np.ascontiguousarray(inputs[name])
        if name == "edge_weight1":
            a = a.reshape(-1)
        if name == "edge_attr_32":
            a = _np.concatenate([a, _np.zeros((EPAD - E, RAD), a.dtype)])
        arrays[f"in_{name}"] = a
        args.append(nc.dram_tensor(f"in_{name}", a.shape, _mybir.dt.from_np(a.dtype), kind="ExternalInput").ap())
    out = nc.dram_tensor("out", (N, C), _mybir.dt.float32, kind="ExternalOutput").ap()
    gnn_kernel(nc, *args, out)
    r = _run(nc, [arrays], core_ids=[0])
    return r.results[0]["out"]
```
